# Optimizing a Trainium2 kernel written in Bass

```python
import numpy as np
import jax
import jax.numpy as jnp

def _softmax(x, axis=-1):
    return jax.nn.softmax(x, axis=axis)

def _gelu(x):
    return jax.nn.gelu(x, approximate=True)

def _silu(x):
    return jax.nn.silu(x)

def _sigmoid(x):
    return jax.nn.sigmoid(x)

def _layernorm(x, axis=-1, eps=1e-05):
    m = jnp.mean(x, axis=axis, keepdims=True)
    v = jnp.var(x, axis=axis, keepdims=True)
    return (x - m) / jnp.sqrt(v + eps)

def _scatter_add(tgt, idx, src, axis=0):
    return tgt.at[idx].add(src)

def _segment_sum(src, seg, n):
    return jax.ops.segment_sum(src, seg, n)
kernel_name = 'mk_early_fusion_embed_d1_tok_img768_r4_8785c7'

def setup_inputs(seed: int=0):
    np.random.seed(seed)
    _w = jnp.asarray

    def _rec_inputs():
        import jax
        import jax.numpy as jnp
        _rk = jax.random.key(seed)
        x = -0.000147625 + 0.999875 * jax.random.normal(jax.random.fold_in(_rk, 1), (64, 3, 224, 224), jnp.float32)
        x_txt = jax.random.randint(jax.random.fold_in(_rk, 51), (64, 77), 0, 31993, jnp.int32)
        return (x, x_txt)
    x, x_txt = _rec_inputs()

    def _L0_tok_setup():
        import jax, jax.numpy as jnp
        import numpy as np
        P = 16

        def _patchify(x):
            B, C, H, W = x.shape
            gh, gw = (H // P, W // P)
            x = x.reshape(B, C, gh, P, gw, P)
            x = x.transpose(0, 2, 4, 1, 3, 5)
            return x.reshape(B, gh * gw, C * P * P)
        key = jax.random.key(seed)
        k1, k2, k3, k4, k5 = jax.random.split(key, 5)
        B, C, H, W_ = (64, 3, 224, 224)
        D = 192
        Din = P * P * C
        seq = H // P * (W_ // P) + 1
        return {'x': jax.random.normal(k1, (B, C, H, W_), dtype=jnp.float32), 'W': jax.random.normal(k2, (D, Din), dtype=jnp.float32) * 0.02, 'b': jax.random.normal(k3, (D,), dtype=jnp.float32) * 0.02, 'class_token': jax.random.normal(k4, (D,), dtype=jnp.float32), 'pos_emb': jax.random.normal(k5, (seq, D), dtype=jnp.float32)}
    _L0_tok_all = _L0_tok_setup()
    _L0_tok_in = {k: v for k, v in _L0_tok_all.items() if k in ('W', 'b', 'class_token', 'pos_emb')}
    del _L0_tok_all

    def _L0_txt_setup():
        import jax, jax.numpy as jnp
        import numpy as np
        EPS = 1e-05

        def pos_encoding(max_steps, d):
            p, i = np.meshgrid(np.arange(max_steps), np.arange(d // 2))
            pe = np.zeros((max_steps, d), dtype=np.float32)
            pe[:, ::2] = np.sin(p / 2500 ** (2 * i / d)).T
            pe[:, 1::2] = np.cos(p / 2500 ** (2 * i / d)).T
            return jnp.asarray(pe)

        def batchnorm(x, gamma, beta):
            mean = jnp.mean(x, axis=(0, 1))
            var = jnp.var(x, axis=(0, 1))
            return (x - mean) * jax.lax.rsqrt(var + EPS) * gamma + beta
        key = jax.random.key(seed)
        ks = jax.random.split(key, 12)
        B, S, D, V = (8, 256, 192, 8000)
        Dc = D // 3
        s = 0.02
        return {'x': jax.random.randint(ks[0], (B, S), 0, V, dtype=jnp.int32), 'emb': jax.random.normal(ks[1], (V, D), dtype=jnp.float32) * s, 'Wq': jax.random.normal(ks[2], (Dc, D), dtype=jnp.float32) * s, 'bq': jnp.zeros((D,), jnp.float32), 'Wk': jax.random.normal(ks[3], (Dc, D), dtype=jnp.float32) * s, 'bk': jnp.zeros((D,), jnp.float32), 'Wv': jax.random.normal(ks[4], (Dc, D), dtype=jnp.float32) * s, 'bv': jnp.zeros((D,), jnp.float32), 'Wf': jax.random.normal(ks[5], (D, D), dtype=jnp.float32) * s, 'bf': jnp.zeros((D,), jnp.float32), 'g1': jnp.ones((D,), jnp.float32), 'b1': jnp.zeros((D,), jnp.float32), 'g2': jnp.ones((D,), jnp.float32), 'b2': jnp.zeros((D,), jnp.float32)}
    _L0_txt_all = _L0_txt_setup()
    _L0_txt_in = {k: v for k, v in _L0_txt_all.items() if k in ('emb', 'Wq', 'bq', 'Wk', 'bk', 'Wv', 'bv', 'Wf', 'bf', 'g1', 'b1', 'g2', 'b2')}
    del _L0_txt_all

    def _L0_attn_setup():
        import jax, jax.numpy as jnp
        import numpy as np
        B, T, DM = (4, 512, 192)
        H, D = (4, 64)
        DIM = H * D

        def _feature_map(x):
            return jax.nn.elu(x) + 1.0
        key = jax.random.key(seed)
        kx, kq, kk, kv, ko, kg = jax.random.split(key, 6)
        s = 0.02
        return {'x': jax.random.normal(kx, (B, T, DM), jnp.float32), 'Wq': jax.random.normal(kq, (DM, DIM), jnp.float32) * s, 'Wk': jax.random.normal(kk, (DM, DIM), jnp.float32) * s, 'Wv': jax.random.normal(kv, (DM, DIM), jnp.float32) * s, 'Wo': jax.random.normal(ko, (DIM, DM), jnp.float32) * s, 'Wg': jax.random.normal(kg, (DM, DM), jnp.float32) * s}
    _L0_attn_all = _L0_attn_setup()
    _L0_attn_in = {k: v for k, v in _L0_attn_all.items() if k in ('Wq', 'Wk', 'Wv', 'Wo', 'Wg')}
    del _L0_attn_all

    def _L0_ffn_setup():
        import jax, jax.numpy as jnp
        import numpy as np
        B, S, D, F, E = (8, 512, 192, 768, 16)
        CAP = 64
        EPS = 1e-06

        def _switch_moe_block(x, ln_w, w_router, wi, wo):
            var = jnp.mean(jnp.square(x.astype(jnp.float32)), axis=-1, keepdims=True)
            normed = (x * jax.lax.rsqrt(var + EPS)).astype(x.dtype) * ln_w
            logits = jnp.einsum('bsd,de->bse', normed.astype(jnp.float32), w_router.astype(jnp.float32))
            probs = jax.nn.softmax(logits, axis=-1)
            expert_idx = jnp.argmax(probs, axis=-1)
            onehot = jax.nn.one_hot(expert_idx, E, dtype=jnp.float32)
            priority = jnp.cumsum(onehot, axis=1)
            keep = onehot * (priority <= CAP)
            pos = (priority - 1.0).astype(jnp.int32)
            dispatch = keep[..., None] * jax.nn.one_hot(pos, CAP, dtype=jnp.float32)
            expert_in = jnp.einsum('bsec,bsd->becd', dispatch, normed)
            h = jax.nn.relu(jnp.einsum('becd,edf->becf', expert_in, wi))
            expert_out = jnp.einsum('becf,efd->becd', h, wo)
            combined = jnp.einsum('bsec,becd->bsd', dispatch, expert_out)
            routed = jnp.sum(dispatch, axis=(2, 3)) > 0
            next_states = jnp.where(routed[..., None], combined.astype(x.dtype), normed)
            router_prob = jnp.max(probs, axis=-1, keepdims=True).astype(x.dtype)
            return x + router_prob * next_states
        key = jax.random.key(seed)
        k_x, k_r, k_wi, k_wo = jax.random.split(key, 4)
        x = jax.random.normal(k_x, (B, S, D), dtype=jnp.float32)
        ln_w = jnp.ones((D,), dtype=jnp.float32)
        w_router = jax.random.normal(k_r, (D, E), dtype=jnp.float32) * 0.02
        wi = jax.random.normal(k_wi, (E, D, F), dtype=jnp.float32) * D ** (-0.5)
        wo = jax.random.normal(k_wo, (E, F, D), dtype=jnp.float32) * F ** (-0.5)
        return {'x': x, 'ln_w': ln_w, 'w_router': w_router, 'wi': wi, 'wo': wo}
    _L0_ffn_all = _L0_ffn_setup()
    _L0_ffn_in = {k: v for k, v in _L0_ffn_all.items() if k in ('ln_w', 'w_router', 'wi', 'wo')}
    del _L0_ffn_all
    return {'x': x, 'x_txt': x_txt, 'L0_tok_W': _L0_tok_in['W'], 'L0_tok_b': _L0_tok_in['b'], 'L0_tok_class_token': _L0_tok_in['class_token'], 'L0_tok_pos_emb': _L0_tok_in['pos_emb'], 'L0_txt_emb': _L0_txt_in['emb'], 'L0_txt_Wq': _L0_txt_in['Wq'], 'L0_txt_bq': _L0_txt_in['bq'], 'L0_txt_Wk': _L0_txt_in['Wk'], 'L0_txt_bk': _L0_txt_in['bk'], 'L0_txt_Wv': _L0_txt_in['Wv'], 'L0_txt_bv': _L0_txt_in['bv'], 'L0_txt_Wf': _L0_txt_in['Wf'], 'L0_txt_bf': _L0_txt_in['bf'], 'L0_txt_g1': _L0_txt_in['g1'], 'L0_txt_b1': _L0_txt_in['b1'], 'L0_txt_g2': _L0_txt_in['g2'], 'L0_txt_b2': _L0_txt_in['b2'], 'L0_attn_Wq': _L0_attn_in['Wq'], 'L0_attn_Wk': _L0_attn_in['Wk'], 'L0_attn_Wv': _L0_attn_in['Wv'], 'L0_attn_Wo': _L0_attn_in['Wo'], 'L0_attn_Wg': _L0_attn_in['Wg'], 'L0_ffn_ln_w': _L0_ffn_in['ln_w'], 'L0_ffn_w_router': _L0_ffn_in['w_router'], 'L0_ffn_wi': _L0_ffn_in['wi'], 'L0_ffn_wo': _L0_ffn_in['wo']}

def reference(x, x_txt, L0_tok_W, L0_tok_b, L0_tok_class_token, L0_tok_pos_emb, L0_txt_emb, L0_txt_Wq, L0_txt_bq, L0_txt_Wk, L0_txt_bk, L0_txt_Wv, L0_txt_bv, L0_txt_Wf, L0_txt_bf, L0_txt_g1, L0_txt_b1, L0_txt_g2, L0_txt_b2, L0_attn_Wq, L0_attn_Wk, L0_attn_Wv, L0_attn_Wo, L0_attn_Wg, L0_ffn_ln_w, L0_ffn_w_router, L0_ffn_wi, L0_ffn_wo):
    import jax
    import jax.numpy as jnp

    def _L0_tok_ref(x, W, b, class_token, pos_emb):
        import jax, jax.numpy as jnp
        import numpy as np
        P = 16

        def _patchify(x):
            B, C, H, W = x.shape
            gh, gw = (H // P, W // P)
            x = x.reshape(B, C, gh, P, gw, P)
            x = x.transpose(0, 2, 4, 1, 3, 5)
            return x.reshape(B, gh * gw, C * P * P)
        B = x.shape[0]
        patches = _patchify(x)
        tok = jnp.einsum('bnd,ed->bne', patches, W) + b
        cls = jnp.broadcast_to(class_token, (B, 1, class_token.shape[0]))
        emb = jnp.concatenate([cls, tok], axis=1)
        return emb + pos_emb[None, :, :]

    def _L0_txt_ref(x, emb, Wq, bq, Wk, bk, Wv, bv, Wf, bf, g1, b1, g2, b2):
        import jax, jax.numpy as jnp
        import numpy as np
        EPS = 1e-05

        def pos_encoding(max_steps, d):
            p, i = np.meshgrid(np.arange(max_steps), np.arange(d // 2))
            pe = np.zeros((max_steps, d), dtype=np.float32)
            pe[:, ::2] = np.sin(p / 2500 ** (2 * i / d)).T
            pe[:, 1::2] = np.cos(p / 2500 ** (2 * i / d)).T
            return jnp.asarray(pe)

        def batchnorm(x, gamma, beta):
            mean = jnp.mean(x, axis=(0, 1))
            var = jnp.var(x, axis=(0, 1))
            return (x - mean) * jax.lax.rsqrt(var + EPS) * gamma + beta
        B, S = x.shape
        D = emb.shape[1]
        H = 12
        hd = D // H
        N = 2
        scale = 1.0 / jnp.sqrt(jnp.asarray(D, jnp.float32))
        e = emb[x]
        P = pos_encoding(S, D)
        h = e + (e + P)

        def split_heads(t):
            return t.reshape(B, S, H, hd)
        for _ in range(N):
            q, k, v = jnp.split(h, 3, axis=-1)
            Q = split_heads(jax.nn.relu(q @ Wq + bq))
            K = split_heads(jax.nn.relu(k @ Wk + bk))
            V = split_heads(jax.nn.relu(v @ Wv + bv))
            scores = jnp.einsum('bqhd,bkhd->bhqk', Q, K) * scale
            attn = jax.nn.softmax(scores, axis=-1)
            o = jnp.einsum('bhqk,bkhd->bqhd', attn, V).reshape(B, S, D)
            t = batchnorm(h + o, g1, b1)
            h = batchnorm(t + (t @ Wf + bf), g2, b2)
        return h

    def _L0_attn_ref(x, Wq, Wk, Wv, Wo, Wg):
        import jax, jax.numpy as jnp
        import numpy as np
        B, T, DM = (4, 512, 192)
        H, D = (4, 64)
        DIM = H * D

        def _feature_map(x):
            return jax.nn.elu(x) + 1.0
        Bx, Tx, _ = x.shape
        q = _feature_map((x @ Wq).reshape(Bx, Tx, H, D))
        k = _feature_map((x @ Wk).reshape(Bx, Tx, H, D))
        v = (x @ Wv).reshape(Bx, Tx, H, D)
        qT = q.transpose(1, 0, 2, 3)
        kT = k.transpose(1, 0, 2, 3)
        vT = v.transpose(1, 0, 2, 3)
        S0 = jnp.zeros((Bx, H, D, D), x.dtype)
        z0 = jnp.zeros((Bx, H, D), x.dtype)

        def step(carry, inp):
            S, z = carry
            qi, ki, vi = inp
            S = S + ki[..., :, None] * vi[..., None, :]
            z = z + ki
            num = jnp.einsum('bhd,bhde->bhe', qi, S)
            den = jnp.maximum(jnp.sum(qi * z, axis=-1), 1e-06)
            return ((S, z), num / den[..., None])
        (_, _), outT = jax.lax.scan(step, (S0, z0), (qT, kT, vT))
        out = outT.transpose(1, 0, 2, 3).reshape(Bx, Tx, DIM)
        gate = jax.nn.sigmoid(x @ Wg)
        return out @ Wo * gate

    def _L0_ffn_ref(x, ln_w, w_router, wi, wo):
        import jax, jax.numpy as jnp
        import numpy as np
        B, S, D, F, E = (8, 512, 192, 768, 16)
        CAP = 64
        EPS = 1e-06

        def _switch_moe_block(x, ln_w, w_router, wi, wo):
            var = jnp.mean(jnp.square(x.astype(jnp.float32)), axis=-1, keepdims=True)
            normed = (x * jax.lax.rsqrt(var + EPS)).astype(x.dtype) * ln_w
            logits = jnp.einsum('bsd,de->bse', normed.astype(jnp.float32), w_router.astype(jnp.float32))
            probs = jax.nn.softmax(logits, axis=-1)
            expert_idx = jnp.argmax(probs, axis=-1)
            onehot = jax.nn.one_hot(expert_idx, E, dtype=jnp.float32)
            priority = jnp.cumsum(onehot, axis=1)
            keep = onehot * (priority <= CAP)
            pos = (priority - 1.0).astype(jnp.int32)
            dispatch = keep[..., None] * jax.nn.one_hot(pos, CAP, dtype=jnp.float32)
            expert_in = jnp.einsum('bsec,bsd->becd', dispatch, normed)
            h = jax.nn.relu(jnp.einsum('becd,edf->becf', expert_in, wi))
            expert_out = jnp.einsum('becf,efd->becd', h, wo)
            combined = jnp.einsum('bsec,becd->bsd', dispatch, expert_out)
            routed = jnp.sum(dispatch, axis=(2, 3)) > 0
            next_states = jnp.where(routed[..., None], combined.astype(x.dtype), normed)
            router_prob = jnp.max(probs, axis=-1, keepdims=True).astype(x.dtype)
            return x + router_prob * next_states
        return _switch_moe_block(x, ln_w, w_router, wi, wo)
    h = _L0_tok_ref(x, L0_tok_W, L0_tok_b, L0_tok_class_token, L0_tok_pos_emb)
    h = jnp.concatenate([h, _L0_txt_ref(x_txt, L0_txt_emb, L0_txt_Wq, L0_txt_bq, L0_txt_Wk, L0_txt_bk, L0_txt_Wv, L0_txt_bv, L0_txt_Wf, L0_txt_bf, L0_txt_g1, L0_txt_b1, L0_txt_g2, L0_txt_b2)], axis=1)
    h = h + _L0_attn_ref(_layernorm(h, axis=-1), L0_attn_Wq, L0_attn_Wk, L0_attn_Wv, L0_attn_Wo, L0_attn_Wg)
    h = h + _L0_ffn_ref(_layernorm(h, axis=-1), L0_ffn_ln_w, L0_ffn_w_router, L0_ffn_wi, L0_ffn_wo)
    return h

_drawn_inputs = setup_inputs


def setup_inputs(seed=0):
    import zlib

    import numpy as np

    out = dict(_drawn_inputs(seed))
    spreads = {'L0_txt_bq': (0.0, 2.0),
     'L0_txt_bk': (0.0, 2.0),
     'L0_txt_bv': (0.0, 0.8),
     'L0_txt_bf': (0.0, 2.0),
     'L0_txt_g1': (1.0, 0.2),
     'L0_txt_b1': (0.0, 2.0),
     'L0_txt_g2': (1.0, 0.2),
     'L0_txt_b2': (0.0, 0.1),
     'L0_ffn_ln_w': (1.0, 0.6)}
    factors = {'L0_tok_b': 3.607,
     'L0_txt_Wq': 8.0,
     'L0_txt_Wk': 8.0,
     'L0_txt_Wv': 7.869,
     'L0_attn_Wq': 8.0,
     'L0_attn_Wk': 8.0,
     'L0_attn_Wv': 8.0,
     'L0_attn_Wo': 8.0,
     'L0_attn_Wg': 8.0}
    for name, (base, spread) in spreads.items():
        noise = np.random.default_rng([zlib.crc32(name.encode()), seed]).standard_normal(out[name].shape)
        drawn = base * np.exp(spread * noise) if base else spread * noise
        out[name] = jnp.asarray(drawn.astype(out[name].dtype))
    for name, factor in factors.items():
        out[name] = (out[name] * factor).astype(out[name].dtype)
    return out
```

```python
from contextlib import ExitStack

import numpy as np

import concourse.bass as bass
from concourse import mybir

F32 = mybir.dt.float32
I32 = mybir.dt.int32
BF16 = mybir.dt.bfloat16
ALU = mybir.AluOpType
ACT = mybir.ActivationFunctionType
AX = mybir.AxisListType
ds = bass.ds

BATCH = 64
TXT = 77
IMG = 196
SEQ = 1 + IMG + TXT
D = 192
D0, D1 = 128, 64
VOCAB = 8000
PATCH = 768
KP = PATCH // 128
TH = 12
HD = D // TH
SLICE = D // 3
LAYERS = 2
HS = TH * TXT
HHALF = HS // 2
VA = TH * (HD + 1)
FCOL = 4 * TXT
FSTEPS = BATCH // 4
BN_EPS = 1e-5
LN_EPS = 1e-5

C_OFF = (0, 99, 197)
C_LEN = (99, 98, 77)
CH = 99
NC_ = 3
PADT = C_OFF[2] + CH
KD = D // 96
AH, AD = 4, 64
DIM = AH * AD
AT0, AT1, AT2 = 0, SEQ, SEQ + (SEQ - C_OFF[1])
ATW = AT2 + C_LEN[2]
EXP = 16
CAP = 64
REGION = BATCH * CAP
TILE = 128
TILES = -(-BATCH * SEQ // TILE) + EXP
TABLE = EXP * REGION + TILE
NO_ROW = 1 << 20
ROW = 2 * D + 4
F = 768
FC = F // 128


class Chain:

    def __init__(self, engine, sem):
        self.engine, self.sem, self.base, self.n = engine, sem, 0, 0

    def step(self, instruction):
        instruction.then_inc(self.sem, 1)
        self.n += 1

    def settle(self):
        self.engine.wait_ge(self.sem, self.base + self.n)

    def enter(self, offset):
        self.outer, self.base, self.n = (self.base + self.n, self.base + self.n + offset, 0)
        self.start = self.outer

    def leave(self, per_turn, turns):
        assert self.n == per_turn, self.n
        self.base, self.n = self.start + per_turn * turns, 0


class Scope:

    def __init__(self, nc, ctx, prefix):
        self.nc, self.ctx, self.prefix = nc, ctx, prefix

    def sb(self, name, shape, dt=F32):
        return self.ctx.enter_context(self.nc.sbuf_tensor(f"{self.prefix}_{name}", shape, dt))

    def ps(self, name, shape, dt=F32):
        return self.ctx.enter_context(self.nc.psum_tensor(f"{self.prefix}_{name}", shape, dt))

    def sem(self, name):
        return self.ctx.enter_context(self.nc.semaphore(f"{self.prefix}_{name}"))


def text_phase(nc, io, txt, ident, sems):
    with ExitStack() as ctx:
        S = Scope(nc, ctx, "t")
        S.sem = lambda name: sems.sem(f"t_{name}")
        h = S.sb("h", [128, 2, BATCH * TXT])
        ids = S.sb("ids", [TXT, BATCH], I32)
        ids_low = S.sb("ids_low", [TXT, BATCH])
        ids_wrapped = S.sb("ids_wrapped", [TXT, BATCH])
        ids_ok = S.sb("ids_ok", [TXT, BATCH], I32)
        ids_now = S.sb("ids_now", [TXT, 2], I32)
        rows = S.sb("rows", [TXT, 2, D])
        pos = S.sb("pos", [128, 2, TXT])
        wqk = S.sb("wqk", [SLICE + 1, 2, 3, 128])
        wv = S.sb("wv", [SLICE + 1, VA])
        wf = S.sb("wf", [128, 2, D])
        vecs = S.sb("vecs", [128, 5, 2])
        hs = S.sb("hs", [SLICE + 1, 3, TXT])
        q_sb = S.sb("q", [128, 2, 3, TXT])
        k_sb = S.sb("k", [128, 2, 3, TXT])
        v_sb = S.sb("v", [TXT, 2, VA])
        top = S.sb("top", [TXT, 4, 3])
        less = S.sb("less", [TXT, 4, 3, TXT])
        probs = S.sb("probs", [TXT, 4, 3, TXT])
        pt = S.sb("pt", [TXT, TH, TXT])
        rsum = S.sb("rsum", [TXT, TH])
        o_sb = S.sb("o", [TXT, TH, HD])
        ot = S.sb("ot", [128, 2, TXT])
        stats = S.sb("stats", [128, 2, BATCH, 6])
        mv = S.sb("mv", [128, 2, 2])
        var_eps = S.sb("var_eps", [128, 2])
        rstd = S.sb("rstd", [128, 2])
        minus_half = S.sb("minus_half", [128, 2])
        shift = S.sb("shift", [128, 2])
        aff1 = S.sb("aff1", [128, 2, 2])
        aff2 = S.sb("aff2", [128, 2, 2])
        tb = S.sb("tb", [128, 2, 2, FCOL])

        ps_s = S.ps("scores", [128, 4, 512])
        ps_pt = S.ps("probsT", [128, 2, 512])
        ps_qk = S.ps("qk", [128, 512])
        ps_vo = S.ps("vo", [128, 512])
        q_ps = ps_qk[:, 0:3 * TXT]
        k_ps = ps_qk[:, 3 * TXT:6 * TXT]
        v_ps = ps_vo[0:TXT, 0:VA]
        o_ps = ps_vo[0:TXT, 256:256 + VA].rearrange("p (h e) -> p h e", h=TH)
        ot_ps = ps_pt[:, 0, 0:2 * TXT].rearrange("p (c t) -> p c t", c=2)

        loaded, const_ready = S.sem("loaded"), S.sem("const_ready")
        ids_ready, ids_copied = S.sem("ids_ready"), S.sem("ids_copied")
        gathered = [S.sem("gathered0"), S.sem("gathered1")]
        rows_turned, embedded = S.sem("rows_turned"), S.sem("embedded")
        aff1_ready, aff2_ready = S.sem("aff1_ready"), S.sem("aff2_ready")
        var_ready, rstd_ready = S.sem("var_ready"), S.sem("rstd_ready")
        staged, qk_projected, v_projected = S.sem("staged"), S.sem("qk_projected"), S.sem("v_projected")
        qk_ready, v_ready = S.sem("qk_ready"), S.sem("v_ready")
        scored, shifted, probs_ready = S.sem("scored"), S.sem("shifted"), S.sem("probs_ready")
        turned, pt_low, pt_high = S.sem("turned"), S.sem("pt_low"), S.sem("pt_high")
        mixed, normed, o_turned = S.sem("mixed"), S.sem("normed"), S.sem("o_turned")
        ot_ready, z_ready = S.sem("ot_ready"), S.sem("z_ready")
        t_ready, f_ready, u_ready = S.sem("t_ready"), S.sem("f_ready"), S.sem("u_ready")
        y_ready, y_turned, y_stored = S.sem("y_ready"), S.sem("y_turned"), S.sem("y_stored")
        dve_chain, passed_dve, passed_pool = S.sem("dve_chain"), S.sem("passed_dve"), S.sem("passed_pool")

        def cols(b):
            return ds(b * TXT, TXT)

        block = ctx.enter_context(nc.Block())
        LOADS = 8

        @block.sync
        def _(sp):
            sp.dma_start(ids[:], io["ids"]).then_inc(loaded, 16)
            sp.dma_start(pos[:], io["pos"]).then_inc(loaded, 16)
            sp.dma_start(wqk[:], io["wqk"]).then_inc(loaded, 16)
            sp.dma_start(wv[:], io["wv"]).then_inc(loaded, 16)
            sp.dma_start(wf[:, 0, :], io["Wf"][0:D0, :]).then_inc(loaded, 16)
            sp.dma_start(wf[0:D1, 1, :], io["Wf"][D0:D, :]).then_inc(loaded, 16)
            sp.dma_start(vecs[:], io["vecs"]).then_inc(loaded, 16)
            sp.dma_start(hs[SLICE:SLICE + 1, :, :], io["ones"]).then_inc(loaded, 16)

        @block.gpsimd
        def _(pool):
            pool.memset(minus_half[:], -0.5).then_inc(const_ready, 1)
            pool.wait_ge(const_ready, 1)
            pool.wait_ge(ids_ready, 1)
            with pool.Fori(0, BATCH // 2) as j:
                for par in range(2):
                    pool.wait_ge(rows_turned, 2 * j + par + 1)
                    pool.tensor_copy(ids_now[:, par:par + 1], ids_ok[:, ds(2 * j + par, 1)]).then_inc(ids_copied, 1)
                    pool.wait_ge(ids_copied, 2 * j + par + 1)
                    pool.sem_inc(passed_pool, 1)
                    pool.indirect_dma_start(
                        out=rows[:, par, :], out_offset=None, in_=io["emb"],
                        in_offset=bass.IndirectOffsetOnAxis(ap=ids_now[:, par:par + 1], axis=0),
                    ).then_inc(gathered[par], 16)
            for n in range(2 * LAYERS):
                pool.wait_ge(var_ready, n + 1)
                pool.tensor_tensor(rstd[:], var_eps[:], minus_half[:], ALU.pow).then_inc(rstd_ready, 1)

        @block.scalar
        def _(act):
            act.wait_ge(loaded, 16 * LOADS)

            def stage(n, b, layer):
                act.activation(hs[0:SLICE, 0, :], h[0:SLICE, 0, cols(b)], ACT.Identity,
                               scale=aff2[0:SLICE, 0, 0:1], bias=aff2[0:SLICE, 1, 0:1])
                act.activation(hs[0:SLICE, 1, :], h[SLICE:D0, 0, cols(b)], ACT.Identity,
                               scale=aff2[SLICE:D0, 0, 0:1], bias=aff2[SLICE:D0, 1, 0:1])
                act.activation(hs[0:SLICE, 2, :], h[0:D1, 1, cols(b)], ACT.Identity,
                               scale=aff2[0:D1, 0, 1:2], bias=aff2[0:D1, 1, 1:2]).then_inc(staged, 1)

            def qk_relu(n, par):
                act.wait_ge(qk_projected, n + 1)
                act.activation(q_sb[:, par, :, :], q_ps.rearrange("p (c t) -> p c t", c=3), ACT.Relu)
                act.activation(k_sb[:, par, :, :], k_ps.rearrange("p (c t) -> p c t", c=3), ACT.Relu).then_inc(qk_ready, 1)

            def v_relu(n, par):
                act.wait_ge(v_projected, n + 1)
                act.activation(v_sb[:, par, :], v_ps, ACT.Relu).then_inc(v_ready, 1)

            def pt_copy(n):
                act.wait_ge(turned, n + 1)
                act.activation(pt[:, 0:TH // 2, :], ps_pt[0:TXT, 0, 0:HHALF].rearrange("p (h t) -> p h t", h=TH // 2),
                               ACT.Copy).then_inc(pt_low, 1)

            def exps(n):
                act.wait_ge(shifted, n + 1)
                act.activation(probs[:], less[:], ACT.Exp, scale=float(D) ** -0.5).then_inc(probs_ready, 1)

            def ot_add(n):
                act.wait_ge(o_turned, n + 1)
                act.wait_ge(z_ready, n + 1)
                act.activation(ot[:, 0, :], ot_ps[:, 0, :], ACT.Identity, bias=aff2[:, 1, 0:1])
                act.activation(ot[0:D1, 1, :], ot_ps[0:D1, 1, :], ACT.Identity, bias=aff2[0:D1, 1, 1:2]).then_inc(ot_ready, 1)

            def turn(n, b, par, first=False, stage_next=True, project_next=True):
                if not first:
                    pt_copy(n - 1)
                if project_next:
                    qk_relu(n + 1, 1 - par)
                exps(n)
                if not first:
                    ot_add(n - 1)
                if project_next:
                    v_relu(n + 1, 1 - par)
                if stage_next:
                    stage(n + 2, b + 2, None)

            act.sem_inc(ot_ready, 1)
            with act.Fori(0, LAYERS) as layer:
                n0 = layer * BATCH
                act.wait_ge(aff2_ready, layer + 1)
                stage(n0, 0, layer)
                qk_relu(n0, 0)
                v_relu(n0, 0)
                stage(n0 + 1, 1, layer)
                turn(n0, 0, 0, first=True)
                with act.Fori(0, BATCH // 2 - 2) as j:
                    for k in range(2):
                        b = 2 * j + 1 + k
                        turn(n0 + b, b, (1 + k) % 2)
                turn(n0 + BATCH - 3, BATCH - 3, 1)
                turn(n0 + BATCH - 2, BATCH - 2, 0, stage_next=False)
                turn(n0 + BATCH - 1, BATCH - 1, 1, stage_next=False, project_next=False)
                pt_copy(n0 + BATCH - 1)
                ot_add(n0 + BATCH - 1)

                act.wait_ge(aff1_ready, layer + 1)
                with act.Fori(0, FSTEPS // 2) as j:
                    for par in range(2):
                        q = 2 * j + par
                        act.wait_ge(u_ready, layer * FSTEPS + q + 1)
                        act.activation(tb[:, par, 0, :], h[:, 0, ds(q * FCOL, FCOL)], ACT.Identity,
                                       scale=aff1[:, 0, 0:1], bias=aff1[:, 1, 0:1])
                        act.activation(tb[0:D1, par, 1, :], h[0:D1, 1, ds(q * FCOL, FCOL)], ACT.Identity,
                                       scale=aff1[0:D1, 0, 1:2], bias=aff1[0:D1, 1, 1:2]).then_inc(t_ready, 1)
            act.wait_ge(aff2_ready, LAYERS + 1)
            with act.Fori(0, BATCH // 2) as j:
                for par in range(2):
                    b = 2 * j + par
                    act.wait_ge(y_stored, b + 1)
                    act.activation(tb[:, par, 0, 0:TXT], h[:, 0, cols(b)], ACT.Identity,
                                   scale=aff2[:, 0, 0:1], bias=aff2[:, 1, 0:1])
                    act.activation(tb[0:D1, par, 1, 0:TXT], h[0:D1, 1, cols(b)], ACT.Identity,
                                   scale=aff2[0:D1, 0, 1:2], bias=aff2[0:D1, 1, 1:2]).then_inc(y_ready, 1)

        @block.tensor
        def _(pe):
            pe.wait_ge(loaded, 16 * LOADS)
            pe.sem_inc(rows_turned, 2)
            with pe.Fori(0, BATCH // 2) as j:
                for par in range(2):
                    pe.wait_ge(gathered[par], 16 * j + 16)
                    pe.wait_ge(embedded, 2 * j + par + 1)
                    pe.transpose(ps_s[:, par, 0:TXT], rows[:, par, 0:D0], ident[0:TXT, 0:TXT])
                    pe.transpose(ps_s[0:D1, par, TXT:2 * TXT], rows[:, par, D0:D], ident[0:TXT, 0:TXT]).then_inc(rows_turned, 1)

            def project_qk(n):
                pe.wait_ge(staged, n + 1)
                for s, out in ((0, q_ps), (1, k_ps)):
                    for c in range(3):
                        mm = pe.matmul(out[:, c * TXT:(c + 1) * TXT], wqk[:, s, c, :], hs[:, s, :], start=True, stop=True)
                mm.then_inc(qk_projected, 1)

            def project_v():
                pe.matmul(v_ps, hs[:, 2, :], wv[:], start=True, stop=True).then_inc(v_projected, 1)

            def scores(n, par):
                pe.wait_ge(qk_ready, n + 1)
                for c in range(3):
                    for r in range(4):
                        g = slice(32 * r, 32 * r + 32)
                        mm = pe.matmul(ps_s[0:TXT, r, c * TXT:(c + 1) * TXT],
                                       q_sb[g, par, c, :], k_sb[g, par, c, :], start=True, stop=True)
                mm.then_inc(scored, 1)

            def turn_probs(n):
                pe.wait_ge(probs_ready, n + 1)
                pe.wait_ge(ot_ready, n + 1)
                for hh in range(TH):
                    a, c = divmod(hh, 6)
                    mm = pe.transpose(ps_pt[0:TXT, a, c * TXT:(c + 1) * TXT], probs[:, hh % 4, hh // 4, :], ident[0:TXT, 0:TXT])
                mm.then_inc(turned, 1)

            def mix(n, par, v_next):
                pe.wait_ge(pt_low, n + 1)
                pe.wait_ge(pt_high, n + 1)
                pe.wait_ge(v_ready, n + 1 + v_next)
                for hh in range(TH):
                    mm = pe.matmul(o_ps[:, hh, :], pt[:, hh, :], v_sb[:, par, hh * (HD + 1):(hh + 1) * (HD + 1)],
                                   start=True, stop=True)
                mm.then_inc(mixed, 1)

            def turn_out(n):
                pe.wait_ge(normed, n + 1)
                o = o_sb[:].rearrange("p h e -> p (h e)")
                pe.transpose(ot_ps[:, 0, :], o[:, 0:D0], ident[0:TXT, 0:TXT])
                pe.transpose(ot_ps[0:D1, 1, :], o[:, D0:D], ident[0:TXT, 0:TXT]).then_inc(o_turned, 1)

            def turn(n, par, first=False, project_next=True):
                if not first:
                    turn_probs(n - 1)
                scores(n, par)
                if project_next:
                    project_qk(n + 1)
                if first:
                    pe.wait_ge(v_ready, n + 1)
                else:
                    mix(n - 1, 1 - par, 1)
                    turn_out(n - 1)
                if project_next:
                    project_v()

            with pe.Fori(0, LAYERS) as layer:
                n0 = layer * BATCH
                project_qk(n0)
                project_v()
                turn(n0, 0, first=True)
                with pe.Fori(0, BATCH // 2 - 2) as j:
                    for k in range(2):
                        turn(n0 + 2 * j + 1 + k, (1 + k) % 2)
                turn(n0 + BATCH - 3, 1)
                turn(n0 + BATCH - 2, 0)
                turn(n0 + BATCH - 1, 1, project_next=False)
                turn_probs(n0 + BATCH - 1)
                mix(n0 + BATCH - 1, 1, 0)
                turn_out(n0 + BATCH - 1)
                with pe.Fori(0, FSTEPS // 2) as j:
                    for par in range(2):
                        pe.wait_ge(t_ready, layer * FSTEPS + 2 * j + par + 1)
                        lo, hi = tb[:, par, 0, :], tb[0:D1, par, 1, :]
                        pe.matmul(ps_s[:, par, 0:FCOL], wf[:, 0, 0:D0], lo, start=True, stop=False)
                        pe.matmul(ps_s[:, par, 0:FCOL], wf[0:D1, 1, 0:D0], hi, start=False, stop=True)
                        pe.matmul(ps_s[0:D1, 2 + par, 0:FCOL], wf[:, 0, D0:D], lo, start=True, stop=False)
                        pe.matmul(ps_s[0:D1, 2 + par, 0:FCOL], wf[0:D1, 1, D0:D], hi, start=False, stop=True).then_inc(f_ready, 1)
            with pe.Fori(0, BATCH // 2) as j:
                for par in range(2):
                    pe.wait_ge(y_ready, 2 * j + par + 1)
                    pe.transpose(ps_s[0:TXT, par, 0:D0], tb[:, par, 0, 0:TXT], ident[:])
                    pe.transpose(ps_s[0:TXT, par, D0:D], tb[0:D1, par, 1, 0:TXT], ident[0:D1, 0:D1]).then_inc(y_turned, 1)

        @block.vector
        def _(dve):
            ch = Chain(dve, dve_chain)
            dve.sem_inc(embedded, 2)
            dve.sem_inc(z_ready, 1)
            dve.sem_inc(u_ready, 2)
            dve.sem_inc(y_stored, 2)
            dve.wait_ge(loaded, 16 * LOADS)
            ch.step(dve.tensor_scalar(ids_low[:], ids[:], 0.0, float(VOCAB), ALU.is_lt, ALU.mult))
            ch.settle()
            ch.step(dve.tensor_tensor(ids_wrapped[:], ids[:], ids_low[:], ALU.add))
            ch.settle()
            dve.tensor_scalar(ids_ok[:], ids_wrapped[:], 0.0, float(VOCAB - 1), ALU.max, ALU.min).then_inc(ids_ready, 1)
            dve.memset(aff2[:, 0, :], 1.0)
            ch.step(dve.memset(aff2[:, 1, :], 0.0))
            ch.step(dve.memset(mv[:], 1.0))
            ch.settle()
            with dve.Fori(0, BATCH // 2) as j:
                for par in range(2):
                    b = 2 * j + par
                    dve.wait_ge(rows_turned, b + 3)
                    dve.scalar_tensor_tensor(out=h[:, 0, cols(b)], in0=ps_s[:, par, 0:TXT], scalar=2.0,
                                             in1=pos[:, 0, :], op0=ALU.mult, op1=ALU.add)
                    dve.scalar_tensor_tensor(out=h[0:D1, 1, cols(b)], in0=ps_s[0:D1, par, TXT:2 * TXT], scalar=2.0,
                                             in1=pos[0:D1, 1, :], op0=ALU.mult, op1=ALU.add).then_inc(embedded, 1)
            dve.wait_ge(embedded, BATCH + 2)
            dve.sem_inc(aff2_ready, 1)

            def soften(n, par, first=False):
                dve.wait_ge(scored, n + 1)
                s = ps_s[0:TXT, :, 0:3 * TXT].rearrange("p r (c t) -> p r c t", c=3)
                ch.step(dve.tensor_reduce(out=top[:], in_=s, axis=AX.X, op=ALU.max))
                ch.settle()
                if not first:
                    dve.wait_ge(probs_ready, n)
                dve.tensor_tensor(less[:], s, top[:].unsqueeze(3).to_broadcast([TXT, 4, 3, TXT]),
                                  ALU.subtract).then_inc(shifted, 1)

            def pt_copy(n):
                dve.wait_ge(turned, n + 1)
                dve.tensor_copy(pt[:, TH // 2:TH, :], ps_pt[0:TXT, 1, 0:HHALF].rearrange("p (h t) -> p h t", h=TH // 2)).then_inc(pt_high, 1)

            def norm(n):
                dve.wait_ge(mixed, n + 1)
                ch.step(dve.reciprocal(rsum[:], o_ps[:, :, HD]))
                ch.settle()
                dve.tensor_tensor(o_sb[:], o_ps[:, :, 0:HD], rsum[:].unsqueeze(2).to_broadcast([TXT, TH, HD]),
                                  ALU.mult).then_inc(normed, 1)

            def residual(n, b):
                dve.wait_ge(ot_ready, n + 2)
                dve.scalar_tensor_tensor(out=h[:, 0, cols(b)], in0=h[:, 0, cols(b)], scalar=aff2[:, 0, 0:1],
                                         in1=ot[:, 0, :], op0=ALU.mult, op1=ALU.add)
                ch.step(dve.scalar_tensor_tensor(out=h[0:D1, 1, cols(b)], in0=h[0:D1, 1, cols(b)], scalar=aff2[0:D1, 0, 1:2],
                                                 in1=ot[0:D1, 1, :], op0=ALU.mult, op1=ALU.add))
                ch.settle()
                dve.bn_stats(out=stats[:, 0, ds(b, 1), :], in_=h[:, 0, cols(b)])
                dve.bn_stats(out=stats[0:D1, 1, ds(b, 1), :], in_=h[0:D1, 1, cols(b)]).then_inc(z_ready, 1)

            def turn(n, b, par, first=False):
                if not first:
                    pt_copy(n - 1)
                soften(n, par, first)
                if not first:
                    norm(n - 1)
                    residual(n - 1, b - 1)

            def affine(aff, count, which, n, ready):
                dve.bn_aggr(out=mv[:, 0, :], in_=stats[:, 0, 0:count, :].rearrange("p n s -> p (n s)"))
                ch.step(dve.bn_aggr(out=mv[0:D1, 1, :], in_=stats[0:D1, 1, 0:count, :].rearrange("p n s -> p (n s)")))
                ch.settle()
                dve.tensor_scalar(var_eps[:], mv[:, :, 1], BN_EPS, None, ALU.add).then_inc(var_ready, 1)
                dve.wait_ge(rstd_ready, n)
                ch.step(dve.tensor_tensor(aff[:, 0, :], vecs[:, which, :], rstd[:], ALU.mult))
                ch.settle()
                ch.step(dve.tensor_tensor(shift[:], mv[:, :, 0], aff[:, 0, :], ALU.mult))
                ch.settle()
                dve.tensor_tensor(aff[:, 1, :], vecs[:, which + 1, :], shift[:], ALU.subtract).then_inc(ready, 1)

            TURN_CHAIN, LAYER_CHAIN = 3, 3 * (BATCH + 0) + FSTEPS + 6
            with dve.Fori(0, LAYERS) as layer:
                ch.enter(layer * LAYER_CHAIN)
                start, base = ch.start, ch.base
                n0 = layer * BATCH
                turn(n0, 0, 0, first=True)
                done = ch.n
                with dve.Fori(0, BATCH // 2 - 2) as j:
                    for k in range(2):
                        ch.base, ch.n = base + done + (2 * j + k) * TURN_CHAIN, 0
                        b = 2 * j + 1 + k
                        turn(n0 + b, b, (1 + k) % 2)
                        assert ch.n == TURN_CHAIN
                ch.base, ch.n = base, done + (BATCH - 4) * TURN_CHAIN
                for b in range(BATCH - 3, BATCH):
                    turn(n0 + b, b, b % 2)
                pt_copy(n0 + BATCH - 1)
                norm(n0 + BATCH - 1)
                residual(n0 + BATCH - 1, BATCH - 1)
                dve.wait_ge(z_ready, n0 + BATCH + 1)
                dve.sem_inc(passed_dve, 1)
                affine(aff1, BATCH, 1, 2 * layer + 1, aff1_ready)
                done = ch.n
                with dve.Fori(0, FSTEPS // 2) as j:
                    for par in range(2):
                        q = 2 * j + par
                        ch.base, ch.n = base + done + q, 0
                        dve.wait_ge(f_ready, layer * FSTEPS + q + 1)
                        dve.scalar_tensor_tensor(out=h[:, 0, ds(q * FCOL, FCOL)], in0=ps_s[:, par, 0:FCOL], scalar=vecs[:, 0, 0:1],
                                                 in1=tb[:, par, 0, :], op0=ALU.add, op1=ALU.add)
                        ch.step(dve.scalar_tensor_tensor(out=h[0:D1, 1, ds(q * FCOL, FCOL)], in0=ps_s[0:D1, 2 + par, 0:FCOL],
                                                         scalar=vecs[0:D1, 0, 1:2], in1=tb[0:D1, par, 1, :], op0=ALU.add, op1=ALU.add))
                        ch.settle()
                        dve.bn_stats(out=stats[:, 0, ds(q, 1), :], in_=h[:, 0, ds(q * FCOL, FCOL)])
                        dve.bn_stats(out=stats[0:D1, 1, ds(q, 1), :], in_=h[0:D1, 1, ds(q * FCOL, FCOL)]).then_inc(u_ready, 1)
                ch.base, ch.n = base, done + FSTEPS
                dve.wait_ge(u_ready, (layer + 1) * FSTEPS + 2)
                dve.sem_inc(passed_dve, 1)
                affine(aff2, FSTEPS, 3, 2 * layer + 2, aff2_ready)
                assert ch.n == LAYER_CHAIN, ch.n
                ch.start = start
            with dve.Fori(0, BATCH // 2) as j:
                for par in range(2):
                    b = 2 * j + par
                    dve.wait_ge(y_turned, b + 1)
                    dve.tensor_copy(txt[:, ds(b, 1), :], ps_s[0:TXT, par, 0:D]).then_inc(y_stored, 1)


def carry(engine, sem):
    engine.sem_inc(sem, 1)


def fusion_phase(nc, io, out, txt, ident, rows_dram, table_dram, run, sems):
    with ExitStack() as ctx:
        S = Scope(nc, ctx, "f")
        S.sem = lambda name: sems.sem(f"f_{name}")
        xk = S.sb("patches", [128, 2, KP, 2 * CH])
        wt = S.sb("w_tok", [128, KP, D])
        posb = S.sb("pos_bias", [CH, 2, D])
        bias = S.sb("bias", [CH, 2, D])
        wq = S.sb("wq", [96, KD, DIM])
        wk = S.sb("wk", [96, KD, DIM])
        wv = S.sb("wv", [96, KD, DIM])
        wg = S.sb("wg", [96, KD, D])
        wo = S.sb("wo", [128, DIM // 128, D])
        wr = S.sb("wr", [96, KD, EXP])
        lnw = S.sb("lnw", [CH, D])
        mask = S.sb("mask", [CH, ATW])
        tri = S.sb("tri", [CH, CH], BF16)
        ones = S.sb("ones", [CH, CH], BF16)
        rank = S.sb("rank", [CH, NC_, EXP])
        minus_half = S.sb("minus_half", [CH, NC_])
        pad_ids = S.sb("pad_ids", [128, TABLE // 128], I32)
        tid = S.sb("tid", [CH, NC_])
        tid_i = S.sb("tid_i", [CH, 2, NC_], I32)

        h = S.sb("h", [CH, 4, NC_, D])
        st1, st2 = S.sb("st1", [CH, NC_, 6]), S.sb("st2", [CH, NC_, 6])
        mv1, mv2 = S.sb("mv1", [CH, NC_, 2]), S.sb("mv2", [CH, NC_, 2])
        ve1, ve2 = S.sb("ve1", [CH, NC_]), S.sb("ve2", [CH, NC_])
        rs1, rs2, rms = S.sb("rs1", [CH, NC_]), S.sb("rs2", [CH, NC_]), S.sb("rms", [CH, NC_])
        ms1, ms2, ms3 = (S.sb(n, [CH, NC_]) for n in ("ms1", "ms2", "ms3"))
        ln = S.sb("ln", [CH, NC_, D])
        xT = S.sb("xT", [96, 2, KD, PADT])
        e_sb = S.sb("e", [128, 4, SEQ])
        r_sb = S.sb("r", [128, 4, SEQ])
        qk = S.sb("qk", [128, 2, 4, PADT])
        va = S.sb("va", [CH, 2, NC_, AH, AD + 1])
        th = S.sb("th", [CH, 2, NC_, D])
        at = S.sb("at", [CH, AH, ATW])
        den, rden = S.sb("den", [CH, NC_, AH]), S.sb("rden", [CH, NC_, AH])
        o = S.sb("o", [CH, NC_, AH, AD])
        oT = S.sb("oT", [128, 2, PADT])
        gated = S.sb("gated", [CH, NC_, D])
        ln2 = S.sb("ln2", [CH, NC_, D])
        rt = S.sb("rt", [CH, 2, NC_, ROW])
        nT = S.sb("nT", [96, KD, PADT])
        best = S.sb("best", [CH, NC_])
        eq, less, ex = (S.sb(n, [CH, NC_, EXP]) for n in ("eq", "less", "ex"))
        esum = S.sb("esum", [CH, NC_])
        ranked = S.sb("ranked", [CH, NC_, EXP])
        first = S.sb("first", [CH, NC_])
        hot = S.sb("hot", [CH, NC_, EXP], BF16)
        at_cum, at_run = S.sb("at_cum", [CH, NC_, EXP]), S.sb("at_run", [CH, NC_, EXP])
        prio, place, over = (S.sb(n, [CH, NC_]) for n in ("prio", "place", "over"))
        slot0 = S.sb("slot0", [CH, NC_])
        slot = S.sb("slot", [CH, 2, NC_], I32)
        ob = S.sb("ob", [CH, 2, NC_, D])

        B = [S.ps(f"bank{n}", [128, 512]) for n in range(8)]

        loaded, made, filled = S.sem("loaded"), S.sem("made"), S.sem("filled")
        xk_in = [S.sem("xk_in0"), S.sem("xk_in1")]
        rows_out = [S.sem("rows_out0"), S.sem("rows_out1")]
        slots_out = [S.sem("slots_out0"), S.sem("slots_out1")]
        (tok_done, h_ready, text_ready, var1, rstd1, ln1, xT_turned, xT_lo, xT_hi, qk_done, qk_read, fm,
         vg_done, vg_ready, at_done, masked, num_done, o_ready, oT_turned, oT_ready, oT_high, y_done, h2_ready,
         var2, rstd2, rms_ready, l_ready, normed, base_ready, nT_turned, nT_ready, lg_done, ex_in, ex_ready,
         rp_ready, hot_ready, cum_done, slots_ready, ob_ready, pool_chain, chain, passed_dve, passed_pool) = (S.sem(n) for n in (
             "tok_done", "h_ready", "text_ready", "var1", "rstd1", "ln1", "xT_turned", "xT_lo", "xT_hi", "qk_done",
             "qk_read", "fm", "vg_done", "vg_ready", "at_done", "masked", "num_done", "o_ready", "oT_turned", "oT_ready", "oT_high",
             "y_done", "h2_ready", "var2", "rstd2", "rms_ready", "l_ready", "normed", "base_ready", "nT_turned",
             "nT_ready", "lg_done", "ex_in", "ex_ready", "rp_ready", "hot_ready", "cum_done", "slots_ready", "ob_ready",
             "pool_chain", "chain", "passed_dve", "passed_pool"))
        LOADS = 12
        MADE = 13

        def turns(engine, turn):
            for i in range(4):
                turn(i, i, i >= 0, i >= 1, i >= 2, i >= 3)
            with engine.Fori(0, BATCH // 4 - 1) as j:
                for k in range(4):
                    turn(4 * j + 4 + k, k, True, True, True, True)
            for i in range(BATCH, BATCH + 3):
                turn(i, i % 4, False, i - 1 < BATCH, i - 2 < BATCH, True)

        passed_sp = S.sem("passed_sp")
        block = ctx.enter_context(nc.Block())
        rows_v = rows_dram.rearrange("(b t) n -> b t n", t=SEQ)

        @block.sync
        def _(sp):
            sp.dma_start(wt[:], io["w_tok"]).then_inc(loaded, 16)
            sp.dma_start(posb[:], io["pos_emb"]).then_inc(loaded, 16)
            sp.dma_start(bias[:], io["tok_bias"]).then_inc(loaded, 16)
            for t, n in ((wq, "a_wq"), (wk, "a_wk"), (wv, "a_wv"), (wg, "a_wg")):
                sp.dma_start(t[:], io[n].rearrange("(k p) n -> p k n", p=96)).then_inc(loaded, 16)
            sp.dma_start(wo[:], io["a_wo"].rearrange("(k p) n -> p k n", p=128)).then_inc(loaded, 16)
            sp.dma_start(wr[:], io["w_router"].rearrange("(k p) n -> p k n", p=96)).then_inc(loaded, 16)
            sp.dma_start(lnw[:], io["ln_w"].partition_broadcast(CH)).then_inc(loaded, 16)
            sp.dma_start(mask[:], io["mask"]).then_inc(loaded, 16)
            sp.dma_start(rank[:], io["rank"]).then_inc(loaded, 16)
            sp.wait_ge(made, MADE)
            sp.dma_start(table_dram.rearrange("(p n) o -> p (n o)", p=128), pad_ids[:]).then_inc(filled, 16)

            def load_patches(b, p2):
                sp.wait_ge(tok_done, b + 1)
                carry(sp, passed_sp)
                sp.dma_start(xk[:, p2, :, :].rearrange("p k t -> p (k t)"),
                             io["patches"][ds(b, 1), :, :].rearrange("b p n -> (b p) n")).then_inc(xk_in[p2], 16)

            def store_rows(b, q):
                sp.wait_ge(ob_ready, b + 1)
                carry(sp, passed_sp)
                for n in range(NC_):
                    rows = slice(0, C_LEN[n])
                    sp.dma_start(rows_v[ds(b, 1), C_OFF[n]:C_OFF[n] + C_LEN[n], :].rearrange("b t n -> (b t) n"),
                                 rt[rows, q, n, :]).then_inc(rows_out[q], 16)
                    sp.dma_start(out[ds(b, 1), C_OFF[n]:C_OFF[n] + C_LEN[n], :].rearrange("b t n -> (b t) n"),
                                 ob[rows, q, n, :]).then_inc(rows_out[q], 16)

            LAG = 5
            for b in range(LAG + 1):
                if b >= LAG:
                    store_rows(b - LAG, (b - LAG) % 2)
                load_patches(b, b % 2)
            with sp.Fori(0, (BATCH - LAG - 1) // 2) as j:
                for k in range(2):
                    store_rows(2 * j + 1 + k, (1 + k) % 2)
                    load_patches(2 * j + LAG + 1 + k, k)
            for b in range(BATCH - LAG, BATCH):
                store_rows(b, b % 2)
            for q in range(2):
                sp.wait_ge(rows_out[q], 16 * 6 * (BATCH // 2))

        @block.gpsimd
        def _(pool):
            pool.memset(pad_ids[:], NO_ROW).then_inc(made, 1)
            for t in (h, th, den):
                pool.memset(t[:], 1.0).then_inc(made, 1)
            for t in (xT, qk, oT, nT, rt):
                pool.memset(t[:], 0.0).then_inc(made, 1)
            pool.memset(va[:], 1.0).then_inc(made, 1)
            pool.memset(minus_half[:], -0.5).then_inc(made, 1)
            pool.memset(ones[:], 1.0).then_inc(made, 1)
            pool.iota(tid[:], [[CH, NC_]], base=0, channel_multiplier=1, allow_small_or_imprecise_dtypes=True).then_inc(made, 1)
            pool.wait_ge(made, MADE)
            pool.wait_ge(loaded, 16 * LOADS)
            pool.wait_ge(filled, 16)

            ch = Chain(pool, pool_chain)

            def turn(i, p4, a, b1, b2, c):
                p2 = p4 % 2
                if a:
                    if not isinstance(i, int) or i >= 4:
                        pool.wait_ge(l_ready, i - 3)
                    pool.tensor_copy(h[0:TXT, p4, 2, :], txt[:, ds(i, 1), :].rearrange("p b n -> p (b n)")).then_inc(text_ready, 1)
                if c:
                    pool.wait_ge(var2, i - 2)
                    pool.tensor_tensor(rs2[:], ve2[:], minus_half[:], ALU.pow).then_inc(rstd2, 1)
                    pool.wait_ge(rstd2, i - 2)
                    ch.step(pool.tensor_tensor(ms1[:], mv2[:, :, 1], rs2[:], ALU.mult))
                    ch.settle()
                    ch.step(pool.tensor_tensor(ms2[:], ms1[:], rs2[:], ALU.mult))
                    ch.settle()
                    carry(pool, passed_pool)
                    ch.step(pool.tensor_scalar(ms3[:], ms2[:], 1e-6, None, ALU.add))
                    ch.settle()
                    pool.tensor_tensor(rms[:], ms3[:], minus_half[:], ALU.pow).then_inc(rms_ready, 1)
                if a:
                    pool.wait_ge(var1, i + 1)
                    pool.tensor_tensor(rs1[:], ve1[:], minus_half[:], ALU.pow).then_inc(rstd1, 1)
                if c:
                    q = 1 - p2
                    pool.wait_ge(normed, i - 2)
                    pool.tensor_tensor(rt[:, q, :, D:2 * D], h[:, (p4 + 1) % 4, :, :], ln2[:], ALU.add).then_inc(base_ready, 1)
                    pool.wait_ge(rp_ready, i - 2)
                    carry(pool, passed_pool)
                    for n in range(NC_):
                        mm = pool.tensor_scalar(ob[:, q, n, :], rt[:, q, n, 0:D], rt[:, q, n, 2 * D:2 * D + 1], None, ALU.mult)
                    ch.step(mm)
                    ch.settle()
                    pool.tensor_tensor(ob[:, q, :, :], ob[:, q, :, :], rt[:, q, :, D:2 * D], ALU.add).then_inc(ob_ready, 1)
                    pool.wait_ge(slots_ready, i - 1)
                    carry(pool, passed_pool)
                    for n in range(NC_):
                        rows = slice(0, C_LEN[n])
                        pool.indirect_dma_start(
                            out=table_dram, out_offset=bass.IndirectOffsetOnAxis(ap=slot[rows, q, n:n + 1], axis=0),
                            in_=tid_i[rows, q, n:n + 1], in_offset=None,
                            bounds_check=EXP * REGION - 1, oob_is_err=False).then_inc(slots_out[q], 16)
            PER = 4
            for i in range(4):
                turn(i, i, i >= 0, i >= 1, i >= 2, i >= 3)
            done = ch.n
            with pool.Fori(0, BATCH // 4 - 1) as j:
                for k in range(4):
                    ch.base, ch.n = done + (4 * j + k) * PER, 0
                    turn(4 * j + 4 + k, k, True, True, True, True)
                    assert ch.n == PER, ch.n
            ch.base, ch.n = done + (BATCH - 4) * PER, 0
            for i in range(BATCH, BATCH + 3):
                turn(i, i % 4, False, i - 1 < BATCH, i - 2 < BATCH, True)
            for q in range(2):
                pool.wait_ge(slots_out[q], 16 * NC_ * (BATCH // 2))

        @block.scalar
        def _(act):
            act.wait_ge(made, MADE)

            def turn(i, p4, a, b1, b2, c):
                p2 = p4 % 2
                if b1:
                    q = 1 - p2
                    for n in range(4):
                        act.wait_ge(qk_done, 4 * (i - 1) + n + 1)
                        act.wait_ge(fm, 4 * (i - 1) + n + 1)
                        act.activation(e_sb[:, n, :], B[3 + n][:, 0:SEQ], ACT.Exp)
                        act.activation(r_sb[:, n, :], B[3 + n][:, 0:SEQ], ACT.Relu).then_inc(qk_read, 1)
                if c:
                    act.wait_ge(nT_turned, i - 2)
                    act.activation(nT[:, 0, 0:SEQ], B[1][0:96, 0:SEQ], ACT.Copy)
                    act.activation(nT[:, 1, 0:SEQ], B[2][0:96, 0:SEQ], ACT.Copy).then_inc(nT_ready, 1)
                if b1:
                    act.wait_ge(vg_done, 4 * (i - 1) + 1)
                    act.activation(va[:, q, 0:2, :, 0:AD], B[3][0:CH, :].rearrange("p (c h e) -> p c h e", c=2, h=AH), ACT.Copy)
                    act.wait_ge(vg_done, 4 * (i - 1) + 2)
                    act.activation(va[:, q, 2, :, 0:AD], B[4][0:CH, 0:DIM].rearrange("p (h e) -> p h e", h=AH), ACT.Copy)
                    act.wait_ge(vg_done, 4 * (i - 1) + 3)
                    act.activation(th[:, q, 0:2, :], B[5][0:CH, 0:2 * D].rearrange("p (c n) -> p c n", c=2), ACT.Tanh, scale=0.5)
                    act.wait_ge(vg_done, 4 * (i - 1) + 4)
                    act.activation(th[:, q, 2, :], B[6][0:CH, 0:D], ACT.Tanh, scale=0.5).then_inc(vg_ready, 1)
                if c:
                    act.wait_ge(ex_in, i - 2)
                    act.activation(ex[:], less[:], ACT.Exp).then_inc(ex_ready, 1)
                if a:
                    act.wait_ge(xT_turned, i + 1)
                    act.activation(xT[:, p2, 0, 0:SEQ], B[1][0:96, 0:SEQ], ACT.Copy).then_inc(xT_lo, 1)
                if b2:
                    act.wait_ge(oT_turned, i - 1)
                    act.activation(oT[:, 0, 0:SEQ], B[1][:, 0:SEQ], ACT.Copy).then_inc(oT_ready, 1)
            turns(act, turn)

        @block.tensor
        def _(pe):
            pe.wait_ge(loaded, 16 * LOADS)
            pe.wait_ge(made, MADE)
            pe.sem_inc(tok_done, 2)

            def tokens(i, p2):
                pe.wait_ge(h_ready, i + 1)
                pe.wait_ge(xk_in[p2], 16 * ((i - p2) // 2) + 16 if isinstance(i, int) else 8 * (i - p2) + 16)
                for n in range(2):
                    for k in range(KP):
                        mm = pe.matmul(B[0][0:CH, n * D:(n + 1) * D], xk[:, p2, k, n * CH:(n + 1) * CH], wt[:, k, :],
                                       start=(k == 0), stop=(k == KP - 1))
                mm.then_inc(tok_done, 1)

            def turned(source):
                for k in range(KD):
                    for n in range(NC_):
                        mm = pe.transpose(B[1 + k][0:96, C_OFF[n]:C_OFF[n] + C_LEN[n]],
                                          source[0:C_LEN[n], n, 96 * k:96 * k + 96], ident[0:C_LEN[n], 0:C_LEN[n]])
                return mm

            def attend(m, p2, projected):
                pe.wait_ge(fm, 4 * m + 8)
                for g in range(2):
                    for part in range(2):
                        for r in range(2):
                            n = 4 * g + 2 * part + r
                            bank = B[3 + n % 4]
                            if n >= 4:
                                pe.wait_ge(masked, 8 * m + n - 3)
                            elif projected:
                                pe.wait_ge(qk_read, 4 * (m + 1) + n + 1)
                            kh = qk[AD * r:AD * r + AD, p2, 2 + g, :]
                            qh = qk[AD * r:AD * r + AD, p2, g, :]
                            if part == 0:
                                mm = pe.matmul(bank[0:CH, 0:SEQ], kh[:, 0:CH], qh[:, 0:SEQ], start=True, stop=True)
                            else:
                                w1 = SEQ - C_OFF[1]
                                pe.matmul(bank[0:CH, 0:w1], kh[:, C_OFF[1]:C_OFF[1] + CH], qh[:, C_OFF[1]:SEQ], start=True, stop=True)
                                mm = pe.matmul(bank[0:CH, w1:w1 + C_LEN[2]], kh[:, C_OFF[2]:PADT], qh[:, C_OFF[2]:SEQ],
                                               start=True, stop=True)
                            mm.then_inc(at_done, 1)

            def queries_keys(m, p2, attended, finished):
                pe.wait_ge(xT_lo, m + 1)
                pe.wait_ge(xT_hi, m + 1)
                if finished:
                    pe.wait_ge(h2_ready, m - 1)
                elif attended:
                    pe.wait_ge(vg_ready, m)
                for n, (w, c) in enumerate(((wq, 0), (wq, 1), (wk, 0), (wk, 1))):
                    for k in range(KD):
                        mm = pe.matmul(B[3 + n][:, 0:SEQ], w[:, k, 128 * c:128 * c + 128], xT[:, p2, k, 0:SEQ],
                                       start=(k == 0), stop=(k == KD - 1))
                    mm.then_inc(qk_done, 1)

            def values_gate(m, p2, attended):
                for n, (w, width, chunks) in enumerate(((wv, DIM, (0, 1)), (wv, DIM, (2,)), (wg, D, (0, 1)), (wg, D, (2,)))):
                    if attended:
                        pe.wait_ge(masked, 8 * (m - 1) + n + 5)
                    else:
                        pe.wait_ge(qk_read, 4 * m + n + 1)
                    for c, cc in enumerate(chunks):
                        for k in range(KD):
                            mm = pe.matmul(B[3 + n][0:CH, c * width:(c + 1) * width], xT[:, p2, k, C_OFF[cc]:C_OFF[cc] + CH], w[:, k, :],
                                           start=(k == 0), stop=(k == KD - 1))
                    mm.then_inc(vg_done, 1)

            def numerators(m, p2, projected):
                pe.wait_ge(masked, 8 * m + 8)
                if projected:
                    pe.wait_ge(vg_ready, m + 2)
                for n in range(NC_):
                    for hh in range(AH):
                        for jj in range(n + 1):
                            at0 = (AT0, AT1, AT2)[jj] + C_OFF[n] - C_OFF[jj]
                            mm = pe.matmul(B[3 + n][0:C_LEN[n], hh * (AD + 1):(hh + 1) * (AD + 1)],
                                           at[0:C_LEN[jj], hh, at0:at0 + C_LEN[n]], va[0:C_LEN[jj], p2, jj, hh, :],
                                           start=(jj == 0), stop=(jj == n))
                    mm.then_inc(num_done, 1)

            def counts(m):
                pe.wait_ge(hot_ready, m + 1)
                for n in range(NC_):
                    for jj in range(n + 1):
                        w = tri if jj == n else ones
                        pe.matmul(B[7][0:CH, n * EXP:(n + 1) * EXP], w[0:C_LEN[jj], :], hot[0:C_LEN[jj], jj, :],
                                  start=(jj == 0), stop=(jj == n))
                for jj in range(NC_):
                    mm = pe.matmul(B[7][0:CH, NC_ * EXP:(NC_ + 1) * EXP], ones[0:C_LEN[jj], :], hot[0:C_LEN[jj], jj, :],
                                   start=(jj == 0), stop=(jj == NC_ - 1))
                mm.then_inc(cum_done, 1)

            def turn(i, p4, a, b1, b2, c):
                p2 = p4 % 2
                q2 = 1 - p2
                if a:
                    tokens(i, p2)
                if b1:
                    queries_keys(i - 1, q2, attended=b2, finished=c)
                if c:
                    pe.wait_ge(normed, i - 2)
                    turned(rt[:, q2, :, :]).then_inc(nT_turned, 1)
                if b2:
                    attend(i - 2, p2, projected=b1)
                if b1:
                    values_gate(i - 1, q2, attended=b2)
                if c:
                    pe.wait_ge(nT_ready, i - 2)
                    pe.wait_ge(slots_ready, i - 2)
                    for n in range(NC_):
                        for k in range(KD):
                            mm = pe.matmul(B[7][0:CH, n * EXP:(n + 1) * EXP], nT[:, k, C_OFF[n]:C_OFF[n] + CH], wr[:, k, :],
                                           start=(k == 0), stop=(k == KD - 1))
                    mm.then_inc(lg_done, 1)
                if b2:
                    numerators(i - 2, p2, projected=b1)
                if a:
                    pe.wait_ge(ln1, i + 1)
                    turned(ln).then_inc(xT_turned, 1)
                if b2:
                    pe.wait_ge(o_ready, i - 1)
                    if a:
                        pe.wait_ge(xT_lo, i + 1)
                        pe.wait_ge(xT_hi, i + 1)
                    for k in range(2):
                        for n in range(NC_):
                            mm = pe.transpose(B[1 + k][:, C_OFF[n]:C_OFF[n] + C_LEN[n]],
                                              o[0:C_LEN[n], n, 2 * k:2 * k + 2, :].rearrange("p h e -> p (h e)"),
                                              ident[0:C_LEN[n], 0:C_LEN[n]])
                    mm.then_inc(oT_turned, 1)
                if c:
                    counts(i - 3)
                if b2:
                    pe.wait_ge(oT_ready, i - 1)
                    pe.wait_ge(oT_high, i - 1)
                    for n in range(NC_):
                        bank, col = (B[6], n * D) if n < 2 else (B[3], 0)
                        for k in range(2):
                            mm = pe.matmul(bank[0:CH, col:col + D], oT[:, k, C_OFF[n]:C_OFF[n] + CH], wo[:, k, :],
                                           start=(k == 0), stop=(k == 1))
                    mm.then_inc(y_done, 1)
            turns(pe, turn)

        @block.vector
        def _(dve):
            ch = Chain(dve, chain)
            dve.sem_inc(h_ready, 1)
            dve.sem_inc(fm, 4)
            dve.sem_inc(slots_ready, 1)
            dve.wait_ge(loaded, 16 * LOADS)
            dve.wait_ge(made, MADE)
            ch.step(dve.tensor_tensor(posb[:], posb[:], bias[:], ALU.add))
            ch.step(dve.tensor_copy(tri[:], mask[:, 0:CH]))
            ch.step(dve.tensor_scalar(run[:], rank[:, 0, :], -float(REGION), float(REGION * EXP - 1), ALU.mult, ALU.add))
            ch.settle()
            ch.step(dve.tensor_scalar(tid[:, 2:3], tid[:, 2:3], float(C_OFF[2] - 2 * CH - 0), None, ALU.add))
            ch.settle()
            ch.step(dve.tensor_scalar(tid[:], tid[:], -float(SEQ), None, ALU.add))
            ch.settle()

            def turn(i, p4, a, b1, b2, c):
                p2 = p4 % 2
                q2 = 1 - p2
                hc = (p4 + 1) % 4
                if c:
                    dve.wait_ge(h2_ready, i - 2)
                    for n in range(NC_):
                        mm = dve.bn_stats(out=st2[:, n, :], in_=h[:, hc, n, :])
                    ch.step(mm)
                    ch.settle()
                    carry(dve, passed_dve)
                    for n in range(NC_):
                        mm = dve.bn_aggr(out=mv2[:, n, :], in_=st2[:, n, :])
                    ch.step(mm)
                    ch.settle()
                    dve.tensor_scalar(ve2[:], mv2[:, :, 1], LN_EPS, None, ALU.add).then_inc(var2, 1)
                if c:
                    dve.wait_ge(rstd2, i - 2)
                    if not isinstance(i, int) or i > 3:
                        dve.wait_ge(base_ready, i - 3)
                    for n in range(NC_):
                        mm = dve.tensor_scalar(ln2[:, n, :], h[:, hc, n, :], mv2[:, n, 0:1], rs2[:, n:n + 1], ALU.subtract, ALU.mult)
                    mm.then_inc(l_ready, 1)
                    dve.wait_ge(l_ready, i - 2)
                    dve.wait_ge(rms_ready, i - 2)
                    if not isinstance(i, int) or i >= 5:
                        dve.wait_ge(rows_out[q2], 48 * (i - 3 - (1 - p2)) if not isinstance(i, int) else 96 * ((i - 3) // 2))
                    for n in range(NC_):
                        mm = dve.scalar_tensor_tensor(out=rt[:, q2, n, 0:D], in0=ln2[:, n, :], scalar=rms[:, n:n + 1],
                                                      in1=lnw[:], op0=ALU.mult, op1=ALU.mult)
                    mm.then_inc(normed, 1)
                if a:
                    dve.wait_ge(tok_done, i + 3)
                    dve.tensor_tensor(h[:, p4, 0:2, :], B[0][0:CH, 0:2 * D].rearrange("p (c n) -> p c n", c=2), posb[:],
                                      ALU.add).then_inc(h_ready, 1)
                    dve.wait_ge(h_ready, i + 2)
                    dve.wait_ge(text_ready, i + 1)
                    for n in range(NC_):
                        mm = dve.bn_stats(out=st1[:, n, :], in_=h[:, p4, n, :])
                    ch.step(mm)
                    ch.settle()
                    carry(dve, passed_dve)
                    for n in range(NC_):
                        mm = dve.bn_aggr(out=mv1[:, n, :], in_=st1[:, n, :])
                    ch.step(mm)
                    ch.settle()
                    dve.tensor_scalar(ve1[:], mv1[:, :, 1], LN_EPS, None, ALU.add).then_inc(var1, 1)
                if b1:
                    for n in range(4):
                        dve.wait_ge(qk_read, 4 * (i - 1) + n + 1)
                        dve.scalar_tensor_tensor(out=qk[:, q2, n, 0:SEQ], in0=e_sb[:, n, :], scalar=1.0, in1=r_sb[:, n, :],
                                                 op0=ALU.min, op1=ALU.add).then_inc(fm, 1)
                if b2:
                    for n in range(8):
                        hh, part = 2 * (n // 4) + n % 2, (n % 4) // 2
                        dve.wait_ge(at_done, 8 * (i - 2) + n + 1)
                        lo, hi = (AT0, AT1) if part == 0 else (AT1, ATW)
                        dve.tensor_tensor(at[:, hh, lo:hi], B[3 + n % 4][0:CH, 0:hi - lo], mask[:, lo:hi], ALU.mult).then_inc(masked, 1)
                if a:
                    dve.wait_ge(rstd1, i + 1)
                    if not isinstance(i, int) or i >= 1:
                        dve.wait_ge(xT_turned, i)
                    for n in range(NC_):
                        mm = dve.tensor_scalar(ln[:, n, :], h[:, p4, n, :], mv1[:, n, 0:1], rs1[:, n:n + 1], ALU.subtract, ALU.mult)
                    mm.then_inc(ln1, 1)
                if c:
                    lg = B[7][0:CH, 0:NC_ * EXP].rearrange("p (c e) -> p c e", c=NC_)
                    wide = [CH, NC_, EXP]
                    dve.wait_ge(lg_done, i - 2)
                    ch.step(dve.tensor_reduce(out=best[:], in_=lg, axis=AX.X, op=ALU.max))
                    ch.settle()
                    dve.tensor_tensor(less[:], lg, best[:].unsqueeze(2).to_broadcast(wide), ALU.subtract).then_inc(ex_in, 1)
                    ch.step(dve.tensor_tensor(eq[:], lg, best[:].unsqueeze(2).to_broadcast(wide), ALU.is_equal))
                    ch.settle()
                    ch.step(dve.tensor_tensor(ranked[:], eq[:], rank[:], ALU.mult))
                    ch.settle()
                    ch.step(dve.tensor_reduce(out=first[:], in_=ranked[:], axis=AX.X, op=ALU.max))
                    ch.settle()
                    dve.tensor_tensor(hot[:], rank[:], first[:].unsqueeze(2).to_broadcast(wide), ALU.is_equal).then_inc(hot_ready, 1)
                    dve.wait_ge(ex_ready, i - 2)
                    ch.step(dve.tensor_reduce(out=esum[:], in_=ex[:], axis=AX.X, op=ALU.add))
                    ch.settle()
                    dve.reciprocal(rt[:, q2, :, 2 * D:2 * D + 1].rearrange("p c o -> p (c o)"), esum[:]).then_inc(rp_ready, 1)
                if b2:
                    for n in range(NC_):
                        dve.wait_ge(num_done, 3 * (i - 2) + n + 1)
                        num = B[3 + n][0:C_LEN[n], 0:AH * (AD + 1)].rearrange("p (h e) -> p h e", h=AH)
                        ch.step(dve.tensor_scalar(den[0:C_LEN[n], n, :], num[:, :, AD], 1e-6, None, ALU.max))
                        ch.settle()
                        ch.step(dve.reciprocal(rden[0:C_LEN[n], n, :], den[0:C_LEN[n], n, :]))
                        ch.settle()
                        mm = dve.tensor_tensor(o[0:C_LEN[n], n, :, :], num[:, :, 0:AD],
                                               rden[0:C_LEN[n], n, :].unsqueeze(2).to_broadcast([C_LEN[n], AH, AD]), ALU.mult)
                    mm.then_inc(o_ready, 1)
                if a:
                    dve.wait_ge(xT_turned, i + 1)
                    dve.tensor_copy(xT[:, p2, 1, 0:SEQ], B[2][0:96, 0:SEQ]).then_inc(xT_hi, 1)
                if b2:
                    dve.wait_ge(oT_turned, i - 1)
                    dve.tensor_copy(oT[:, 1, 0:SEQ], B[2][:, 0:SEQ]).then_inc(oT_high, 1)
                if c:
                    cum = B[7][0:CH, 0:NC_ * EXP].rearrange("p (c e) -> p c e", c=NC_)
                    dve.wait_ge(cum_done, i - 2)
                    dve.tensor_tensor(at_cum[:], cum, hot[:], ALU.mult)
                    ch.step(dve.tensor_tensor(at_run[:], hot[:], run[:].unsqueeze(1).to_broadcast(wide), ALU.mult))
                    ch.settle()
                    dve.tensor_reduce(out=prio[:], in_=at_cum[:], axis=AX.X, op=ALU.add)
                    ch.step(dve.tensor_reduce(out=place[:], in_=at_run[:], axis=AX.X, op=ALU.add))
                    ch.step(dve.scalar_tensor_tensor(out=run[:], in0=B[7][0:CH, NC_ * EXP:(NC_ + 1) * EXP], scalar=float(CAP),
                                                     in1=run[:], op0=ALU.min, op1=ALU.add))
                    ch.step(dve.tensor_scalar(tid[:], tid[:], float(SEQ), None, ALU.add))
                    ch.settle()
                    dve.tensor_scalar(over[:], prio[:], CAP + 0.5, float(NO_ROW), ALU.is_gt, ALU.mult)
                    ch.step(dve.tensor_tensor(slot0[:], prio[:], place[:], ALU.add))
                    ch.settle()
                    if not isinstance(i, int) or i >= 5:
                        dve.wait_ge(slots_out[q2], 24 * (i - 3 - (1 - p2)) if not isinstance(i, int) else 48 * ((i - 3) // 2))
                    dve.tensor_copy(tid_i[:, q2, :], tid[:])
                    dve.tensor_tensor(slot[:, q2, :], slot0[:], over[:], ALU.add).then_inc(slots_ready, 1)
                if b2:
                    dve.wait_ge(y_done, i - 1)
                    dve.scalar_tensor_tensor(out=gated[:, 0:2, :], in0=th[:, p2, 0:2, :], scalar=1.0,
                                             in1=B[6][0:CH, 0:2 * D].rearrange("p (c n) -> p c n", c=2), op0=ALU.add, op1=ALU.mult)
                    ch.step(dve.scalar_tensor_tensor(out=gated[:, 2, :], in0=th[:, p2, 2, :], scalar=1.0, in1=B[3][0:CH, 0:D],
                                                     op0=ALU.add, op1=ALU.mult))
                    ch.settle()
                    dve.scalar_tensor_tensor(out=h[:, (p4 + 2) % 4, :, :], in0=gated[:], scalar=0.5, in1=h[:, (p4 + 2) % 4, :, :],
                                             op0=ALU.mult, op1=ALU.add).then_inc(h2_ready, 1)

            PER = 21
            for i in range(4):
                turn(i, i, i >= 0, i >= 1, i >= 2, i >= 3)
            done = ch.n
            with dve.Fori(0, BATCH // 4 - 1) as j:
                for k in range(4):
                    ch.base, ch.n = done + (4 * j + k) * PER, 0
                    turn(4 * j + 4 + k, k, True, True, True, True)
                    assert ch.n == PER, ch.n
            ch.base, ch.n = done + (BATCH - 4) * PER, 0
            for i in range(BATCH, BATCH + 3):
                turn(i, i % 4, False, i - 1 < BATCH, i - 2 < BATCH, True)
            ch.settle()


def moe_phase(nc, io, out, ident, rows_dram, table_dram, run, sems):
    with ExitStack() as ctx:
        S = Scope(nc, ctx, "m")
        S.sem = lambda name: sems.sem(f"m_{name}")
        wi0 = S.sb("wi0", [128, EXP, F])
        wir = S.sb("wir", [128, EXP, F // 2])
        wo = S.sb("wo", [128, EXP, FC, D])
        cnt = S.sb("cnt", [1, EXP])
        cnt_i, nt_i = S.sb("cnt_i", [1, EXP], I32), S.sb("nt_i", [1, EXP], I32)
        nt = S.sb("nt", [1, EXP])
        below = S.sb("below", [1, EXP, EXP])
        upto = S.sb("upto", [1, EXP, EXP])
        ends = S.sb("ends", [1, EXP])
        rank = S.sb("rank", [1, EXP])
        tnum = S.sb("tnum", [1, TILES])
        past = S.sb("past", [1, TILES, EXP])
        start = S.sb("start", [1, TILES])
        expert = S.sb("expert", [1, TILES])
        expert_i, offs_i = S.sb("expert_i", [1, TILES], I32), S.sb("offs_i", [1, TILES], I32)
        offs = S.sb("offs", [1, TILES])
        N3 = 3
        idt = S.sb("ids", [TILE, N3], I32)
        ids_g, ids_s = S.sb("ids_g", [TILE, N3], I32), S.sb("ids_s", [TILE, N3], I32)
        g = S.sb("rows", [TILE, N3, ROW])
        xa = S.sb("xa", [128, TILE])
        xr = S.sb("xr", [128, 2, TILE])
        hid = S.sb("hid", [TILE, F])
        hidT = S.sb("hidT", [128, FC, TILE])
        ob = S.sb("ob", [TILE, N3, D])
        ps_x, ps_y = S.ps("x", [128, 512]), S.ps("y", [128, 512])
        ps_u = [S.ps("u0", [128, 512]), S.ps("u1", [128, 512])]
        ps_t = [S.ps("t0", [128, 512]), S.ps("t1", [128, 512])]
        FH = F // 2
        loaded, small, made, tiles_ready = S.sem("loaded"), S.sem("small"), S.sem("made"), S.sem("tiles_ready")
        ids_in = [S.sem(f"ids_in{n}") for n in range(N3)]
        rows_in = [S.sem(f"rows_in{n}") for n in range(N3)]
        rows_out = [S.sem(f"rows_out{n}") for n in range(N3)]
        (x_turned, x_ready, up_done, relu_lo, relu_hi, h_turned, hT_lo, hT_hi, y_done, y_ready, chain, passed) = (S.sem(n) for n in (
            "x_turned", "x_ready", "up_done", "relu_lo", "relu_hi", "h_turned", "hT_lo", "hT_hi", "y_done", "y_ready", "chain", "passed"))
        passed_sp, ids_taken, ids_kept = S.sem("passed_sp"), S.sem("ids_taken"), S.sem("ids_kept")
        block = ctx.enter_context(nc.Block())
        GRP = TILES // N3
        assert GRP * N3 == TILES

        @block.sync
        def _(sp):
            sp.dma_start(below[:], io["below"]).then_inc(small, 16)
            sp.dma_start(tnum[:], io["tnum"]).then_inc(small, 16)
            sp.dma_start(rank[:], io["rank"][0:1, 0, :]).then_inc(small, 16)
            sp.dma_start(wi0[:], io["wi0"]).then_inc(loaded, 16)
            sp.dma_start(wir[:], io["wir"]).then_inc(loaded, 16)
            sp.dma_start(wo[:], io["wo"]).then_inc(loaded, 16)
            sp.wait_ge(tiles_ready, 1)

            def load_ids(j, p):
                off = sp.value_load(offs_i[0:1, ds(N3 * j + p, 1)], min_val=0, max_val=EXP * REGION)
                if not isinstance(j, int):
                    sp.wait_ge(ids_taken, N3 * j + p - N3 + 1)
                    carry(sp, passed_sp)
                sp.dma_start(idt[:, p:p + 1], table_dram[ds(off, TILE), :]).then_inc(ids_in[p], 16)

            for p in range(N3):
                load_ids(0, p)
            with sp.Fori(1, GRP) as j:
                for p in range(N3):
                    load_ids(j, p)

        @block.gpsimd
        def _(pool):
            pool.memset(g[:], 0.0).then_inc(made, 1)
            pool.memset(xr[:], 0.0).then_inc(made, 1)
            pool.wait_ge(made, 2)

            def gather(t, j, p):
                pool.wait_ge(ids_in[p], 16 * j + 16)
                carry(pool, passed)
                pool.tensor_copy(ids_g[:, p:p + 1], idt[:, p:p + 1]).then_inc(ids_taken, 1)
                pool.wait_ge(ids_taken, t + 1)
                pool.wait_ge(y_ready, t + 1)
                carry(pool, passed)
                pool.indirect_dma_start(
                    out=g[:, p, :], out_offset=None, in_=rows_dram,
                    in_offset=bass.IndirectOffsetOnAxis(ap=ids_g[:, p:p + 1], axis=0),
                    bounds_check=BATCH * SEQ - 1, oob_is_err=False).then_inc(rows_in[p], 16)

            def scatter(t, j, p):
                if not isinstance(j, int) or j > 0:
                    pool.wait_ge(rows_out[p], 16 * j)
                carry(pool, passed)
                pool.tensor_copy(ids_s[:, p:p + 1], ids_g[:, p:p + 1]).then_inc(ids_kept, 1)
                pool.wait_ge(ids_kept, t + 1)
                pool.wait_ge(y_ready, t + 4)
                carry(pool, passed)
                pool.indirect_dma_start(
                    out=out.rearrange("b t n -> (b t) n"), out_offset=bass.IndirectOffsetOnAxis(ap=ids_s[:, p:p + 1], axis=0),
                    in_=ob[:, p, :], in_offset=None,
                    bounds_check=BATCH * SEQ - 1, oob_is_err=False).then_inc(rows_out[p], 16)

            gather(0, 0, 0)
            gather(1, 0, 1)

            def three(j):
                for p in range(N3):
                    gather(N3 * j + p + 2, j + (p + 2) // N3, (p + 2) % N3)
                    scatter(N3 * j + p, j, p)

            three(0)
            with pool.Fori(1, GRP - 1) as j:
                three(j)
            gather(TILES - 1, GRP - 1, 2)
            for p in range(N3):
                scatter(TILES - N3 + p, GRP - 1, p)
            for p in range(N3):
                pool.wait_ge(rows_out[p], 16 * GRP)

        @block.scalar
        def _(act):
            act.wait_ge(made, 2)

            def relu(t):
                act.wait_ge(up_done, t + 1)
                act.activation(hid[:, 0:FH], ps_u[0][:, 0:FH], ACT.Relu).then_inc(relu_lo, 1)

            def hT(t):
                act.wait_ge(h_turned, t + 1)
                act.activation(hidT[:, 0:3, :], ps_t[0][:, 0:FH].rearrange("p (f t) -> p f t", f=3), ACT.Copy).then_inc(hT_lo, 1)

            def x_copy(t):
                act.wait_ge(x_turned, t + 1)
                act.activation(xa[:], ps_x[:, 0:TILE], ACT.Copy)
                act.activation(xr[0:D1, 0, :], ps_x[0:D1, TILE:2 * TILE], ACT.Copy)
                act.activation(xr[D1:128, 1, :], ps_x[0:D1, TILE:2 * TILE], ACT.Copy).then_inc(x_ready, 1)

            act.sem_inc(x_ready, 1)
            x_copy(0)
            relu(0)
            x_copy(1)
            with act.Fori(0, TILES - 2) as t:
                hT(t)
                relu(t + 1)
                x_copy(t + 2)
            hT(TILES - 2)
            relu(TILES - 1)
            hT(TILES - 1)

        @block.tensor
        def _(pe):
            pe.wait_ge(loaded, 48)
            pe.wait_ge(tiles_ready, 1)

            def turn_x(t, j, p):
                pe.wait_ge(rows_in[p], 16 * j + 16)
                pe.wait_ge(x_ready, t + 1)
                pe.transpose(ps_x[:, 0:TILE], g[:, p, 0:D0], ident[:])
                pe.transpose(ps_x[0:D1, TILE:2 * TILE], g[:, p, D0:D], ident[:]).then_inc(x_turned, 1)

            def up(t):
                e = pe.value_load(expert_i[0:1, ds(t, 1)], min_val=0, max_val=EXP - 1)
                pe.wait_ge(x_ready, t + 2)
                for half in range(2):
                    pe.matmul(ps_u[half][:, 0:FH], xa[:], wi0[:, ds(e, 1), half * FH:(half + 1) * FH].rearrange("p e f -> p (e f)"),
                              start=True, stop=False)
                    mm = pe.matmul(ps_u[half][:, 0:FH], xr[:, half, :], wir[:, ds(e, 1), :].rearrange("p e f -> p (e f)"),
                                   start=False, stop=True)
                mm.then_inc(up_done, 1)

            def turn_h(t):
                pe.wait_ge(relu_lo, t + 1)
                pe.wait_ge(relu_hi, t + 1)
                for f in range(FC):
                    mm = pe.transpose(ps_t[f // 3][:, (f % 3) * TILE:(f % 3 + 1) * TILE], hid[:, f * 128:(f + 1) * 128], ident[:])
                mm.then_inc(h_turned, 1)

            def down(t):
                e = pe.value_load(expert_i[0:1, ds(t, 1)], min_val=0, max_val=EXP - 1)
                pe.wait_ge(hT_lo, t + 1)
                pe.wait_ge(hT_hi, t + 1)
                pe.wait_ge(y_ready, t + 3)
                for f in range(FC):
                    mm = pe.matmul(ps_y[:, 0:D], hidT[:, f, :], wo[:, ds(e, 1), f, :].rearrange("p e n -> p (e n)"),
                                   start=(f == 0), stop=(f == FC - 1))
                mm.then_inc(y_done, 1)

            turn_x(0, 0, 0)
            up(0)
            turn_x(1, 0, 1)
            with pe.Fori(0, GRP - 1) as j:
                for p in range(N3):
                    t = N3 * j + p
                    turn_h(t)
                    up(t + 1)
                    down(t)
                    turn_x(t + 2, j + (p + 2) // N3, (p + 2) % N3)
            t = TILES - 3
            turn_h(t)
            up(t + 1)
            down(t)
            turn_x(t + 2, GRP - 1, 2)
            turn_h(t + 1)
            up(t + 2)
            down(t + 1)
            turn_h(t + 2)
            down(t + 2)

        @block.vector
        def _(dve):
            ch = Chain(dve, chain)
            dve.sem_inc(y_ready, 3)
            dve.wait_ge(small, 48)
            dve.wait_ge(made, 2)
            ch.step(dve.scalar_tensor_tensor(out=cnt[:], in0=rank[:], scalar=float(REGION), in1=run[0:1, :], op0=ALU.mult, op1=ALU.add))
            ch.settle()
            ch.step(dve.tensor_scalar(cnt_i[:], cnt[:], float(1 - REGION * EXP + TILE - 1), None, ALU.add))
            ch.settle()
            ch.step(dve.tensor_scalar(nt_i[:], cnt_i[:], TILE.bit_length() - 1, None, ALU.arith_shift_right))
            ch.settle()
            ch.step(dve.tensor_copy(nt[:], nt_i[:]))
            ch.settle()
            ch.step(dve.tensor_tensor(upto[:], below[:], nt[:].unsqueeze(1).to_broadcast([1, EXP, EXP]), ALU.mult))
            ch.settle()
            ch.step(dve.tensor_reduce(out=ends[:], in_=upto[:], axis=AX.X, op=ALU.add))
            ch.settle()
            w = [1, TILES, EXP]
            ch.step(dve.tensor_tensor(past[:], tnum[:].unsqueeze(2).to_broadcast(w), ends[:].unsqueeze(1).to_broadcast(w), ALU.is_ge))
            ch.settle()
            ch.step(dve.tensor_reduce(out=expert[:], in_=past[:], axis=AX.X, op=ALU.add))
            ch.settle()
            ch.step(dve.tensor_tensor(past[:], past[:], nt[:].unsqueeze(1).to_broadcast(w), ALU.mult))
            ch.settle()
            ch.step(dve.tensor_reduce(out=start[:], in_=past[:], axis=AX.X, op=ALU.add))
            ch.settle()
            ch.step(dve.tensor_tensor(start[:], tnum[:], start[:], ALU.subtract))
            ch.settle()
            ch.step(dve.tensor_scalar(start[:], start[:], float(TILE), None, ALU.mult))
            ch.settle()
            ch.step(dve.scalar_tensor_tensor(out=offs[:], in0=expert[:], scalar=float(REGION), in1=start[:], op0=ALU.mult, op1=ALU.add))
            ch.settle()
            dve.tensor_scalar(offs_i[:], offs[:], float(EXP * REGION), None, ALU.min)
            ch.step(dve.tensor_scalar(expert_i[:], expert[:], float(EXP - 1), None, ALU.min))
            ch.settle()
            dve.sem_inc(tiles_ready, 1)

            def relu(t):
                dve.wait_ge(up_done, t + 1)
                dve.tensor_scalar(hid[:, FH:F], ps_u[1][:, 0:FH], 0.0, None, ALU.max).then_inc(relu_hi, 1)

            def hT(t):
                dve.wait_ge(h_turned, t + 1)
                dve.tensor_copy(hidT[:, 3:6, :], ps_t[1][:, 0:FH].rearrange("p (f t) -> p f t", f=3)).then_inc(hT_hi, 1)

            def finish(t, j, p):
                dve.wait_ge(y_done, t + 1)
                if not isinstance(j, int) or j > 0:
                    dve.wait_ge(rows_out[p], 16 * j)
                dve.scalar_tensor_tensor(out=ob[:, p, :], in0=ps_y[:, 0:D], scalar=g[:, p, 2 * D:2 * D + 1], in1=g[:, p, D:2 * D],
                                         op0=ALU.mult, op1=ALU.add).then_inc(y_ready, 1)

            relu(0)

            def three(j):
                for p in range(N3):
                    t = N3 * j + p
                    hT(t)
                    relu(t + 1)
                    finish(t, j, p)

            three(0)
            with dve.Fori(1, GRP - 1) as j:
                three(j)
            t = TILES - 3
            hT(t)
            relu(t + 1)
            finish(t, GRP - 1, 0)
            hT(t + 1)
            relu(t + 2)
            finish(t + 1, GRP - 1, 1)
            hT(t + 2)
            finish(t + 2, GRP - 1, 2)


def build(nc, io, out):
    with ExitStack() as ctx:
        S = Scope(nc, ctx, "g")
        rows_dram = nc.dram_tensor("token_rows", [BATCH * SEQ, ROW], F32, kind="Internal").ap()
        table_dram = nc.dram_tensor("expert_table", [TABLE, 1], I32, kind="Internal").ap()
        ident = S.sb("ident", [128, 128])
        run = S.sb("run", [CH, EXP])
        made = S.sem("made")
        with nc.Block() as block:
            @block.gpsimd
            def _(pool):
                pool.memset(ident[:], 0.0).then_inc(made, 1)
                pool.wait_ge(made, 1)
                pool.affine_select(out=ident[:], in_=ident[:], compare_op=ALU.not_equal, fill=1.0, base=0,
                                   pattern=[[-1, 128]], channel_multiplier=1).then_inc(made, 1)
                pool.wait_ge(made, 2)
        with ExitStack() as texts:
            txt = Scope(nc, texts, "g").sb("txt", [TXT, BATCH, D])
            text_phase(nc, io, txt, ident, S)
            fusion_phase(nc, io, out, txt, ident, rows_dram, table_dram, run, S)
        moe_phase(nc, io, out, ident, rows_dram, table_dram, run, S)


def layout(inputs):
    a = {k: np.asarray(v) for k, v in inputs.items()}
    f = np.float32
    r = {}
    r["ids"] = np.ascontiguousarray(a["x_txt"].T)
    r["emb"] = a["L0_txt_emb"]
    p, i = np.meshgrid(np.arange(TXT), np.arange(D // 2))
    pe = np.zeros((TXT, D), f)
    pe[:, ::2] = np.sin(p / 2500 ** (2 * i / D)).T
    pe[:, 1::2] = np.cos(p / 2500 ** (2 * i / D)).T
    pos = np.zeros((128, 2, TXT), f)
    pos[:, 0] = pe.T[0:D0]
    pos[0:D1, 1] = pe.T[D0:D]
    r["pos"] = pos
    wqk = np.zeros((SLICE + 1, 2, 3, 4, 32), f)
    for s, n in enumerate("qk"):
        wqk[0:SLICE, s, :, :, 0:HD] = a[f"L0_txt_W{n}"].reshape(SLICE, 3, 4, HD)
        wqk[SLICE, s, :, :, 0:HD] = a[f"L0_txt_b{n}"].reshape(3, 4, HD)
    r["wqk"] = wqk.reshape(SLICE + 1, 2, 3, 128)
    wv = np.zeros((SLICE + 1, TH, HD + 1), f)
    wv[0:SLICE, :, 0:HD] = a["L0_txt_Wv"].reshape(SLICE, TH, HD)
    wv[SLICE, :, 0:HD] = a["L0_txt_bv"].reshape(TH, HD)
    wv[SLICE, :, HD] = 1.0
    r["wv"] = wv.reshape(SLICE + 1, VA)
    r["Wf"] = a["L0_txt_Wf"]
    vecs = np.zeros((128, 5, 2), f)
    for n, name in enumerate(("bf", "g1", "b1", "g2", "b2")):
        vecs[:, n, 0] = a[f"L0_txt_{name}"][0:D0]
        vecs[0:D1, n, 1] = a[f"L0_txt_{name}"][D0:D]
    r["vecs"] = vecs
    r["ones"] = np.ones((1, 3, TXT), f)
    G, P = 14, 16
    x = a["x"].reshape(BATCH, 3, G, P, G, P).transpose(0, 1, 3, 5, 2, 4).reshape(BATCH, KP, 128, IMG)
    patches = np.zeros((BATCH, 128, KP, 2 * CH), f)
    patches[:, :, :, 1:1 + IMG] = x.transpose(0, 2, 1, 3)
    r["patches"] = patches.reshape(BATCH, 128, KP * 2 * CH)
    r["w_tok"] = a["L0_tok_W"].T.reshape(KP, 128, D).transpose(1, 0, 2)
    pe = np.zeros((2 * CH, D), f)
    pe[0:1 + IMG] = a["L0_tok_pos_emb"]
    r["pos_emb"] = pe.reshape(2, CH, D).transpose(1, 0, 2)
    tb = np.zeros((2 * CH, D), f)
    tb[0] = a["L0_tok_class_token"]
    tb[1:1 + IMG] = a["L0_tok_b"]
    r["tok_bias"] = tb.reshape(2, CH, D).transpose(1, 0, 2)
    for n in ("Wq", "Wk", "Wv", "Wo", "Wg"):
        r["a_" + n.lower()] = a["L0_attn_" + n]
    r["w_router"] = a["L0_ffn_w_router"]
    r["ln_w"] = a["L0_ffn_ln_w"]
    s, t = np.arange(CH)[:, None], np.arange(SEQ)[None, :]
    r["mask"] = np.concatenate([(t[:, o:] >= s + o) for o in C_OFF], axis=1).astype(f)
    r["rank"] = np.broadcast_to(np.arange(EXP, 0, -1, dtype=f), (CH, NC_, EXP))
    r["below"] = np.tril(np.ones((EXP, EXP), f))[None]
    r["tnum"] = np.arange(TILES, dtype=f)[None]
    wi, wo = a["L0_ffn_wi"], a["L0_ffn_wo"]
    r["wi0"] = wi[:, 0:D0].transpose(1, 0, 2)
    r["wir"] = wi[:, D0:D].reshape(EXP, D1, 2, F // 2).transpose(2, 1, 0, 3).reshape(128, EXP, F // 2)
    r["wo"] = wo.reshape(EXP, FC, 128, D).transpose(2, 0, 1, 3)
    return {k: np.ascontiguousarray(v) for k, v in r.items()}


def kernel(**inputs):
    from concourse import bacc
    from concourse.bass_utils import run_bass_kernel_spmd as run

    nc = bacc.Bacc("TRN2", target_bir_lowering=False, num_devices=1)
    arrays = layout(inputs)
    io = {k: nc.dram_tensor(f"in_{k}", v.shape, mybir.dt.from_np(v.dtype), kind="ExternalInput").ap()
          for k, v in arrays.items()}
    out = nc.dram_tensor("out", [BATCH, SEQ, D], F32, kind="ExternalOutput").ap()
    build(nc, io, out)
    r = run(nc, [{f"in_{k}": v for k, v in arrays.items()}], core_ids=[0])
    return r.results[0]["out"]
```

```python
from contextlib import ExitStack

import numpy as np

import concourse.bass as bass
from concourse import mybir

F32 = mybir.dt.float32
I32 = mybir.dt.int32
BF16 = mybir.dt.bfloat16
ALU = mybir.AluOpType
ACT = mybir.ActivationFunctionType
AX = mybir.AxisListType
ds = bass.ds

BATCH = 64
TXT = 77
IMG = 196
SEQ = 1 + IMG + TXT
D = 192
D0, D1 = 128, 64
VOCAB = 8000
PATCH = 768
KP = PATCH // 128
TH = 12
HD = D // TH
SLICE = D // 3
LAYERS = 2
HHALF = TH * TXT // 2
GATHERS = 4
FCOL = 4 * TXT
FSTEPS = BATCH // 4
BN_EPS = 1e-5
LN_EPS = 1e-5

C_OFF = (0, 99, 197)
C_LEN = (99, 98, 77)
CH = 99
NC_ = 3
PADT = C_OFF[2] + CH
KD = D // 96
AH, AD = 4, 64
DIM = AH * AD
AT0, AT1, AT2 = 0, SEQ, SEQ + (SEQ - C_OFF[1])
ATW = AT2 + C_LEN[2]
EXP = 16
CAP = 64
REGION = BATCH * CAP
TILE = 128
TILES = -(-BATCH * SEQ // TILE) + EXP
TABLE = EXP * REGION + TILE
NO_ROW = 1 << 20
ROW = 2 * D + 4
F = 768
FC = F // 128


class Chain:

    def __init__(self, engine, sem):
        self.engine, self.sem, self.base, self.n = engine, sem, 0, 0

    def step(self, instruction):
        instruction.then_inc(self.sem, 1)
        self.n += 1

    def settle(self):
        self.engine.wait_ge(self.sem, self.base + self.n)

    def enter(self, offset):
        self.outer, self.base, self.n = (self.base + self.n, self.base + self.n + offset, 0)
        self.start = self.outer

    def leave(self, per_turn, turns):
        assert self.n == per_turn, self.n
        self.base, self.n = self.start + per_turn * turns, 0


class Scope:

    def __init__(self, nc, ctx, prefix):
        self.nc, self.ctx, self.prefix = nc, ctx, prefix

    def sb(self, name, shape, dt=F32):
        return self.ctx.enter_context(self.nc.sbuf_tensor(f"{self.prefix}_{name}", shape, dt))

    def ps(self, name, shape, dt=F32):
        return self.ctx.enter_context(self.nc.psum_tensor(f"{self.prefix}_{name}", shape, dt))

    def sem(self, name):
        return self.ctx.enter_context(self.nc.semaphore(f"{self.prefix}_{name}"))


def text_phase(nc, io, txt, ident, sems):
    with ExitStack() as ctx:
        S = Scope(nc, ctx, "t")
        S.sem = lambda name: sems.sem(f"t_{name}")
        h = S.sb("h", [128, 2, BATCH * TXT])
        ids = S.sb("ids", [TXT, BATCH], I32)
        ids_low = S.sb("ids_low", [TXT, BATCH])
        ids_wrapped = S.sb("ids_wrapped", [TXT, BATCH])
        ids_ok = S.sb("ids_ok", [TXT, BATCH], I32)
        ids_now = S.sb("ids_now", [TXT, 2, GATHERS], I32)
        rows = S.sb("rows", [TXT, 2, GATHERS, D])
        pos = S.sb("pos", [128, 2, TXT])
        wqk = S.sb("wqk", [SLICE + 1, 2, 3, 128])
        wv = S.sb("wv", [SLICE + 1, D])
        wf = S.sb("wf", [128, 2, D])
        vecs = S.sb("vecs", [128, 5, 2])
        hs = S.sb("hs", [SLICE + 1, 2, 3, 2 * TXT])
        q_sb = S.sb("q", [128, 2, 3, 2 * TXT])
        k_sb = S.sb("k", [128, 2, 3, 2 * TXT])
        v_sb = S.sb("v", [TXT, 4, 2 * D])
        top = S.sb("top", [TXT, 4, 3])
        rsum = S.sb("rsum", [TXT, 2, 4, 3])
        rinv = S.sb("rinv", [TXT, 2, 4, 3])
        probs = S.sb("probs", [TXT, 2, 4, 3, TXT])
        pt = S.sb("pt", [TXT, TH, TXT])
        stats = S.sb("stats", [128, 2, BATCH, 6])
        mv = S.sb("mv", [128, 2, 2])
        var_eps = S.sb("var_eps", [128, 2])
        rstd = S.sb("rstd", [128, 2])
        minus_half = S.sb("minus_half", [128, 2])
        shift = S.sb("shift", [128, 2])
        aff1 = S.sb("aff1", [128, 2, 2])
        aff2 = S.sb("aff2", [128, 2, 2])
        tb = S.sb("tb", [128, 2, 2, FCOL])

        ps_s = S.ps("scores", [128, 4, 512])
        ps_pt = S.ps("probsT", [128, 2, 512])
        ps_qk = S.ps("qk", [128, 512])
        ps_o = S.ps("mixed", [128, 512])
        v_ps = ps_s[0:TXT, 3, 3 * TXT:3 * TXT + D]
        o_ps = ps_o[:, 0:2 * TXT].rearrange("p (c t) -> p c t", c=2)

        loaded, const_ready = S.sem("loaded"), S.sem("const_ready")
        ids_ready, ids_copied = S.sem("ids_ready"), S.sem("ids_copied")
        gathered = [S.sem("gathered0"), S.sem("gathered1")]
        rows_turned, embedded, v_cleared = S.sem("rows_turned"), S.sem("embedded"), S.sem("v_cleared")
        aff1_ready, aff2_ready = S.sem("aff1_ready"), S.sem("aff2_ready")
        var_ready, rstd_ready = S.sem("var_ready"), S.sem("rstd_ready")
        base_low, base_high = S.sem("base_low"), S.sem("base_high")
        staged, projected, projection_read = S.sem("staged"), S.sem("projected"), S.sem("projection_read")
        v_projected, v_read = S.sem("v_projected"), S.sem("v_read")
        inverted, keys_staged = S.sem("inverted"), S.sem("keys_staged")
        scored, topped, exp_done, normed = S.sem("scored"), S.sem("topped"), S.sem("exp_done"), S.sem("normed")
        turned, pt_ready, mixed, added, z_ready = (S.sem("turned"), S.sem("pt_ready"), S.sem("mixed"), S.sem("added"),
                                                   S.sem("z_ready"))
        t_ready, f_ready, u_ready = S.sem("t_ready"), S.sem("f_ready"), S.sem("u_ready")
        y_ready, y_turned, y_stored = S.sem("y_ready"), S.sem("y_turned"), S.sem("y_stored")
        dve_chain, passed_dve, passed_pool = S.sem("dve_chain"), S.sem("passed_dve"), S.sem("passed_pool")

        def cols(b):
            return ds(b * TXT, TXT)

        def turns(engine, n0, pair0, turn):
            for b in range(4):
                turn(n0 + b, b, pair0 + b // 2, b)
            with engine.Fori(0, BATCH // 4 - 2) as j:
                for k in range(4):
                    turn(n0 + 4 * j + 4 + k, 4 * j + 4 + k, pair0 + 2 * j + 2 + k // 2, k)
            for b in range(BATCH - 4, BATCH):
                turn(n0 + b, b, pair0 + b // 2, b % 4)

        def within(b, ahead):
            return not isinstance(b, int) or b + ahead < BATCH

        PAIRS = BATCH // 2
        block = ctx.enter_context(nc.Block())
        LOADS = 9

        @block.sync
        def _(sp):
            sp.dma_start(ids[:], io["ids"]).then_inc(loaded, 16)
            sp.dma_start(pos[:], io["pos"]).then_inc(loaded, 16)
            sp.dma_start(wqk[:], io["wqk"]).then_inc(loaded, 16)
            sp.dma_start(wv[:], io["wv"]).then_inc(loaded, 16)
            sp.dma_start(wf[:, 0, :], io["Wf"][0:D0, :]).then_inc(loaded, 16)
            sp.dma_start(wf[0:D1, 1, :], io["Wf"][D0:D, :]).then_inc(loaded, 16)
            sp.dma_start(vecs[:], io["vecs"]).then_inc(loaded, 16)
            for par in range(2):
                sp.dma_start(hs[SLICE:SLICE + 1, par, :, :], io["ones"]).then_inc(loaded, 16)

        @block.gpsimd
        def _(pool):
            pool.memset(minus_half[:], -0.5).then_inc(const_ready, 1)
            pool.wait_ge(const_ready, 1)
            pool.wait_ge(ids_ready, 1)
            with pool.Fori(0, BATCH // (2 * GATHERS)) as j:
                for par in range(2):
                    b = 2 * GATHERS * j + par * GATHERS
                    pool.wait_ge(rows_turned, b + GATHERS)
                    pool.tensor_copy(ids_now[:, par, :], ids_ok[:, ds(b, GATHERS)]).then_inc(ids_copied, 1)
                    pool.wait_ge(ids_copied, 2 * j + par + 1)
                    pool.sem_inc(passed_pool, 1)
                    for g in range(GATHERS):
                        pool.indirect_dma_start(
                            out=rows[:, par, g, :], out_offset=None, in_=io["emb"],
                            in_offset=bass.IndirectOffsetOnAxis(ap=ids_now[:, par, g:g + 1], axis=0),
                        ).then_inc(gathered[par], 16)

            def stage(pair, first_batch, par):
                c = ds(first_batch * TXT, 2 * TXT)
                pool.tensor_copy(hs[0:SLICE, par, 1, :], h[SLICE:D0, 0, c]).then_inc(keys_staged, 1)
                pool.wait_ge(keys_staged, pair + 1)
                carry(pool, passed_pool)
                pool.tensor_copy(hs[0:SLICE, par, 0, :], h[0:SLICE, 0, c])
                pool.tensor_copy(hs[0:SLICE, par, 2, :], h[0:D1, 1, c]).then_inc(staged, 1)

            def turn(n, b, pair, p4):
                if p4 % 2 and within(b, 4):
                    pool.wait_ge(v_projected, n + 1)
                    pool.wait_ge(normed, 4 * n)
                    carry(pool, passed_pool)
                    stage(pair + 2, b + 3, p4 // 2)
                for r in range(4):
                    pool.wait_ge(inverted, 4 * n + r + 1)
                    pool.tensor_tensor(probs[:, p4 % 2, r, :, :], probs[:, p4 % 2, r, :, :],
                                       rinv[:, p4 % 2, r, :].unsqueeze(2).to_broadcast([TXT, 3, TXT]),
                                       ALU.mult).then_inc(normed, 1)

            with pool.Fori(0, LAYERS) as layer:
                pool.wait_ge(base_low, layer + 1)
                pool.wait_ge(base_high, layer + 1)
                carry(pool, passed_pool)
                stage(layer * PAIRS, 0, 0)
                pool.wait_ge(staged, layer * PAIRS + 1)
                carry(pool, passed_pool)
                stage(layer * PAIRS + 1, 2, 1)
                turns(pool, layer * BATCH, layer * PAIRS, turn)
                for k in range(2):
                    pool.wait_ge(var_ready, 2 * layer + k + 1)
                    pool.tensor_tensor(rstd[:], var_eps[:], minus_half[:], ALU.pow).then_inc(rstd_ready, 1)

        @block.scalar
        def _(act):
            act.wait_ge(loaded, 16 * LOADS)

            def turn(n, b, pair, p4):
                par = p4 % 2
                for r in range(4):
                    act.wait_ge(topped, 4 * n + r + 1)
                    for c in range(3):
                        e = act.activation(probs[:, par, r, c, :], ps_s[0:TXT, r, c * TXT:(c + 1) * TXT], ACT.Exp,
                                           bias=top[:, r, c:c + 1], accum_out=rsum[:, par, r, c:c + 1])
                    e.then_inc(exp_done, 1)
                if within(b, 1):
                    v_relu(n + 1, (p4 + 1) % 4)
                if within(b, 2):
                    (k_relu if par else q_relu)(pair + 1, (p4 // 2 + 1) % 2)

            def q_relu(pair, par):
                act.wait_ge(projected, 2 * pair + 1)
                act.activation(q_sb[:, par, :, :], ps_qk[:, 0:6 * TXT].rearrange("p (c t) -> p c t", c=3), ACT.Relu,
                               scale=float(D) ** -0.5).then_inc(projection_read, 1)

            def k_relu(pair, par):
                act.wait_ge(projected, 2 * pair + 2)
                act.activation(k_sb[:, par, :, :], ps_qk[:, 0:6 * TXT].rearrange("p (c t) -> p c t", c=3),
                               ACT.Relu).then_inc(projection_read, 1)

            def v_relu(n, par):
                act.wait_ge(v_projected, n + 1)
                v4 = v_ps.rearrange("p (g two d) -> p g two d", two=2, d=HD)
                to = v_sb[:, par, :].rearrange("p (g w) -> p g w", w=4 * HD)
                act.activation(to[:, :, 0:HD], v4[:, :, 0, :], ACT.Relu)
                act.activation(to[:, :, 3 * HD:4 * HD], v4[:, :, 1, :], ACT.Relu).then_inc(v_read, 1)

            act.wait_ge(v_cleared, 1)
            with act.Fori(0, LAYERS) as layer:
                n0, pair0 = layer * BATCH, layer * PAIRS
                act.wait_ge(aff2_ready, layer + 1)
                act.activation(h[:, 0, :], h[:, 0, :], ACT.Identity, scale=aff2[:, 0, 0:1],
                               bias=aff2[:, 1, 0:1]).then_inc(base_low, 1)
                q_relu(pair0, 0)
                k_relu(pair0, 0)
                v_relu(n0, 0)
                turns(act, n0, pair0, turn)

                act.wait_ge(aff1_ready, layer + 1)
                with act.Fori(0, FSTEPS // 2) as j:
                    for par in range(2):
                        q = 2 * j + par
                        act.wait_ge(u_ready, layer * FSTEPS + q + 1)
                        act.activation(tb[:, par, 0, :], h[:, 0, ds(q * FCOL, FCOL)], ACT.Identity,
                                       scale=aff1[:, 0, 0:1], bias=aff1[:, 1, 0:1])
                        act.activation(tb[0:D1, par, 1, :], h[0:D1, 1, ds(q * FCOL, FCOL)], ACT.Identity,
                                       scale=aff1[0:D1, 0, 1:2], bias=aff1[0:D1, 1, 1:2]).then_inc(t_ready, 1)
            act.wait_ge(aff2_ready, LAYERS + 1)
            with act.Fori(0, BATCH // 2) as j:
                for par in range(2):
                    b = 2 * j + par
                    act.wait_ge(y_stored, b + 1)
                    act.activation(tb[:, par, 0, 0:TXT], h[:, 0, cols(b)], ACT.Identity,
                                   scale=aff2[:, 0, 0:1], bias=aff2[:, 1, 0:1])
                    act.activation(tb[0:D1, par, 1, 0:TXT], h[0:D1, 1, cols(b)], ACT.Identity,
                                   scale=aff2[0:D1, 0, 1:2], bias=aff2[0:D1, 1, 1:2]).then_inc(y_ready, 1)

        @block.tensor
        def _(pe):
            pe.wait_ge(loaded, 16 * LOADS)
            pe.sem_inc(rows_turned, 2 * GATHERS)
            with pe.Fori(0, BATCH // (2 * GATHERS)) as j:
                for par in range(2):
                    pe.wait_ge(gathered[par], GATHERS * (16 * j + 16))
                    for g in range(GATHERS):
                        pe.wait_ge(embedded, 2 * GATHERS * j + par * GATHERS + g + 1)
                        pe.transpose(ps_s[:, g % 2, 0:TXT], rows[:, par, g, 0:D0], ident[0:TXT, 0:TXT])
                        pe.transpose(ps_s[0:D1, g % 2, TXT:2 * TXT], rows[:, par, g, D0:D], ident[0:TXT, 0:TXT]).then_inc(rows_turned, 1)

            def project(pair, par, which):
                pe.wait_ge(staged, pair + 1)
                for c in range(3):
                    mm = pe.matmul(ps_qk[:, 2 * c * TXT:2 * (c + 1) * TXT], wqk[:, which, c, :], hs[:, par, which, :],
                                   start=True, stop=True)
                mm.then_inc(projected, 1)

            def project_v(par, k):
                pe.matmul(v_ps, hs[:, par, 2, k * TXT:(k + 1) * TXT], wv[:], start=True, stop=True).then_inc(v_projected, 1)

            def scores(n, p4, r):
                g, t = slice(32 * r, 32 * r + 32), slice((p4 % 2) * TXT, (p4 % 2 + 1) * TXT)
                for c in range(3):
                    mm = pe.matmul(ps_s[0:TXT, r, c * TXT:(c + 1) * TXT], q_sb[g, p4 // 2, c, t], k_sb[g, p4 // 2, c, t],
                                   start=True, stop=True)
                mm.then_inc(scored, 1)

            def turn_probs(n, p4):
                for r in range(4):
                    pe.wait_ge(normed, 4 * n + r + 1)
                    for c in range(3):
                        hh = 3 * (r % 2) + c
                        mm = pe.transpose(ps_pt[0:TXT, r // 2, hh * TXT:(hh + 1) * TXT], probs[:, p4 % 2, r, c, :], ident[0:TXT, 0:TXT])
                    if r % 2:
                        mm.then_inc(turned, 1)

            def mix(n, p4):
                pe.wait_ge(added, n + 1)
                for half in range(2):
                    pe.wait_ge(pt_ready, 2 * n + half + 1)
                    for c in range(3):
                        g = 2 * c + half
                        for k in range(2):
                            mm = pe.matmul(o_ps[32 * (g % 4):32 * (g % 4) + 32, g // 4, :],
                                           v_sb[:, p4, 32 * (2 * g + k):32 * (2 * g + k) + 32],
                                           pt[:, 6 * half + 3 * k + c, :], start=(k == 0), stop=(k == 1))
                mm.then_inc(mixed, 1)

            def turn(n, b, pair, p4):
                pe.wait_ge(projection_read, 2 * pair + 2)
                for r in range(3):
                    pe.wait_ge(exp_done, 4 * n + r + 1)
                    scores(n, p4, r)
                pe.wait_ge(exp_done, 4 * n + 4)
                pe.wait_ge(v_read, n + 1)
                if within(b, 1):
                    project_v(((p4 + 1) // 2) % 2, (p4 + 1) % 2)
                scores(n, p4, 3)
                if p4 or not isinstance(b, int) or b:
                    turn_probs(n - 1, (p4 + 3) % 4)
                if within(b, 2):
                    pe.wait_ge(projection_read, 2 * pair + 2 + p4 % 2)
                    project(pair + 1, (p4 // 2 + 1) % 2, p4 % 2)
                if p4 or not isinstance(b, int) or b:
                    mix(n - 1, (p4 + 3) % 4)

            with pe.Fori(0, LAYERS) as layer:
                n0, pair0 = layer * BATCH, layer * PAIRS
                project(pair0, 0, 0)
                pe.wait_ge(projection_read, 2 * pair0 + 1)
                project(pair0, 0, 1)
                project_v(0, 0)
                turns(pe, n0, pair0, turn)
                turn_probs(n0 + BATCH - 1, 3)
                mix(n0 + BATCH - 1, 3)
                with pe.Fori(0, FSTEPS // 2) as j:
                    for par in range(2):
                        pe.wait_ge(t_ready, layer * FSTEPS + 2 * j + par + 1)
                        lo, hi = tb[:, par, 0, :], tb[0:D1, par, 1, :]
                        pe.matmul(ps_s[:, par, 0:FCOL], wf[:, 0, 0:D0], lo, start=True, stop=False)
                        pe.matmul(ps_s[:, par, 0:FCOL], wf[0:D1, 1, 0:D0], hi, start=False, stop=True)
                        pe.matmul(ps_s[0:D1, 2 + par, 0:FCOL], wf[:, 0, D0:D], lo, start=True, stop=False)
                        pe.matmul(ps_s[0:D1, 2 + par, 0:FCOL], wf[0:D1, 1, D0:D], hi, start=False, stop=True).then_inc(f_ready, 1)
            with pe.Fori(0, BATCH // 2) as j:
                for par in range(2):
                    pe.wait_ge(y_ready, 2 * j + par + 1)
                    pe.transpose(ps_s[0:TXT, par, 0:D0], tb[:, par, 0, 0:TXT], ident[:])
                    pe.transpose(ps_s[0:TXT, par, D0:D], tb[0:D1, par, 1, 0:TXT], ident[0:D1, 0:D1]).then_inc(y_turned, 1)

        @block.vector
        def _(dve):
            ch = Chain(dve, dve_chain)
            dve.sem_inc(embedded, 2)
            dve.sem_inc(added, 1)
            dve.sem_inc(exp_done, 4)
            dve.memset(v_sb[:], 0.0).then_inc(v_cleared, 1)
            dve.sem_inc(u_ready, 2)
            dve.sem_inc(y_stored, 2)
            dve.wait_ge(loaded, 16 * LOADS)
            ch.step(dve.tensor_scalar(ids_low[:], ids[:], 0.0, float(VOCAB), ALU.is_lt, ALU.mult))
            ch.settle()
            ch.step(dve.tensor_tensor(ids_wrapped[:], ids[:], ids_low[:], ALU.add))
            ch.settle()
            dve.tensor_scalar(ids_ok[:], ids_wrapped[:], 0.0, float(VOCAB - 1), ALU.max, ALU.min).then_inc(ids_ready, 1)
            dve.memset(aff2[:, 0, :], 1.0)
            ch.step(dve.memset(aff2[:, 1, :], 0.0))
            ch.step(dve.memset(mv[:], 1.0))
            ch.settle()
            with dve.Fori(0, BATCH // 2) as j:
                for par in range(2):
                    b = 2 * j + par
                    dve.wait_ge(rows_turned, b + 2 * GATHERS + 1)
                    dve.scalar_tensor_tensor(out=h[:, 0, cols(b)], in0=ps_s[:, par, 0:TXT], scalar=2.0,
                                             in1=pos[:, 0, :], op0=ALU.mult, op1=ALU.add)
                    dve.scalar_tensor_tensor(out=h[0:D1, 1, cols(b)], in0=ps_s[0:D1, par, TXT:2 * TXT], scalar=2.0,
                                             in1=pos[0:D1, 1, :], op0=ALU.mult, op1=ALU.add).then_inc(embedded, 1)
            dve.wait_ge(embedded, BATCH + 2)
            dve.sem_inc(aff2_ready, 1)

            def turn(n, b, pair, p4):
                for r in range(4):
                    dve.wait_ge(scored, 4 * n + r + 1)
                    dve.tensor_reduce(out=top[:, r, :], in_=ps_s[0:TXT, r, 0:3 * TXT].rearrange("p (c t) -> p c t", c=3),
                                      axis=AX.X, op=ALU.max, negate=True).then_inc(topped, 1)
                invert(n, p4 % 2, 0)
                if p4 or not isinstance(b, int) or b:
                    copy_probs(n - 1)
                invert(n, p4 % 2, 2)
                if p4 or not isinstance(b, int) or b:
                    add_mixed(n - 1, b - 1)

            def invert(n, par, first):
                for r in range(first, first + 2):
                    dve.wait_ge(exp_done, 4 * n + r + 5)
                    dve.reciprocal(rinv[:, par, r, :], rsum[:, par, r, :]).then_inc(inverted, 1)

            def copy_probs(n):
                for half in range(2):
                    dve.wait_ge(turned, 2 * n + half + 1)
                    dve.tensor_copy(pt[:, 6 * half:6 * half + 6, :],
                                    ps_pt[0:TXT, half, 0:HHALF].rearrange("p (h t) -> p h t", h=TH // 2)).then_inc(pt_ready, 1)

            def add_mixed(n, b):
                dve.wait_ge(mixed, n + 1)
                dve.tensor_tensor(h[:, 0, cols(b)], h[:, 0, cols(b)], o_ps[:, 0, :], ALU.add)
                dve.tensor_tensor(h[0:D1, 1, cols(b)], h[0:D1, 1, cols(b)], o_ps[0:D1, 1, :], ALU.add).then_inc(added, 1)
                dve.wait_ge(added, n + 2)
                dve.bn_stats(out=stats[:, 0, ds(b, 1), :], in_=h[:, 0, cols(b)])
                dve.bn_stats(out=stats[0:D1, 1, ds(b, 1), :], in_=h[0:D1, 1, cols(b)]).then_inc(z_ready, 1)

            def affine(aff, count, which, n, ready):
                dve.bn_aggr(out=mv[:, 0, :], in_=stats[:, 0, 0:count, :].rearrange("p n s -> p (n s)"))
                ch.step(dve.bn_aggr(out=mv[0:D1, 1, :], in_=stats[0:D1, 1, 0:count, :].rearrange("p n s -> p (n s)")))
                ch.settle()
                dve.tensor_scalar(var_eps[:], mv[:, :, 1], BN_EPS, None, ALU.add).then_inc(var_ready, 1)
                dve.wait_ge(rstd_ready, n)
                ch.step(dve.tensor_tensor(aff[:, 0, :], vecs[:, which, :], rstd[:], ALU.mult))
                ch.settle()
                ch.step(dve.tensor_tensor(shift[:], mv[:, :, 0], aff[:, 0, :], ALU.mult))
                ch.settle()
                dve.tensor_tensor(aff[:, 1, :], vecs[:, which + 1, :], shift[:], ALU.subtract).then_inc(ready, 1)

            LAYER_CHAIN = FSTEPS + 6
            with dve.Fori(0, LAYERS) as layer:
                ch.enter(layer * LAYER_CHAIN)
                start, base = ch.start, ch.base
                n0 = layer * BATCH
                dve.wait_ge(aff2_ready, layer + 1)
                dve.tensor_scalar(h[0:D1, 1, :], h[0:D1, 1, :], aff2[0:D1, 0, 1:2], aff2[0:D1, 1, 1:2],
                                  ALU.mult, ALU.add).then_inc(base_high, 1)
                turns(dve, n0, layer * PAIRS, turn)
                copy_probs(n0 + BATCH - 1)
                add_mixed(n0 + BATCH - 1, BATCH - 1)
                dve.wait_ge(z_ready, n0 + BATCH)
                dve.sem_inc(passed_dve, 1)
                affine(aff1, BATCH, 1, 2 * layer + 1, aff1_ready)
                done = ch.n
                with dve.Fori(0, FSTEPS // 2) as j:
                    for par in range(2):
                        q = 2 * j + par
                        ch.base, ch.n = base + done + q, 0
                        dve.wait_ge(f_ready, layer * FSTEPS + q + 1)
                        dve.scalar_tensor_tensor(out=h[:, 0, ds(q * FCOL, FCOL)], in0=ps_s[:, par, 0:FCOL], scalar=vecs[:, 0, 0:1],
                                                 in1=tb[:, par, 0, :], op0=ALU.add, op1=ALU.add)
                        ch.step(dve.scalar_tensor_tensor(out=h[0:D1, 1, ds(q * FCOL, FCOL)], in0=ps_s[0:D1, 2 + par, 0:FCOL],
                                                         scalar=vecs[0:D1, 0, 1:2], in1=tb[0:D1, par, 1, :], op0=ALU.add, op1=ALU.add))
                        ch.settle()
                        dve.bn_stats(out=stats[:, 0, ds(q, 1), :], in_=h[:, 0, ds(q * FCOL, FCOL)])
                        dve.bn_stats(out=stats[0:D1, 1, ds(q, 1), :], in_=h[0:D1, 1, ds(q * FCOL, FCOL)]).then_inc(u_ready, 1)
                ch.base, ch.n = base, done + FSTEPS
                dve.wait_ge(u_ready, (layer + 1) * FSTEPS + 2)
                dve.sem_inc(passed_dve, 1)
                affine(aff2, FSTEPS, 3, 2 * layer + 2, aff2_ready)
                assert ch.n == LAYER_CHAIN, ch.n
                ch.start = start
            with dve.Fori(0, BATCH // 2) as j:
                for par in range(2):
                    b = 2 * j + par
                    dve.wait_ge(y_turned, b + 1)
                    dve.tensor_copy(txt[:, ds(b, 1), :], ps_s[0:TXT, par, 0:D]).then_inc(y_stored, 1)


def carry(engine, sem):
    engine.sem_inc(sem, 1)


def fusion_phase(nc, io, out, txt, ident, rows_dram, table_dram, run, sems):
    with ExitStack() as ctx:
        S = Scope(nc, ctx, "f")
        S.sem = lambda name: sems.sem(f"f_{name}")
        xk = S.sb("patches", [128, 2, KP, 2 * CH])
        wt = S.sb("w_tok", [128, KP, D])
        posb = S.sb("pos_bias", [CH, 2, D])
        bias = S.sb("bias", [CH, 2, D])
        wq = S.sb("wq", [96, KD, DIM])
        wk = S.sb("wk", [96, KD, DIM])
        wv = S.sb("wv", [96, KD, DIM])
        wg = S.sb("wg", [96, KD, D])
        wo = S.sb("wo", [128, DIM // 128, D])
        wr = S.sb("wr", [96, KD, EXP])
        lnw = S.sb("lnw", [CH, D])
        mask = S.sb("mask", [CH, ATW])
        tri = S.sb("tri", [CH, CH], BF16)
        ones = S.sb("ones", [CH, CH], BF16)
        rank = S.sb("rank", [CH, NC_, EXP])
        minus_half = S.sb("minus_half", [CH, NC_])
        pad_ids = S.sb("pad_ids", [128, TABLE // 128], I32)
        tid = S.sb("tid", [CH, NC_])
        tid_i = S.sb("tid_i", [CH, 2, NC_], I32)

        h = S.sb("h", [CH, 4, NC_, D])
        st1, st2 = S.sb("st1", [CH, NC_, 6]), S.sb("st2", [CH, NC_, 6])
        mv1, mv2 = S.sb("mv1", [CH, NC_, 2]), S.sb("mv2", [CH, NC_, 2])
        ve1, ve2 = S.sb("ve1", [CH, NC_]), S.sb("ve2", [CH, NC_])
        rs1, rs2, rms = S.sb("rs1", [CH, NC_]), S.sb("rs2", [CH, NC_]), S.sb("rms", [CH, NC_])
        ms1, ms2, ms3 = (S.sb(n, [CH, NC_]) for n in ("ms1", "ms2", "ms3"))
        ln = S.sb("ln", [CH, NC_, D])
        xT = S.sb("xT", [96, 2, KD, PADT])
        e_sb = S.sb("e", [128, 4, SEQ])
        r_sb = S.sb("r", [128, 4, SEQ])
        qk = S.sb("qk", [128, 2, 4, PADT])
        va = S.sb("va", [CH, 2, NC_, AH, AD + 1])
        th = S.sb("th", [CH, 2, NC_, D])
        at = S.sb("at", [CH, AH, ATW])
        den, rden = S.sb("den", [CH, NC_, AH]), S.sb("rden", [CH, NC_, AH])
        o = S.sb("o", [CH, NC_, AH, AD])
        oT = S.sb("oT", [128, 2, PADT])
        gated = S.sb("gated", [CH, NC_, D])
        ln2 = S.sb("ln2", [CH, NC_, D])
        rt = S.sb("rt", [CH, 2, NC_, ROW])
        nT = S.sb("nT", [96, KD, PADT])
        best = S.sb("best", [CH, NC_])
        eq, less, ex = (S.sb(n, [CH, NC_, EXP]) for n in ("eq", "less", "ex"))
        esum = S.sb("esum", [CH, NC_])
        ranked = S.sb("ranked", [CH, NC_, EXP])
        first = S.sb("first", [CH, NC_])
        hot = S.sb("hot", [CH, NC_, EXP], BF16)
        at_cum, at_run = S.sb("at_cum", [CH, NC_, EXP]), S.sb("at_run", [CH, NC_, EXP])
        prio, place, over = (S.sb(n, [CH, NC_]) for n in ("prio", "place", "over"))
        slot0 = S.sb("slot0", [CH, NC_])
        slot = S.sb("slot", [CH, 2, NC_], I32)
        ob = S.sb("ob", [CH, 2, NC_, D])

        B = [S.ps(f"bank{n}", [128, 512]) for n in range(8)]

        loaded, made, filled = S.sem("loaded"), S.sem("made"), S.sem("filled")
        xk_in = [S.sem("xk_in0"), S.sem("xk_in1")]
        rows_out = [S.sem("rows_out0"), S.sem("rows_out1")]
        slots_out = [S.sem("slots_out0"), S.sem("slots_out1")]
        (tok_done, h_ready, text_ready, var1, rstd1, ln1, xT_turned, xT_lo, xT_hi, qk_done, qk_read, fm,
         vg_done, vg_ready, at_done, masked, num_done, o_ready, oT_turned, oT_ready, oT_high, y_done, h2_ready,
         var2, rstd2, rms_ready, l_ready, normed, base_ready, nT_turned, nT_ready, lg_done, ex_in, ex_ready,
         rp_ready, hot_ready, cum_done, slots_ready, ob_ready, pool_chain, chain, passed_dve, passed_pool) = (S.sem(n) for n in (
             "tok_done", "h_ready", "text_ready", "var1", "rstd1", "ln1", "xT_turned", "xT_lo", "xT_hi", "qk_done",
             "qk_read", "fm", "vg_done", "vg_ready", "at_done", "masked", "num_done", "o_ready", "oT_turned", "oT_ready", "oT_high",
             "y_done", "h2_ready", "var2", "rstd2", "rms_ready", "l_ready", "normed", "base_ready", "nT_turned",
             "nT_ready", "lg_done", "ex_in", "ex_ready", "rp_ready", "hot_ready", "cum_done", "slots_ready", "ob_ready",
             "pool_chain", "chain", "passed_dve", "passed_pool"))
        LOADS = 12
        MADE = 13

        def turns(engine, turn):
            for i in range(4):
                turn(i, i, i >= 0, i >= 1, i >= 2, i >= 3)
            with engine.Fori(0, BATCH // 4 - 1) as j:
                for k in range(4):
                    turn(4 * j + 4 + k, k, True, True, True, True)
            for i in range(BATCH, BATCH + 3):
                turn(i, i % 4, False, i - 1 < BATCH, i - 2 < BATCH, True)

        passed_sp = S.sem("passed_sp")
        block = ctx.enter_context(nc.Block())
        rows_v = rows_dram.rearrange("(b t) n -> b t n", t=SEQ)

        @block.sync
        def _(sp):
            sp.dma_start(wt[:], io["w_tok"]).then_inc(loaded, 16)
            sp.dma_start(posb[:], io["pos_emb"]).then_inc(loaded, 16)
            sp.dma_start(bias[:], io["tok_bias"]).then_inc(loaded, 16)
            for t, n in ((wq, "a_wq"), (wk, "a_wk"), (wv, "a_wv"), (wg, "a_wg")):
                sp.dma_start(t[:], io[n].rearrange("(k p) n -> p k n", p=96)).then_inc(loaded, 16)
            sp.dma_start(wo[:], io["a_wo"].rearrange("(k p) n -> p k n", p=128)).then_inc(loaded, 16)
            sp.dma_start(wr[:], io["w_router"].rearrange("(k p) n -> p k n", p=96)).then_inc(loaded, 16)
            sp.dma_start(lnw[:], io["ln_w"].partition_broadcast(CH)).then_inc(loaded, 16)
            sp.dma_start(mask[:], io["mask"]).then_inc(loaded, 16)
            sp.dma_start(rank[:], io["rank"]).then_inc(loaded, 16)
            sp.wait_ge(made, MADE)
            sp.dma_start(table_dram.rearrange("(p n) o -> p (n o)", p=128), pad_ids[:]).then_inc(filled, 16)

            def load_patches(b, p2):
                sp.wait_ge(tok_done, b + 1)
                carry(sp, passed_sp)
                sp.dma_start(xk[:, p2, :, :].rearrange("p k t -> p (k t)"),
                             io["patches"][ds(b, 1), :, :].rearrange("b p n -> (b p) n")).then_inc(xk_in[p2], 16)

            def store_rows(b, q):
                sp.wait_ge(ob_ready, b + 1)
                carry(sp, passed_sp)
                for n in range(NC_):
                    rows = slice(0, C_LEN[n])
                    sp.dma_start(rows_v[ds(b, 1), C_OFF[n]:C_OFF[n] + C_LEN[n], :].rearrange("b t n -> (b t) n"),
                                 rt[rows, q, n, :]).then_inc(rows_out[q], 16)
                    sp.dma_start(out[ds(b, 1), C_OFF[n]:C_OFF[n] + C_LEN[n], :].rearrange("b t n -> (b t) n"),
                                 ob[rows, q, n, :]).then_inc(rows_out[q], 16)

            LAG = 5
            for b in range(LAG + 1):
                if b >= LAG:
                    store_rows(b - LAG, (b - LAG) % 2)
                load_patches(b, b % 2)
            with sp.Fori(0, (BATCH - LAG - 1) // 2) as j:
                for k in range(2):
                    store_rows(2 * j + 1 + k, (1 + k) % 2)
                    load_patches(2 * j + LAG + 1 + k, k)
            for b in range(BATCH - LAG, BATCH):
                store_rows(b, b % 2)
            for q in range(2):
                sp.wait_ge(rows_out[q], 16 * 6 * (BATCH // 2))

        @block.gpsimd
        def _(pool):
            pool.memset(pad_ids[:], NO_ROW).then_inc(made, 1)
            for t in (h, th, den):
                pool.memset(t[:], 1.0).then_inc(made, 1)
            for t in (xT, qk, oT, nT, rt):
                pool.memset(t[:], 0.0).then_inc(made, 1)
            pool.memset(va[:], 1.0).then_inc(made, 1)
            pool.memset(minus_half[:], -0.5).then_inc(made, 1)
            pool.memset(ones[:], 1.0).then_inc(made, 1)
            pool.iota(tid[:], [[CH, NC_]], base=0, channel_multiplier=1, allow_small_or_imprecise_dtypes=True).then_inc(made, 1)
            pool.wait_ge(made, MADE)
            pool.wait_ge(loaded, 16 * LOADS)
            pool.wait_ge(filled, 16)

            ch = Chain(pool, pool_chain)

            def turn(i, p4, a, b1, b2, c):
                p2 = p4 % 2
                if a:
                    if not isinstance(i, int) or i >= 4:
                        pool.wait_ge(l_ready, i - 3)
                    pool.tensor_copy(h[0:TXT, p4, 2, :], txt[:, ds(i, 1), :].rearrange("p b n -> p (b n)")).then_inc(text_ready, 1)
                if c:
                    pool.wait_ge(var2, i - 2)
                    pool.tensor_tensor(rs2[:], ve2[:], minus_half[:], ALU.pow).then_inc(rstd2, 1)
                    pool.wait_ge(rstd2, i - 2)
                    ch.step(pool.tensor_tensor(ms1[:], mv2[:, :, 1], rs2[:], ALU.mult))
                    ch.settle()
                    ch.step(pool.tensor_tensor(ms2[:], ms1[:], rs2[:], ALU.mult))
                    ch.settle()
                    carry(pool, passed_pool)
                    ch.step(pool.tensor_scalar(ms3[:], ms2[:], 1e-6, None, ALU.add))
                    ch.settle()
                    pool.tensor_tensor(rms[:], ms3[:], minus_half[:], ALU.pow).then_inc(rms_ready, 1)
                if a:
                    pool.wait_ge(var1, i + 1)
                    pool.tensor_tensor(rs1[:], ve1[:], minus_half[:], ALU.pow).then_inc(rstd1, 1)
                if c:
                    q = 1 - p2
                    pool.wait_ge(normed, i - 2)
                    pool.tensor_tensor(rt[:, q, :, D:2 * D], h[:, (p4 + 1) % 4, :, :], ln2[:], ALU.add).then_inc(base_ready, 1)
                    pool.wait_ge(rp_ready, i - 2)
                    carry(pool, passed_pool)
                    for n in range(NC_):
                        mm = pool.tensor_scalar(ob[:, q, n, :], rt[:, q, n, 0:D], rt[:, q, n, 2 * D:2 * D + 1], None, ALU.mult)
                    ch.step(mm)
                    ch.settle()
                    pool.tensor_tensor(ob[:, q, :, :], ob[:, q, :, :], rt[:, q, :, D:2 * D], ALU.add).then_inc(ob_ready, 1)
                    pool.wait_ge(slots_ready, i - 1)
                    carry(pool, passed_pool)
                    for n in range(NC_):
                        rows = slice(0, C_LEN[n])
                        pool.indirect_dma_start(
                            out=table_dram, out_offset=bass.IndirectOffsetOnAxis(ap=slot[rows, q, n:n + 1], axis=0),
                            in_=tid_i[rows, q, n:n + 1], in_offset=None,
                            bounds_check=EXP * REGION - 1, oob_is_err=False).then_inc(slots_out[q], 16)
            PER = 4
            for i in range(4):
                turn(i, i, i >= 0, i >= 1, i >= 2, i >= 3)
            done = ch.n
            with pool.Fori(0, BATCH // 4 - 1) as j:
                for k in range(4):
                    ch.base, ch.n = done + (4 * j + k) * PER, 0
                    turn(4 * j + 4 + k, k, True, True, True, True)
                    assert ch.n == PER, ch.n
            ch.base, ch.n = done + (BATCH - 4) * PER, 0
            for i in range(BATCH, BATCH + 3):
                turn(i, i % 4, False, i - 1 < BATCH, i - 2 < BATCH, True)
            for q in range(2):
                pool.wait_ge(slots_out[q], 16 * NC_ * (BATCH // 2))

        @block.scalar
        def _(act):
            act.wait_ge(made, MADE)

            def turn(i, p4, a, b1, b2, c):
                p2 = p4 % 2
                if b1:
                    q = 1 - p2
                    for n in range(4):
                        act.wait_ge(qk_done, 4 * (i - 1) + n + 1)
                        act.wait_ge(fm, 4 * (i - 1) + n + 1)
                        act.activation(e_sb[:, n, :], B[3 + n][:, 0:SEQ], ACT.Exp)
                        act.activation(r_sb[:, n, :], B[3 + n][:, 0:SEQ], ACT.Relu).then_inc(qk_read, 1)
                if c:
                    act.wait_ge(nT_turned, i - 2)
                    act.activation(nT[:, 0, 0:SEQ], B[1][0:96, 0:SEQ], ACT.Copy)
                    act.activation(nT[:, 1, 0:SEQ], B[2][0:96, 0:SEQ], ACT.Copy).then_inc(nT_ready, 1)
                if b1:
                    act.wait_ge(vg_done, 4 * (i - 1) + 1)
                    act.activation(va[:, q, 0:2, :, 0:AD], B[3][0:CH, :].rearrange("p (c h e) -> p c h e", c=2, h=AH), ACT.Copy)
                    act.wait_ge(vg_done, 4 * (i - 1) + 2)
                    act.activation(va[:, q, 2, :, 0:AD], B[4][0:CH, 0:DIM].rearrange("p (h e) -> p h e", h=AH), ACT.Copy)
                    act.wait_ge(vg_done, 4 * (i - 1) + 3)
                    act.activation(th[:, q, 0:2, :], B[5][0:CH, 0:2 * D].rearrange("p (c n) -> p c n", c=2), ACT.Tanh, scale=0.5)
                    act.wait_ge(vg_done, 4 * (i - 1) + 4)
                    act.activation(th[:, q, 2, :], B[6][0:CH, 0:D], ACT.Tanh, scale=0.5).then_inc(vg_ready, 1)
                if c:
                    act.wait_ge(ex_in, i - 2)
                    act.activation(ex[:], less[:], ACT.Exp).then_inc(ex_ready, 1)
                if a:
                    act.wait_ge(xT_turned, i + 1)
                    act.activation(xT[:, p2, 0, 0:SEQ], B[1][0:96, 0:SEQ], ACT.Copy).then_inc(xT_lo, 1)
                if b2:
                    act.wait_ge(oT_turned, i - 1)
                    act.activation(oT[:, 0, 0:SEQ], B[1][:, 0:SEQ], ACT.Copy).then_inc(oT_ready, 1)
            turns(act, turn)

        @block.tensor
        def _(pe):
            pe.wait_ge(loaded, 16 * LOADS)
            pe.wait_ge(made, MADE)
            pe.sem_inc(tok_done, 2)

            def tokens(i, p2):
                pe.wait_ge(h_ready, i + 1)
                pe.wait_ge(xk_in[p2], 16 * ((i - p2) // 2) + 16 if isinstance(i, int) else 8 * (i - p2) + 16)
                for n in range(2):
                    for k in range(KP):
                        mm = pe.matmul(B[0][0:CH, n * D:(n + 1) * D], xk[:, p2, k, n * CH:(n + 1) * CH], wt[:, k, :],
                                       start=(k == 0), stop=(k == KP - 1))
                mm.then_inc(tok_done, 1)

            def turned(source):
                for k in range(KD):
                    for n in range(NC_):
                        mm = pe.transpose(B[1 + k][0:96, C_OFF[n]:C_OFF[n] + C_LEN[n]],
                                          source[0:C_LEN[n], n, 96 * k:96 * k + 96], ident[0:C_LEN[n], 0:C_LEN[n]])
                return mm

            def attend(m, p2, projected):
                pe.wait_ge(fm, 4 * m + 8)
                for g in range(2):
                    for part in range(2):
                        for r in range(2):
                            n = 4 * g + 2 * part + r
                            bank = B[3 + n % 4]
                            if n >= 4:
                                pe.wait_ge(masked, 8 * m + n - 3)
                            elif projected:
                                pe.wait_ge(qk_read, 4 * (m + 1) + n + 1)
                            kh = qk[AD * r:AD * r + AD, p2, 2 + g, :]
                            qh = qk[AD * r:AD * r + AD, p2, g, :]
                            if part == 0:
                                mm = pe.matmul(bank[0:CH, 0:SEQ], kh[:, 0:CH], qh[:, 0:SEQ], start=True, stop=True)
                            else:
                                w1 = SEQ - C_OFF[1]
                                pe.matmul(bank[0:CH, 0:w1], kh[:, C_OFF[1]:C_OFF[1] + CH], qh[:, C_OFF[1]:SEQ], start=True, stop=True)
                                mm = pe.matmul(bank[0:CH, w1:w1 + C_LEN[2]], kh[:, C_OFF[2]:PADT], qh[:, C_OFF[2]:SEQ],
                                               start=True, stop=True)
                            mm.then_inc(at_done, 1)

            def queries_keys(m, p2, attended, finished):
                pe.wait_ge(xT_lo, m + 1)
                pe.wait_ge(xT_hi, m + 1)
                if finished:
                    pe.wait_ge(h2_ready, m - 1)
                elif attended:
                    pe.wait_ge(vg_ready, m)
                for n, (w, c) in enumerate(((wq, 0), (wq, 1), (wk, 0), (wk, 1))):
                    for k in range(KD):
                        mm = pe.matmul(B[3 + n][:, 0:SEQ], w[:, k, 128 * c:128 * c + 128], xT[:, p2, k, 0:SEQ],
                                       start=(k == 0), stop=(k == KD - 1))
                    mm.then_inc(qk_done, 1)

            def values_gate(m, p2, attended):
                for n, (w, width, chunks) in enumerate(((wv, DIM, (0, 1)), (wv, DIM, (2,)), (wg, D, (0, 1)), (wg, D, (2,)))):
                    if attended:
                        pe.wait_ge(masked, 8 * (m - 1) + n + 5)
                    else:
                        pe.wait_ge(qk_read, 4 * m + n + 1)
                    for c, cc in enumerate(chunks):
                        for k in range(KD):
                            mm = pe.matmul(B[3 + n][0:CH, c * width:(c + 1) * width], xT[:, p2, k, C_OFF[cc]:C_OFF[cc] + CH], w[:, k, :],
                                           start=(k == 0), stop=(k == KD - 1))
                    mm.then_inc(vg_done, 1)

            def numerators(m, p2, projected):
                pe.wait_ge(masked, 8 * m + 8)
                if projected:
                    pe.wait_ge(vg_ready, m + 2)
                for n in range(NC_):
                    for hh in range(AH):
                        for jj in range(n + 1):
                            at0 = (AT0, AT1, AT2)[jj] + C_OFF[n] - C_OFF[jj]
                            mm = pe.matmul(B[3 + n][0:C_LEN[n], hh * (AD + 1):(hh + 1) * (AD + 1)],
                                           at[0:C_LEN[jj], hh, at0:at0 + C_LEN[n]], va[0:C_LEN[jj], p2, jj, hh, :],
                                           start=(jj == 0), stop=(jj == n))
                    mm.then_inc(num_done, 1)

            def counts(m):
                pe.wait_ge(hot_ready, m + 1)
                for n in range(NC_):
                    for jj in range(n + 1):
                        w = tri if jj == n else ones
                        pe.matmul(B[7][0:CH, n * EXP:(n + 1) * EXP], w[0:C_LEN[jj], :], hot[0:C_LEN[jj], jj, :],
                                  start=(jj == 0), stop=(jj == n))
                for jj in range(NC_):
                    mm = pe.matmul(B[7][0:CH, NC_ * EXP:(NC_ + 1) * EXP], ones[0:C_LEN[jj], :], hot[0:C_LEN[jj], jj, :],
                                   start=(jj == 0), stop=(jj == NC_ - 1))
                mm.then_inc(cum_done, 1)

            def turn(i, p4, a, b1, b2, c):
                p2 = p4 % 2
                q2 = 1 - p2
                if a:
                    tokens(i, p2)
                if b1:
                    queries_keys(i - 1, q2, attended=b2, finished=c)
                if c:
                    pe.wait_ge(normed, i - 2)
                    turned(rt[:, q2, :, :]).then_inc(nT_turned, 1)
                if b2:
                    attend(i - 2, p2, projected=b1)
                if b1:
                    values_gate(i - 1, q2, attended=b2)
                if c:
                    pe.wait_ge(nT_ready, i - 2)
                    pe.wait_ge(slots_ready, i - 2)
                    for n in range(NC_):
                        for k in range(KD):
                            mm = pe.matmul(B[7][0:CH, n * EXP:(n + 1) * EXP], nT[:, k, C_OFF[n]:C_OFF[n] + CH], wr[:, k, :],
                                           start=(k == 0), stop=(k == KD - 1))
                    mm.then_inc(lg_done, 1)
                if b2:
                    numerators(i - 2, p2, projected=b1)
                if a:
                    pe.wait_ge(ln1, i + 1)
                    turned(ln).then_inc(xT_turned, 1)
                if b2:
                    pe.wait_ge(o_ready, i - 1)
                    if a:
                        pe.wait_ge(xT_lo, i + 1)
                        pe.wait_ge(xT_hi, i + 1)
                    for k in range(2):
                        for n in range(NC_):
                            mm = pe.transpose(B[1 + k][:, C_OFF[n]:C_OFF[n] + C_LEN[n]],
                                              o[0:C_LEN[n], n, 2 * k:2 * k + 2, :].rearrange("p h e -> p (h e)"),
                                              ident[0:C_LEN[n], 0:C_LEN[n]])
                    mm.then_inc(oT_turned, 1)
                if c:
                    counts(i - 3)
                if b2:
                    pe.wait_ge(oT_ready, i - 1)
                    pe.wait_ge(oT_high, i - 1)
                    for n in range(NC_):
                        bank, col = (B[6], n * D) if n < 2 else (B[3], 0)
                        for k in range(2):
                            mm = pe.matmul(bank[0:CH, col:col + D], oT[:, k, C_OFF[n]:C_OFF[n] + CH], wo[:, k, :],
                                           start=(k == 0), stop=(k == 1))
                    mm.then_inc(y_done, 1)
            turns(pe, turn)

        @block.vector
        def _(dve):
            ch = Chain(dve, chain)
            dve.sem_inc(h_ready, 1)
            dve.sem_inc(fm, 4)
            dve.sem_inc(slots_ready, 1)
            dve.wait_ge(loaded, 16 * LOADS)
            dve.wait_ge(made, MADE)
            ch.step(dve.tensor_tensor(posb[:], posb[:], bias[:], ALU.add))
            ch.step(dve.tensor_copy(tri[:], mask[:, 0:CH]))
            ch.step(dve.tensor_scalar(run[:], rank[:, 0, :], -float(REGION), float(REGION * EXP - 1), ALU.mult, ALU.add))
            ch.settle()
            ch.step(dve.tensor_scalar(tid[:, 2:3], tid[:, 2:3], float(C_OFF[2] - 2 * CH - 0), None, ALU.add))
            ch.settle()
            ch.step(dve.tensor_scalar(tid[:], tid[:], -float(SEQ), None, ALU.add))
            ch.settle()

            def turn(i, p4, a, b1, b2, c):
                p2 = p4 % 2
                q2 = 1 - p2
                hc = (p4 + 1) % 4
                if c:
                    dve.wait_ge(h2_ready, i - 2)
                    for n in range(NC_):
                        mm = dve.bn_stats(out=st2[:, n, :], in_=h[:, hc, n, :])
                    ch.step(mm)
                    ch.settle()
                    carry(dve, passed_dve)
                    for n in range(NC_):
                        mm = dve.bn_aggr(out=mv2[:, n, :], in_=st2[:, n, :])
                    ch.step(mm)
                    ch.settle()
                    dve.tensor_scalar(ve2[:], mv2[:, :, 1], LN_EPS, None, ALU.add).then_inc(var2, 1)
                if c:
                    dve.wait_ge(rstd2, i - 2)
                    if not isinstance(i, int) or i > 3:
                        dve.wait_ge(base_ready, i - 3)
                    for n in range(NC_):
                        mm = dve.tensor_scalar(ln2[:, n, :], h[:, hc, n, :], mv2[:, n, 0:1], rs2[:, n:n + 1], ALU.subtract, ALU.mult)
                    mm.then_inc(l_ready, 1)
                    dve.wait_ge(l_ready, i - 2)
                    dve.wait_ge(rms_ready, i - 2)
                    if not isinstance(i, int) or i >= 5:
                        dve.wait_ge(rows_out[q2], 48 * (i - 3 - (1 - p2)) if not isinstance(i, int) else 96 * ((i - 3) // 2))
                    for n in range(NC_):
                        mm = dve.scalar_tensor_tensor(out=rt[:, q2, n, 0:D], in0=ln2[:, n, :], scalar=rms[:, n:n + 1],
                                                      in1=lnw[:], op0=ALU.mult, op1=ALU.mult)
                    mm.then_inc(normed, 1)
                if a:
                    dve.wait_ge(tok_done, i + 3)
                    dve.tensor_tensor(h[:, p4, 0:2, :], B[0][0:CH, 0:2 * D].rearrange("p (c n) -> p c n", c=2), posb[:],
                                      ALU.add).then_inc(h_ready, 1)
                    dve.wait_ge(h_ready, i + 2)
                    dve.wait_ge(text_ready, i + 1)
                    for n in range(NC_):
                        mm = dve.bn_stats(out=st1[:, n, :], in_=h[:, p4, n, :])
                    ch.step(mm)
                    ch.settle()
                    carry(dve, passed_dve)
                    for n in range(NC_):
                        mm = dve.bn_aggr(out=mv1[:, n, :], in_=st1[:, n, :])
                    ch.step(mm)
                    ch.settle()
                    dve.tensor_scalar(ve1[:], mv1[:, :, 1], LN_EPS, None, ALU.add).then_inc(var1, 1)
                if b1:
                    for n in range(4):
                        dve.wait_ge(qk_read, 4 * (i - 1) + n + 1)
                        dve.scalar_tensor_tensor(out=qk[:, q2, n, 0:SEQ], in0=e_sb[:, n, :], scalar=1.0, in1=r_sb[:, n, :],
                                                 op0=ALU.min, op1=ALU.add).then_inc(fm, 1)
                if b2:
                    for n in range(8):
                        hh, part = 2 * (n // 4) + n % 2, (n % 4) // 2
                        dve.wait_ge(at_done, 8 * (i - 2) + n + 1)
                        lo, hi = (AT0, AT1) if part == 0 else (AT1, ATW)
                        dve.tensor_tensor(at[:, hh, lo:hi], B[3 + n % 4][0:CH, 0:hi - lo], mask[:, lo:hi], ALU.mult).then_inc(masked, 1)
                if a:
                    dve.wait_ge(rstd1, i + 1)
                    if not isinstance(i, int) or i >= 1:
                        dve.wait_ge(xT_turned, i)
                    for n in range(NC_):
                        mm = dve.tensor_scalar(ln[:, n, :], h[:, p4, n, :], mv1[:, n, 0:1], rs1[:, n:n + 1], ALU.subtract, ALU.mult)
                    mm.then_inc(ln1, 1)
                if c:
                    lg = B[7][0:CH, 0:NC_ * EXP].rearrange("p (c e) -> p c e", c=NC_)
                    wide = [CH, NC_, EXP]
                    dve.wait_ge(lg_done, i - 2)
                    ch.step(dve.tensor_reduce(out=best[:], in_=lg, axis=AX.X, op=ALU.max))
                    ch.settle()
                    dve.tensor_tensor(less[:], lg, best[:].unsqueeze(2).to_broadcast(wide), ALU.subtract).then_inc(ex_in, 1)
                    ch.step(dve.tensor_tensor(eq[:], lg, best[:].unsqueeze(2).to_broadcast(wide), ALU.is_equal))
                    ch.settle()
                    ch.step(dve.tensor_tensor(ranked[:], eq[:], rank[:], ALU.mult))
                    ch.settle()
                    ch.step(dve.tensor_reduce(out=first[:], in_=ranked[:], axis=AX.X, op=ALU.max))
                    ch.settle()
                    dve.tensor_tensor(hot[:], rank[:], first[:].unsqueeze(2).to_broadcast(wide), ALU.is_equal).then_inc(hot_ready, 1)
                    dve.wait_ge(ex_ready, i - 2)
                    ch.step(dve.tensor_reduce(out=esum[:], in_=ex[:], axis=AX.X, op=ALU.add))
                    ch.settle()
                    dve.reciprocal(rt[:, q2, :, 2 * D:2 * D + 1].rearrange("p c o -> p (c o)"), esum[:]).then_inc(rp_ready, 1)
                if b2:
                    for n in range(NC_):
                        dve.wait_ge(num_done, 3 * (i - 2) + n + 1)
                        num = B[3 + n][0:C_LEN[n], 0:AH * (AD + 1)].rearrange("p (h e) -> p h e", h=AH)
                        ch.step(dve.tensor_scalar(den[0:C_LEN[n], n, :], num[:, :, AD], 1e-6, None, ALU.max))
                        ch.settle()
                        ch.step(dve.reciprocal(rden[0:C_LEN[n], n, :], den[0:C_LEN[n], n, :]))
                        ch.settle()
                        mm = dve.tensor_tensor(o[0:C_LEN[n], n, :, :], num[:, :, 0:AD],
                                               rden[0:C_LEN[n], n, :].unsqueeze(2).to_broadcast([C_LEN[n], AH, AD]), ALU.mult)
                    mm.then_inc(o_ready, 1)
                if a:
                    dve.wait_ge(xT_turned, i + 1)
                    dve.tensor_copy(xT[:, p2, 1, 0:SEQ], B[2][0:96, 0:SEQ]).then_inc(xT_hi, 1)
                if b2:
                    dve.wait_ge(oT_turned, i - 1)
                    dve.tensor_copy(oT[:, 1, 0:SEQ], B[2][:, 0:SEQ]).then_inc(oT_high, 1)
                if c:
                    cum = B[7][0:CH, 0:NC_ * EXP].rearrange("p (c e) -> p c e", c=NC_)
                    dve.wait_ge(cum_done, i - 2)
                    dve.tensor_tensor(at_cum[:], cum, hot[:], ALU.mult)
                    ch.step(dve.tensor_tensor(at_run[:], hot[:], run[:].unsqueeze(1).to_broadcast(wide), ALU.mult))
                    ch.settle()
                    dve.tensor_reduce(out=prio[:], in_=at_cum[:], axis=AX.X, op=ALU.add)
                    ch.step(dve.tensor_reduce(out=place[:], in_=at_run[:], axis=AX.X, op=ALU.add))
                    ch.step(dve.scalar_tensor_tensor(out=run[:], in0=B[7][0:CH, NC_ * EXP:(NC_ + 1) * EXP], scalar=float(CAP),
                                                     in1=run[:], op0=ALU.min, op1=ALU.add))
                    ch.step(dve.tensor_scalar(tid[:], tid[:], float(SEQ), None, ALU.add))
                    ch.settle()
                    dve.tensor_scalar(over[:], prio[:], CAP + 0.5, float(NO_ROW), ALU.is_gt, ALU.mult)
                    ch.step(dve.tensor_tensor(slot0[:], prio[:], place[:], ALU.add))
                    ch.settle()
                    if not isinstance(i, int) or i >= 5:
                        dve.wait_ge(slots_out[q2], 24 * (i - 3 - (1 - p2)) if not isinstance(i, int) else 48 * ((i - 3) // 2))
                    dve.tensor_copy(tid_i[:, q2, :], tid[:])
                    dve.tensor_tensor(slot[:, q2, :], slot0[:], over[:], ALU.add).then_inc(slots_ready, 1)
                if b2:
                    dve.wait_ge(y_done, i - 1)
                    dve.scalar_tensor_tensor(out=gated[:, 0:2, :], in0=th[:, p2, 0:2, :], scalar=1.0,
                                             in1=B[6][0:CH, 0:2 * D].rearrange("p (c n) -> p c n", c=2), op0=ALU.add, op1=ALU.mult)
                    ch.step(dve.scalar_tensor_tensor(out=gated[:, 2, :], in0=th[:, p2, 2, :], scalar=1.0, in1=B[3][0:CH, 0:D],
                                                     op0=ALU.add, op1=ALU.mult))
                    ch.settle()
                    dve.scalar_tensor_tensor(out=h[:, (p4 + 2) % 4, :, :], in0=gated[:], scalar=0.5, in1=h[:, (p4 + 2) % 4, :, :],
                                             op0=ALU.mult, op1=ALU.add).then_inc(h2_ready, 1)

            PER = 21
            for i in range(4):
                turn(i, i, i >= 0, i >= 1, i >= 2, i >= 3)
            done = ch.n
            with dve.Fori(0, BATCH // 4 - 1) as j:
                for k in range(4):
                    ch.base, ch.n = done + (4 * j + k) * PER, 0
                    turn(4 * j + 4 + k, k, True, True, True, True)
                    assert ch.n == PER, ch.n
            ch.base, ch.n = done + (BATCH - 4) * PER, 0
            for i in range(BATCH, BATCH + 3):
                turn(i, i % 4, False, i - 1 < BATCH, i - 2 < BATCH, True)
            ch.settle()


def moe_phase(nc, io, out, ident, rows_dram, table_dram, run, sems):
    with ExitStack() as ctx:
        S = Scope(nc, ctx, "m")
        S.sem = lambda name: sems.sem(f"m_{name}")
        wi0 = S.sb("wi0", [128, EXP, F])
        wir = S.sb("wir", [128, EXP, F // 2])
        wo = S.sb("wo", [128, EXP, FC, D])
        cnt = S.sb("cnt", [1, EXP])
        cnt_i, nt_i = S.sb("cnt_i", [1, EXP], I32), S.sb("nt_i", [1, EXP], I32)
        nt = S.sb("nt", [1, EXP])
        below = S.sb("below", [1, EXP, EXP])
        upto = S.sb("upto", [1, EXP, EXP])
        ends = S.sb("ends", [1, EXP])
        rank = S.sb("rank", [1, EXP])
        tnum = S.sb("tnum", [1, TILES])
        past = S.sb("past", [1, TILES, EXP])
        start = S.sb("start", [1, TILES])
        expert = S.sb("expert", [1, TILES])
        expert_i, offs_i = S.sb("expert_i", [1, TILES], I32), S.sb("offs_i", [1, TILES], I32)
        offs = S.sb("offs", [1, TILES])
        N3 = 3
        idt = S.sb("ids", [TILE, N3], I32)
        ids_g, ids_s = S.sb("ids_g", [TILE, N3], I32), S.sb("ids_s", [TILE, N3], I32)
        g = S.sb("rows", [TILE, N3, ROW])
        xa = S.sb("xa", [128, TILE])
        xr = S.sb("xr", [128, 2, TILE])
        hid = S.sb("hid", [TILE, F])
        hidT = S.sb("hidT", [128, FC, TILE])
        ob = S.sb("ob", [TILE, N3, D])
        ps_x, ps_y = S.ps("x", [128, 512]), S.ps("y", [128, 512])
        ps_u = [S.ps("u0", [128, 512]), S.ps("u1", [128, 512])]
        ps_t = [S.ps("t0", [128, 512]), S.ps("t1", [128, 512])]
        FH = F // 2
        loaded, small, made, tiles_ready = S.sem("loaded"), S.sem("small"), S.sem("made"), S.sem("tiles_ready")
        ids_in = [S.sem(f"ids_in{n}") for n in range(N3)]
        rows_in = [S.sem(f"rows_in{n}") for n in range(N3)]
        rows_out = [S.sem(f"rows_out{n}") for n in range(N3)]
        (x_turned, x_ready, up_done, relu_lo, relu_hi, h_turned, hT_lo, hT_hi, y_done, y_ready, chain, passed) = (S.sem(n) for n in (
            "x_turned", "x_ready", "up_done", "relu_lo", "relu_hi", "h_turned", "hT_lo", "hT_hi", "y_done", "y_ready", "chain", "passed"))
        passed_sp, ids_taken, ids_kept = S.sem("passed_sp"), S.sem("ids_taken"), S.sem("ids_kept")
        block = ctx.enter_context(nc.Block())
        GRP = TILES // N3
        assert GRP * N3 == TILES

        @block.sync
        def _(sp):
            sp.dma_start(below[:], io["below"]).then_inc(small, 16)
            sp.dma_start(tnum[:], io["tnum"]).then_inc(small, 16)
            sp.dma_start(rank[:], io["rank"][0:1, 0, :]).then_inc(small, 16)
            sp.dma_start(wi0[:], io["wi0"]).then_inc(loaded, 16)
            sp.dma_start(wir[:], io["wir"]).then_inc(loaded, 16)
            sp.dma_start(wo[:], io["wo"]).then_inc(loaded, 16)
            sp.wait_ge(tiles_ready, 1)

            def load_ids(j, p):
                off = sp.value_load(offs_i[0:1, ds(N3 * j + p, 1)], min_val=0, max_val=EXP * REGION)
                if not isinstance(j, int):
                    sp.wait_ge(ids_taken, N3 * j + p - N3 + 1)
                    carry(sp, passed_sp)
                sp.dma_start(idt[:, p:p + 1], table_dram[ds(off, TILE), :]).then_inc(ids_in[p], 16)

            for p in range(N3):
                load_ids(0, p)
            with sp.Fori(1, GRP) as j:
                for p in range(N3):
                    load_ids(j, p)

        @block.gpsimd
        def _(pool):
            pool.memset(g[:], 0.0).then_inc(made, 1)
            pool.memset(xr[:], 0.0).then_inc(made, 1)
            pool.wait_ge(made, 2)

            def gather(t, j, p):
                pool.wait_ge(ids_in[p], 16 * j + 16)
                carry(pool, passed)
                pool.tensor_copy(ids_g[:, p:p + 1], idt[:, p:p + 1]).then_inc(ids_taken, 1)
                pool.wait_ge(ids_taken, t + 1)
                pool.wait_ge(y_ready, t + 1)
                carry(pool, passed)
                pool.indirect_dma_start(
                    out=g[:, p, :], out_offset=None, in_=rows_dram,
                    in_offset=bass.IndirectOffsetOnAxis(ap=ids_g[:, p:p + 1], axis=0),
                    bounds_check=BATCH * SEQ - 1, oob_is_err=False).then_inc(rows_in[p], 16)

            def scatter(t, j, p):
                if not isinstance(j, int) or j > 0:
                    pool.wait_ge(rows_out[p], 16 * j)
                carry(pool, passed)
                pool.tensor_copy(ids_s[:, p:p + 1], ids_g[:, p:p + 1]).then_inc(ids_kept, 1)
                pool.wait_ge(ids_kept, t + 1)
                pool.wait_ge(y_ready, t + 4)
                carry(pool, passed)
                pool.indirect_dma_start(
                    out=out.rearrange("b t n -> (b t) n"), out_offset=bass.IndirectOffsetOnAxis(ap=ids_s[:, p:p + 1], axis=0),
                    in_=ob[:, p, :], in_offset=None,
                    bounds_check=BATCH * SEQ - 1, oob_is_err=False).then_inc(rows_out[p], 16)

            gather(0, 0, 0)
            gather(1, 0, 1)

            def three(j):
                for p in range(N3):
                    gather(N3 * j + p + 2, j + (p + 2) // N3, (p + 2) % N3)
                    scatter(N3 * j + p, j, p)

            three(0)
            with pool.Fori(1, GRP - 1) as j:
                three(j)
            gather(TILES - 1, GRP - 1, 2)
            for p in range(N3):
                scatter(TILES - N3 + p, GRP - 1, p)
            for p in range(N3):
                pool.wait_ge(rows_out[p], 16 * GRP)

        @block.scalar
        def _(act):
            act.wait_ge(made, 2)

            def relu(t):
                act.wait_ge(up_done, t + 1)
                act.activation(hid[:, 0:FH], ps_u[0][:, 0:FH], ACT.Relu).then_inc(relu_lo, 1)

            def hT(t):
                act.wait_ge(h_turned, t + 1)
                act.activation(hidT[:, 0:3, :], ps_t[0][:, 0:FH].rearrange("p (f t) -> p f t", f=3), ACT.Copy).then_inc(hT_lo, 1)

            def x_copy(t):
                act.wait_ge(x_turned, t + 1)
                act.activation(xa[:], ps_x[:, 0:TILE], ACT.Copy)
                act.activation(xr[0:D1, 0, :], ps_x[0:D1, TILE:2 * TILE], ACT.Copy)
                act.activation(xr[D1:128, 1, :], ps_x[0:D1, TILE:2 * TILE], ACT.Copy).then_inc(x_ready, 1)

            act.sem_inc(x_ready, 1)
            x_copy(0)
            relu(0)
            x_copy(1)
            with act.Fori(0, TILES - 2) as t:
                hT(t)
                relu(t + 1)
                x_copy(t + 2)
            hT(TILES - 2)
            relu(TILES - 1)
            hT(TILES - 1)

        @block.tensor
        def _(pe):
            pe.wait_ge(loaded, 48)
            pe.wait_ge(tiles_ready, 1)

            def turn_x(t, j, p):
                pe.wait_ge(rows_in[p], 16 * j + 16)
                pe.wait_ge(x_ready, t + 1)
                pe.transpose(ps_x[:, 0:TILE], g[:, p, 0:D0], ident[:])
                pe.transpose(ps_x[0:D1, TILE:2 * TILE], g[:, p, D0:D], ident[:]).then_inc(x_turned, 1)

            def up(t):
                e = pe.value_load(expert_i[0:1, ds(t, 1)], min_val=0, max_val=EXP - 1)
                pe.wait_ge(x_ready, t + 2)
                for half in range(2):
                    pe.matmul(ps_u[half][:, 0:FH], xa[:], wi0[:, ds(e, 1), half * FH:(half + 1) * FH].rearrange("p e f -> p (e f)"),
                              start=True, stop=False)
                    mm = pe.matmul(ps_u[half][:, 0:FH], xr[:, half, :], wir[:, ds(e, 1), :].rearrange("p e f -> p (e f)"),
                                   start=False, stop=True)
                mm.then_inc(up_done, 1)

            def turn_h(t):
                pe.wait_ge(relu_lo, t + 1)
                pe.wait_ge(relu_hi, t + 1)
                for f in range(FC):
                    mm = pe.transpose(ps_t[f // 3][:, (f % 3) * TILE:(f % 3 + 1) * TILE], hid[:, f * 128:(f + 1) * 128], ident[:])
                mm.then_inc(h_turned, 1)

            def down(t):
                e = pe.value_load(expert_i[0:1, ds(t, 1)], min_val=0, max_val=EXP - 1)
                pe.wait_ge(hT_lo, t + 1)
                pe.wait_ge(hT_hi, t + 1)
                pe.wait_ge(y_ready, t + 3)
                for f in range(FC):
                    mm = pe.matmul(ps_y[:, 0:D], hidT[:, f, :], wo[:, ds(e, 1), f, :].rearrange("p e n -> p (e n)"),
                                   start=(f == 0), stop=(f == FC - 1))
                mm.then_inc(y_done, 1)

            turn_x(0, 0, 0)
            up(0)
            turn_x(1, 0, 1)
            with pe.Fori(0, GRP - 1) as j:
                for p in range(N3):
                    t = N3 * j + p
                    turn_h(t)
                    up(t + 1)
                    down(t)
                    turn_x(t + 2, j + (p + 2) // N3, (p + 2) % N3)
            t = TILES - 3
            turn_h(t)
            up(t + 1)
            down(t)
            turn_x(t + 2, GRP - 1, 2)
            turn_h(t + 1)
            up(t + 2)
            down(t + 1)
            turn_h(t + 2)
            down(t + 2)

        @block.vector
        def _(dve):
            ch = Chain(dve, chain)
            dve.sem_inc(y_ready, 3)
            dve.wait_ge(small, 48)
            dve.wait_ge(made, 2)
            ch.step(dve.scalar_tensor_tensor(out=cnt[:], in0=rank[:], scalar=float(REGION), in1=run[0:1, :], op0=ALU.mult, op1=ALU.add))
            ch.settle()
            ch.step(dve.tensor_scalar(cnt_i[:], cnt[:], float(1 - REGION * EXP + TILE - 1), None, ALU.add))
            ch.settle()
            ch.step(dve.tensor_scalar(nt_i[:], cnt_i[:], TILE.bit_length() - 1, None, ALU.arith_shift_right))
            ch.settle()
            ch.step(dve.tensor_copy(nt[:], nt_i[:]))
            ch.settle()
            ch.step(dve.tensor_tensor(upto[:], below[:], nt[:].unsqueeze(1).to_broadcast([1, EXP, EXP]), ALU.mult))
            ch.settle()
            ch.step(dve.tensor_reduce(out=ends[:], in_=upto[:], axis=AX.X, op=ALU.add))
            ch.settle()
            w = [1, TILES, EXP]
            ch.step(dve.tensor_tensor(past[:], tnum[:].unsqueeze(2).to_broadcast(w), ends[:].unsqueeze(1).to_broadcast(w), ALU.is_ge))
            ch.settle()
            ch.step(dve.tensor_reduce(out=expert[:], in_=past[:], axis=AX.X, op=ALU.add))
            ch.settle()
            ch.step(dve.tensor_tensor(past[:], past[:], nt[:].unsqueeze(1).to_broadcast(w), ALU.mult))
            ch.settle()
            ch.step(dve.tensor_reduce(out=start[:], in_=past[:], axis=AX.X, op=ALU.add))
            ch.settle()
            ch.step(dve.tensor_tensor(start[:], tnum[:], start[:], ALU.subtract))
            ch.settle()
            ch.step(dve.tensor_scalar(start[:], start[:], float(TILE), None, ALU.mult))
            ch.settle()
            ch.step(dve.scalar_tensor_tensor(out=offs[:], in0=expert[:], scalar=float(REGION), in1=start[:], op0=ALU.mult, op1=ALU.add))
            ch.settle()
            dve.tensor_scalar(offs_i[:], offs[:], float(EXP * REGION), None, ALU.min)
            ch.step(dve.tensor_scalar(expert_i[:], expert[:], float(EXP - 1), None, ALU.min))
            ch.settle()
            dve.sem_inc(tiles_ready, 1)

            def relu(t):
                dve.wait_ge(up_done, t + 1)
                dve.tensor_scalar(hid[:, FH:F], ps_u[1][:, 0:FH], 0.0, None, ALU.max).then_inc(relu_hi, 1)

            def hT(t):
                dve.wait_ge(h_turned, t + 1)
                dve.tensor_copy(hidT[:, 3:6, :], ps_t[1][:, 0:FH].rearrange("p (f t) -> p f t", f=3)).then_inc(hT_hi, 1)

            def finish(t, j, p):
                dve.wait_ge(y_done, t + 1)
                if not isinstance(j, int) or j > 0:
                    dve.wait_ge(rows_out[p], 16 * j)
                dve.scalar_tensor_tensor(out=ob[:, p, :], in0=ps_y[:, 0:D], scalar=g[:, p, 2 * D:2 * D + 1], in1=g[:, p, D:2 * D],
                                         op0=ALU.mult, op1=ALU.add).then_inc(y_ready, 1)

            relu(0)

            def three(j):
                for p in range(N3):
                    t = N3 * j + p
                    hT(t)
                    relu(t + 1)
                    finish(t, j, p)

            three(0)
            with dve.Fori(1, GRP - 1) as j:
                three(j)
            t = TILES - 3
            hT(t)
            relu(t + 1)
            finish(t, GRP - 1, 0)
            hT(t + 1)
            relu(t + 2)
            finish(t + 1, GRP - 1, 1)
            hT(t + 2)
            finish(t + 2, GRP - 1, 2)


def build(nc, io, out):
    with ExitStack() as ctx:
        S = Scope(nc, ctx, "g")
        rows_dram = nc.dram_tensor("token_rows", [BATCH * SEQ, ROW], F32, kind="Internal").ap()
        table_dram = nc.dram_tensor("expert_table", [TABLE, 1], I32, kind="Internal").ap()
        ident = S.sb("ident", [128, 128])
        run = S.sb("run", [CH, EXP])
        made = S.sem("made")
        with nc.Block() as block:
            @block.gpsimd
            def _(pool):
                pool.memset(ident[:], 0.0).then_inc(made, 1)
                pool.wait_ge(made, 1)
                pool.affine_select(out=ident[:], in_=ident[:], compare_op=ALU.not_equal, fill=1.0, base=0,
                                   pattern=[[-1, 128]], channel_multiplier=1).then_inc(made, 1)
                pool.wait_ge(made, 2)
        with ExitStack() as texts:
            txt = Scope(nc, texts, "g").sb("txt", [TXT, BATCH, D])
            text_phase(nc, io, txt, ident, S)
            fusion_phase(nc, io, out, txt, ident, rows_dram, table_dram, run, S)
        moe_phase(nc, io, out, ident, rows_dram, table_dram, run, S)


def layout(inputs):
    a = {k: np.asarray(v) for k, v in inputs.items()}
    f = np.float32
    r = {}
    r["ids"] = np.ascontiguousarray(a["x_txt"].T)
    r["emb"] = a["L0_txt_emb"]
    p, i = np.meshgrid(np.arange(TXT), np.arange(D // 2))
    pe = np.zeros((TXT, D), f)
    pe[:, ::2] = np.sin(p / 2500 ** (2 * i / D)).T
    pe[:, 1::2] = np.cos(p / 2500 ** (2 * i / D)).T
    pos = np.zeros((128, 2, TXT), f)
    pos[:, 0] = pe.T[0:D0]
    pos[0:D1, 1] = pe.T[D0:D]
    r["pos"] = pos
    wqk = np.zeros((SLICE + 1, 2, 3, 4, 32), f)
    for s, n in enumerate("qk"):
        wqk[0:SLICE, s, :, :, 0:HD] = a[f"L0_txt_W{n}"].reshape(SLICE, 3, 4, HD)
        wqk[SLICE, s, :, :, 0:HD] = a[f"L0_txt_b{n}"].reshape(3, 4, HD)
    r["wqk"] = wqk.reshape(SLICE + 1, 2, 3, 128)
    r["wv"] = np.concatenate([a["L0_txt_Wv"], a["L0_txt_bv"][None]], axis=0)
    r["Wf"] = a["L0_txt_Wf"]
    vecs = np.zeros((128, 5, 2), f)
    for n, name in enumerate(("bf", "g1", "b1", "g2", "b2")):
        vecs[:, n, 0] = a[f"L0_txt_{name}"][0:D0]
        vecs[0:D1, n, 1] = a[f"L0_txt_{name}"][D0:D]
    r["vecs"] = vecs
    r["ones"] = np.ones((1, 3, 2 * TXT), f)
    G, P = 14, 16
    x = a["x"].reshape(BATCH, 3, G, P, G, P).transpose(0, 1, 3, 5, 2, 4).reshape(BATCH, KP, 128, IMG)
    patches = np.zeros((BATCH, 128, KP, 2 * CH), f)
    patches[:, :, :, 1:1 + IMG] = x.transpose(0, 2, 1, 3)
    r["patches"] = patches.reshape(BATCH, 128, KP * 2 * CH)
    r["w_tok"] = a["L0_tok_W"].T.reshape(KP, 128, D).transpose(1, 0, 2)
    pe = np.zeros((2 * CH, D), f)
    pe[0:1 + IMG] = a["L0_tok_pos_emb"]
    r["pos_emb"] = pe.reshape(2, CH, D).transpose(1, 0, 2)
    tb = np.zeros((2 * CH, D), f)
    tb[0] = a["L0_tok_class_token"]
    tb[1:1 + IMG] = a["L0_tok_b"]
    r["tok_bias"] = tb.reshape(2, CH, D).transpose(1, 0, 2)
    for n in ("Wq", "Wk", "Wv", "Wo", "Wg"):
        r["a_" + n.lower()] = a["L0_attn_" + n]
    r["w_router"] = a["L0_ffn_w_router"]
    r["ln_w"] = a["L0_ffn_ln_w"]
    s, t = np.arange(CH)[:, None], np.arange(SEQ)[None, :]
    r["mask"] = np.concatenate([(t[:, o:] >= s + o) for o in C_OFF], axis=1).astype(f)
    r["rank"] = np.broadcast_to(np.arange(EXP, 0, -1, dtype=f), (CH, NC_, EXP))
    r["below"] = np.tril(np.ones((EXP, EXP), f))[None]
    r["tnum"] = np.arange(TILES, dtype=f)[None]
    wi, wo = a["L0_ffn_wi"], a["L0_ffn_wo"]
    r["wi0"] = wi[:, 0:D0].transpose(1, 0, 2)
    r["wir"] = wi[:, D0:D].reshape(EXP, D1, 2, F // 2).transpose(2, 1, 0, 3).reshape(128, EXP, F // 2)
    r["wo"] = wo.reshape(EXP, FC, 128, D).transpose(2, 0, 1, 3)
    return {k: np.ascontiguousarray(v) for k, v in r.items()}


def kernel(**inputs):
    from concourse import bacc
    from concourse.bass_utils import run_bass_kernel_spmd as run

    nc = bacc.Bacc("TRN2", target_bir_lowering=False, num_devices=1)
    arrays = layout(inputs)
    io = {k: nc.dram_tensor(f"in_{k}", v.shape, mybir.dt.from_np(v.dtype), kind="ExternalInput").ap()
          for k, v in arrays.items()}
    out = nc.dram_tensor("out", [BATCH, SEQ, D], F32, kind="ExternalOutput").ap()
    build(nc, io, out)
    r = run(nc, [{f"in_{k}": v for k, v in arrays.items()}], core_ids=[0])
    return r.results[0]["out"]
```

```python
from contextlib import ExitStack

import numpy as np

import concourse.bass as bass
from concourse import mybir

F32 = mybir.dt.float32
I32 = mybir.dt.int32
BF16 = mybir.dt.bfloat16
ALU = mybir.AluOpType
ACT = mybir.ActivationFunctionType
AX = mybir.AxisListType
ds = bass.ds

BATCH = 64
TXT = 77
IMG = 196
SEQ = 1 + IMG + TXT
D = 192
D0, D1 = 128, 64
VOCAB = 8000
PATCH = 768
KP = PATCH // 128
TH = 12
HD = D // TH
SLICE = D // 3
LAYERS = 2
HHALF = TH * TXT // 2
GATHERS = 4
FCOL = 4 * TXT
FSTEPS = BATCH // 4
BN_EPS = 1e-5
LN_EPS = 1e-5

C_OFF = (0, 99, 197)
C_LEN = (99, 98, 77)
CH = 99
NC_ = 3
PADT = C_OFF[2] + CH
KD = D // 96
AH, AD = 4, 64
DIM = AH * AD
AT0, AT1, AT2 = 0, SEQ, SEQ + (SEQ - C_OFF[1])
ATW = AT2 + C_LEN[2]
EXP = 16
CAP = 64
REGION = BATCH * CAP
TILE = 128
TILES = -(-BATCH * SEQ // TILE) + EXP
TABLE = EXP * REGION + TILE
NO_ROW = 1 << 20
ROW = 2 * D + 4
F = 768
FC = F // 128


class Chain:

    def __init__(self, engine, sem):
        self.engine, self.sem, self.base, self.n = engine, sem, 0, 0

    def step(self, instruction):
        instruction.then_inc(self.sem, 1)
        self.n += 1

    def settle(self):
        self.engine.wait_ge(self.sem, self.base + self.n)

    def enter(self, offset):
        self.outer, self.base, self.n = (self.base + self.n, self.base + self.n + offset, 0)
        self.start = self.outer

    def leave(self, per_turn, turns):
        assert self.n == per_turn, self.n
        self.base, self.n = self.start + per_turn * turns, 0


class Scope:

    def __init__(self, nc, ctx, prefix):
        self.nc, self.ctx, self.prefix = nc, ctx, prefix

    def sb(self, name, shape, dt=F32):
        return self.ctx.enter_context(self.nc.sbuf_tensor(f"{self.prefix}_{name}", shape, dt))

    def ps(self, name, shape, dt=F32):
        return self.ctx.enter_context(self.nc.psum_tensor(f"{self.prefix}_{name}", shape, dt))

    def sem(self, name):
        return self.ctx.enter_context(self.nc.semaphore(f"{self.prefix}_{name}"))


def text_phase(nc, io, txt, ident, wir, wir_in, sems):
    with ExitStack() as ctx:
        S = Scope(nc, ctx, "t")
        S.sem = lambda name: sems.sem(f"t_{name}")
        h = S.sb("h", [128, 2, BATCH * TXT])
        ids = S.sb("ids", [TXT, BATCH], I32)
        ids_low = S.sb("ids_low", [TXT, BATCH])
        ids_wrapped = S.sb("ids_wrapped", [TXT, BATCH])
        ids_ok = S.sb("ids_ok", [TXT, BATCH], I32)
        ids_now = S.sb("ids_now", [TXT, 2, GATHERS], I32)
        rows = S.sb("rows", [TXT, 2, GATHERS, D])
        pos = S.sb("pos", [128, 2, TXT])
        wqk = S.sb("wqk", [128, 2, 3, 128])
        wv = S.sb("wv", [128, D])
        wf = S.sb("wf", [128, 2, D])
        vecs = S.sb("vecs", [128, 5, 2])
        hs = S.sb("hs", [128, 2, 3, 2 * TXT])
        q_all = S.sb("q_all", [128, 3, 2 * TXT])
        q_sb = S.sb("q", [128, 4, 2, 3, 2 * TXT])
        k_sb = S.sb("k", [128, 2, 3, 2 * TXT])
        v_sb = S.sb("v", [128, 4, 2 * D])
        top = S.sb("top", [TXT, 4, 3])
        rsum = S.sb("rsum", [TXT, 2, 4, 3])
        rinv = S.sb("rinv", [TXT, 2, 4, 3])
        probs = S.sb("probs", [128, 2, 4, 3, TXT])
        pt = S.sb("pt", [128, TH, TXT])
        stats = S.sb("stats", [128, 2, BATCH, 6])
        mv = S.sb("mv", [128, 2, 2])
        var_eps = S.sb("var_eps", [128, 2])
        rstd = S.sb("rstd", [128, 2])
        minus_half = S.sb("minus_half", [128, 2])
        shift = S.sb("shift", [128, 2])
        aff1 = S.sb("aff1", [128, 2, 2])
        aff2 = S.sb("aff2", [128, 2, 2])
        tb = S.sb("tb", [128, 2, 2, FCOL])

        ps_s = S.ps("scores", [128, 4, 512])
        ps_pt = S.ps("probsT", [128, 2, 512])
        ps_qk = S.ps("qk", [128, 512])
        ps_o = S.ps("mixed", [128, 512])
        v_ps = ps_s[0:TXT, 3, 3 * TXT:3 * TXT + D]
        o_ps = ps_o[:, 0:2 * TXT].rearrange("p (c t) -> p c t", c=2)

        loaded, const_ready = S.sem("loaded"), S.sem("const_ready")
        ids_ready, ids_copied = S.sem("ids_ready"), S.sem("ids_copied")
        gathered = [S.sem("gathered0"), S.sem("gathered1")]
        rows_turned, embedded, cleared = S.sem("rows_turned"), S.sem("embedded"), S.sem("cleared")
        aff1_ready, aff2_ready = S.sem("aff1_ready"), S.sem("aff2_ready")
        var_ready, rstd_ready = S.sem("var_ready"), S.sem("rstd_ready")
        base_low, base_high = S.sem("base_low"), S.sem("base_high")
        staged, projected, k_made = S.sem("staged"), S.sem("projected"), S.sem("k_made")
        q_made, q_in = S.sem("q_made"), [S.sem("q_in0"), S.sem("q_in1")]
        v_projected, v_read = S.sem("v_projected"), S.sem("v_read")
        inverted, keys_staged = S.sem("inverted"), S.sem("keys_staged")
        scored, topped, exp_done, normed = S.sem("scored"), S.sem("topped"), S.sem("exp_done"), S.sem("normed")
        turned, pt_ready, mixed, added, z_ready = (S.sem("turned"), S.sem("pt_ready"), S.sem("mixed"), S.sem("added"),
                                                   S.sem("z_ready"))
        t_ready, f_ready, u_made, u_ready = S.sem("t_ready"), S.sem("f_ready"), S.sem("u_made"), S.sem("u_ready")
        y_ready, y_turned, y_stored = S.sem("y_ready"), S.sem("y_turned"), S.sem("y_stored")
        dve_chain, passed_dve, passed_pool = S.sem("dve_chain"), S.sem("passed_dve"), S.sem("passed_pool")
        passed_sp = S.sem("passed_sp")

        def cols(b):
            return ds(b * TXT, TXT)

        def turns(engine, layer, turn):
            n0, pair0, quad0 = layer * BATCH, layer * PAIRS, layer * (BATCH // 4)
            for b in range(4):
                turn(n0 + b, b, pair0 + b // 2, quad0 + b // 4, b)
            with engine.Fori(0, BATCH // 4 - 2) as j:
                for k in range(4):
                    turn(n0 + 4 * j + 4 + k, 4 * j + 4 + k, pair0 + 2 * j + 2 + k // 2, quad0 + j + 1, k)
            for b in range(BATCH - 4, BATCH):
                turn(n0 + b, b, pair0 + b // 2, quad0 + b // 4, b % 4)

        def within(b, ahead):
            return not isinstance(b, int) or b + ahead < BATCH

        PAIRS = BATCH // 2
        block = ctx.enter_context(nc.Block())
        LOADS = 8

        @block.sync
        def _(sp):
            sp.dma_start(ids[:], io["ids"]).then_inc(loaded, 16)
            sp.dma_start(pos[:], io["pos"]).then_inc(loaded, 16)
            sp.dma_start(wqk[:], io["wqk"]).then_inc(loaded, 16)
            sp.dma_start(wv[:], io["wv"]).then_inc(loaded, 16)
            sp.dma_start(wf[:], io["Wf"]).then_inc(loaded, 16)
            sp.dma_start(vecs[:], io["vecs"]).then_inc(loaded, 16)
            sp.wait_ge(cleared, 6)
            for par in range(2):
                sp.dma_start(hs[SLICE:SLICE + 1, par, :, :], io["ones"]).then_inc(loaded, 16)

            sp.dma_start(wir[:], io["wir"]).then_inc(wir_in, 16)

            def spread(pair, par):
                sp.wait_ge(q_made, pair + 1)
                carry(sp, passed_sp)
                for r in range(4):
                    g = slice(32 * r, 32 * r + 32)
                    sp.dma_start(q_sb[g, r, par, :, :].rearrange("p c t -> p (c t)"),
                                 q_all[g, :, :].rearrange("p c t -> p (c t)")).then_inc(q_in[par], 16)

            def turn(n, b, pair, quad, p4):
                if p4 % 2 == 0 and within(b, 2):
                    spread(pair + 1, (p4 // 2 + 1) % 2)

            with sp.Fori(0, LAYERS) as layer:
                spread(layer * PAIRS, 0)
                turns(sp, layer, turn)

        @block.gpsimd
        def _(pool):
            pool.memset(minus_half[:], -0.5).then_inc(const_ready, 1)
            pool.wait_ge(const_ready, 1)
            pool.wait_ge(ids_ready, 1)
            with pool.Fori(0, BATCH // (2 * GATHERS)) as j:
                for par in range(2):
                    b = 2 * GATHERS * j + par * GATHERS
                    pool.wait_ge(rows_turned, b + GATHERS)
                    pool.tensor_copy(ids_now[:, par, :], ids_ok[:, ds(b, GATHERS)]).then_inc(ids_copied, 1)
                    pool.wait_ge(ids_copied, 2 * j + par + 1)
                    pool.sem_inc(passed_pool, 1)
                    for g in range(GATHERS):
                        pool.indirect_dma_start(
                            out=rows[:, par, g, :], out_offset=None, in_=io["emb"],
                            in_offset=bass.IndirectOffsetOnAxis(ap=ids_now[:, par, g:g + 1], axis=0),
                        ).then_inc(gathered[par], 16)

            def stage(pair, first_batch, par):
                c = ds(first_batch * TXT, 2 * TXT)
                pool.tensor_copy(hs[0:SLICE, par, 1, :], h[SLICE:D0, 0, c]).then_inc(keys_staged, 1)
                pool.wait_ge(keys_staged, pair + 1)
                carry(pool, passed_pool)
                pool.tensor_copy(hs[0:SLICE, par, 0, :], h[0:SLICE, 0, c])
                pool.tensor_copy(hs[0:SLICE, par, 2, :], h[0:D1, 1, c]).then_inc(staged, 1)

            def turn(n, b, pair, quad, p4):
                if p4 % 2 and within(b, 4):
                    pool.wait_ge(v_projected, n + 1)
                    pool.wait_ge(normed, 4 * n)
                    carry(pool, passed_pool)
                    stage(pair + 2, b + 3, p4 // 2)
                for r in range(4):
                    pool.wait_ge(inverted, 4 * n + r + 1)
                    pool.tensor_tensor(probs[0:TXT, p4 % 2, r, :, :], probs[0:TXT, p4 % 2, r, :, :],
                                       rinv[:, p4 % 2, r, :].unsqueeze(2).to_broadcast([TXT, 3, TXT]),
                                       ALU.mult).then_inc(normed, 1)

            with pool.Fori(0, LAYERS) as layer:
                pool.wait_ge(base_low, layer + 1)
                pool.wait_ge(base_high, layer + 1)
                carry(pool, passed_pool)
                stage(layer * PAIRS, 0, 0)
                pool.wait_ge(staged, layer * PAIRS + 1)
                carry(pool, passed_pool)
                stage(layer * PAIRS + 1, 2, 1)
                turns(pool, layer, turn)
                for k in range(2):
                    pool.wait_ge(var_ready, 2 * layer + k + 1)
                    pool.tensor_tensor(rstd[:], var_eps[:], minus_half[:], ALU.pow).then_inc(rstd_ready, 1)

        @block.scalar
        def _(act):
            act.wait_ge(loaded, 16 * LOADS)

            def turn(n, b, pair, quad, p4):
                par = p4 % 2
                for r in range(4):
                    if r == 2 and within(b, 2):
                        if par:
                            k_relu(pair + 1, (p4 // 2 + 1) % 2)
                        else:
                            act.wait_ge(q_in[p4 // 2], 64 * quad + 64)
                            q_relu(pair + 1)
                    act.wait_ge(topped, 4 * n + r + 1)
                    for c in range(3):
                        e = act.activation(probs[0:TXT, par, r, c, :], ps_s[0:TXT, r, c * TXT:(c + 1) * TXT], ACT.Exp,
                                           bias=top[:, r, c:c + 1], accum_out=rsum[:, par, r, c:c + 1])
                    e.then_inc(exp_done, 1)

            def q_relu(pair):
                act.wait_ge(projected, 2 * pair + 1)
                q = ps_qk[:, 0:6 * TXT].rearrange("p (c t) -> p c t", c=3)
                act.activation(q_all[:], q, ACT.Relu, scale=float(D) ** -0.5).then_inc(q_made, 1)

            def k_relu(pair, par):
                act.wait_ge(projected, 2 * pair + 2)
                act.activation(k_sb[:, par, :, :], ps_qk[:, 0:6 * TXT].rearrange("p (c t) -> p c t", c=3),
                               ACT.Relu).then_inc(k_made, 1)

            act.wait_ge(cleared, 6)
            with act.Fori(0, LAYERS) as layer:
                n0, pair0 = layer * BATCH, layer * PAIRS
                act.wait_ge(aff2_ready, layer + 1)
                act.activation(h[:, 0, :], h[:, 0, :], ACT.Identity, scale=aff2[:, 0, 0:1],
                               bias=aff2[:, 1, 0:1]).then_inc(base_low, 1)
                q_relu(pair0)
                k_relu(pair0, 0)
                turns(act, layer, turn)

                act.wait_ge(aff1_ready, layer + 1)
                with act.Fori(0, FSTEPS // 2) as j:
                    for par in range(2):
                        q = 2 * j + par
                        act.wait_ge(u_made, layer * FSTEPS + q + 1)
                        act.activation(tb[:, par, 0, :], h[:, 0, ds(q * FCOL, FCOL)], ACT.Identity,
                                       scale=aff1[:, 0, 0:1], bias=aff1[:, 1, 0:1])
                        act.activation(tb[0:D1, par, 1, :], h[0:D1, 1, ds(q * FCOL, FCOL)], ACT.Identity,
                                       scale=aff1[0:D1, 0, 1:2], bias=aff1[0:D1, 1, 1:2]).then_inc(t_ready, 1)
            act.wait_ge(aff2_ready, LAYERS + 1)
            with act.Fori(0, FSTEPS // 2) as j:
                for par in range(2):
                    q = 2 * j + par
                    act.wait_ge(y_stored, 4 * q + 4)
                    act.activation(tb[:, par, 0, :], h[:, 0, ds(q * FCOL, FCOL)], ACT.Identity,
                                   scale=aff2[:, 0, 0:1], bias=aff2[:, 1, 0:1])
                    act.activation(tb[0:D1, par, 1, :], h[0:D1, 1, ds(q * FCOL, FCOL)], ACT.Identity,
                                   scale=aff2[0:D1, 0, 1:2], bias=aff2[0:D1, 1, 1:2]).then_inc(y_ready, 1)

        @block.tensor
        def _(pe):
            pe.wait_ge(loaded, 16 * LOADS)
            pe.sem_inc(rows_turned, 2 * GATHERS)
            with pe.Fori(0, BATCH // (2 * GATHERS)) as j:
                for par in range(2):
                    pe.wait_ge(gathered[par], GATHERS * (16 * j + 16))
                    for g in range(GATHERS):
                        pe.wait_ge(embedded, 2 * GATHERS * j + par * GATHERS + g + 1)
                        pe.transpose(ps_s[:, g % 2, 0:TXT], rows[:, par, g, 0:D0], ident[0:TXT, 0:TXT])
                        pe.transpose(ps_s[0:D1, g % 2, TXT:2 * TXT], rows[:, par, g, D0:D], ident[0:TXT, 0:TXT]).then_inc(rows_turned, 1)

            def project(pair, par, which):
                pe.wait_ge(staged, pair + 1)
                for c in range(3):
                    mm = pe.matmul(ps_qk[:, 2 * c * TXT:2 * (c + 1) * TXT], wqk[:, which, c, :], hs[:, par, which, :],
                                   start=True, stop=True)
                mm.then_inc(projected, 1)

            def project_v(par, k):
                pe.matmul(v_ps, hs[:, par, 2, k * TXT:(k + 1) * TXT], wv[:], start=True, stop=True).then_inc(v_projected, 1)

            def scores(n, p4, r):
                t = slice((p4 % 2) * TXT, (p4 % 2 + 1) * TXT)
                for c in range(3):
                    mm = pe.matmul(ps_s[0:TXT, r, c * TXT:(c + 1) * TXT], q_sb[:, r, p4 // 2, c, t], k_sb[:, p4 // 2, c, t],
                                   start=True, stop=True)
                mm.then_inc(scored, 1)

            def turn_probs(n, p4):
                for r in range(4):
                    pe.wait_ge(normed, 4 * n + r + 1)
                    for c in range(3):
                        hh = 3 * (r % 2) + c
                        mm = pe.transpose(ps_pt[0:TXT, r // 2, hh * TXT:(hh + 1) * TXT], probs[0:TXT, p4 % 2, r, c, :], ident[0:TXT, 0:TXT])
                    if r % 2:
                        mm.then_inc(turned, 1)

            def mix(n, p4):
                pe.wait_ge(added, n + 1)
                for half in range(2):
                    pe.wait_ge(pt_ready, 2 * n + half + 1)
                    for c in range(3):
                        g = 2 * c + half
                        for k in range(2):
                            mm = pe.matmul(o_ps[32 * (g % 4):32 * (g % 4) + 32, g // 4, :],
                                           v_sb[:, p4, 32 * (2 * g + k):32 * (2 * g + k) + 32],
                                           pt[:, 6 * half + 3 * k + c, :], start=(k == 0), stop=(k == 1))
                mm.then_inc(mixed, 1)

            def turn(n, b, pair, quad, p4):
                pe.wait_ge(q_in[p4 // 2], 64 * quad + 64)
                pe.wait_ge(k_made, pair + 1)
                for r in range(3):
                    pe.wait_ge(exp_done, 4 * n + r + 1)
                    scores(n, p4, r)
                pe.wait_ge(exp_done, 4 * n + 4)
                pe.wait_ge(v_read, n + 1)
                if within(b, 1):
                    project_v(((p4 + 1) // 2) % 2, (p4 + 1) % 2)
                scores(n, p4, 3)
                if within(b, 2):
                    if p4 % 2:
                        pe.wait_ge(q_made, pair + 2)
                    project(pair + 1, (p4 // 2 + 1) % 2, p4 % 2)
                if p4 or not isinstance(b, int) or b:
                    turn_probs(n - 1, (p4 + 3) % 4)
                if p4 or not isinstance(b, int) or b:
                    mix(n - 1, (p4 + 3) % 4)

            with pe.Fori(0, LAYERS) as layer:
                n0, pair0 = layer * BATCH, layer * PAIRS
                project(pair0, 0, 0)
                pe.wait_ge(q_made, pair0 + 1)
                project(pair0, 0, 1)
                project_v(0, 0)
                turns(pe, layer, turn)
                turn_probs(n0 + BATCH - 1, 3)
                mix(n0 + BATCH - 1, 3)
                with pe.Fori(0, FSTEPS // 2) as j:
                    for par in range(2):
                        pe.wait_ge(t_ready, layer * FSTEPS + 2 * j + par + 1)
                        lo, hi = tb[:, par, 0, :], tb[:, par, 1, :]
                        pe.matmul(ps_s[:, par, 0:FCOL], wf[:, 0, 0:D0], lo, start=True, stop=False)
                        pe.matmul(ps_s[:, par, 0:FCOL], wf[:, 1, 0:D0], hi, start=False, stop=True)
                        pe.matmul(ps_s[0:D1, 2 + par, 0:FCOL], wf[:, 0, D0:D], lo, start=True, stop=False)
                        pe.matmul(ps_s[0:D1, 2 + par, 0:FCOL], wf[:, 1, D0:D], hi, start=False, stop=True).then_inc(f_ready, 1)
            with pe.Fori(0, FSTEPS // 2) as j:
                for par in range(2):
                    pe.wait_ge(y_ready, 2 * j + par + 1)
                    for k in range(4):
                        t = slice(k * TXT, (k + 1) * TXT)
                        pe.wait_ge(y_stored, 8 * j + 4 * par + k + 7)
                        pe.transpose(ps_s[0:TXT, k % 2, 0:D0], tb[:, par, 0, t], ident[:])
                        pe.transpose(ps_s[0:TXT, k % 2, D0:D], tb[0:D1, par, 1, t], ident[0:D1, 0:D1]).then_inc(y_turned, 1)

        @block.vector
        def _(dve):
            ch = Chain(dve, dve_chain)
            for t in (hs, v_sb, probs, pt, q_sb, tb):
                dve.memset(t[:], 0.0).then_inc(cleared, 1)
            dve.sem_inc(embedded, 2)
            dve.sem_inc(added, 1)
            dve.sem_inc(exp_done, 4)
            dve.sem_inc(u_made, 2)
            dve.sem_inc(y_stored, 8)
            dve.wait_ge(loaded, 16 * LOADS)
            ch.step(dve.tensor_scalar(ids_low[:], ids[:], 0.0, float(VOCAB), ALU.is_lt, ALU.mult))
            ch.settle()
            ch.step(dve.tensor_tensor(ids_wrapped[:], ids[:], ids_low[:], ALU.add))
            ch.settle()
            dve.tensor_scalar(ids_ok[:], ids_wrapped[:], 0.0, float(VOCAB - 1), ALU.max, ALU.min).then_inc(ids_ready, 1)
            dve.memset(aff2[:, 0, :], 1.0)
            ch.step(dve.memset(aff2[:, 1, :], 0.0))
            ch.step(dve.memset(mv[:], 1.0))
            ch.settle()
            with dve.Fori(0, BATCH // 2) as j:
                for par in range(2):
                    b = 2 * j + par
                    dve.wait_ge(rows_turned, b + 2 * GATHERS + 1)
                    dve.scalar_tensor_tensor(out=h[:, 0, cols(b)], in0=ps_s[:, par, 0:TXT], scalar=2.0,
                                             in1=pos[:, 0, :], op0=ALU.mult, op1=ALU.add)
                    dve.scalar_tensor_tensor(out=h[0:D1, 1, cols(b)], in0=ps_s[0:D1, par, TXT:2 * TXT], scalar=2.0,
                                             in1=pos[0:D1, 1, :], op0=ALU.mult, op1=ALU.add).then_inc(embedded, 1)
            dve.wait_ge(embedded, BATCH + 2)
            dve.sem_inc(aff2_ready, 1)

            def v_relu(n, par):
                v4 = v_ps.rearrange("p (g two d) -> p g two d", two=2, d=HD)
                to = v_sb[0:TXT, par, :].rearrange("p (g w) -> p g w", w=4 * HD)
                dve.wait_ge(v_projected, n + 1)
                dve.tensor_scalar(to[:, :, 0:HD], v4[:, :, 0, :], 0.0, None, ALU.max)
                dve.tensor_scalar(to[:, :, 3 * HD:4 * HD], v4[:, :, 1, :], 0.0, None, ALU.max).then_inc(v_read, 1)

            def turn(n, b, pair, quad, p4):
                for r in range(4):
                    dve.wait_ge(scored, 4 * n + r + 1)
                    if r == 2 and not (isinstance(b, int) and b < 2):
                        add_mixed(n - 2, b - 2)
                    if r == 3 and within(b, 1):
                        v_relu(n + 1, (p4 + 1) % 4)
                    dve.tensor_reduce(out=top[:, r, :], in_=ps_s[0:TXT, r, 0:3 * TXT].rearrange("p (c t) -> p c t", c=3),
                                      axis=AX.X, op=ALU.max, negate=True).then_inc(topped, 1)
                if p4 or not isinstance(b, int) or b:
                    copy_probs(n - 1)
                invert(n, p4 % 2, 0)
                invert(n, p4 % 2, 2)

            def invert(n, par, first):
                for r in range(first, first + 2):
                    dve.wait_ge(exp_done, 4 * n + r + 5)
                    dve.reciprocal(rinv[:, par, r, :], rsum[:, par, r, :]).then_inc(inverted, 1)

            def copy_probs(n):
                for half in range(2):
                    dve.wait_ge(turned, 2 * n + half + 1)
                    dve.tensor_copy(pt[0:TXT, 6 * half:6 * half + 6, :],
                                    ps_pt[0:TXT, half, 0:HHALF].rearrange("p (h t) -> p h t", h=TH // 2)).then_inc(pt_ready, 1)

            def add_mixed(n, b):
                dve.wait_ge(mixed, n + 1)
                dve.tensor_tensor(h[:, 0, cols(b)], h[:, 0, cols(b)], o_ps[:, 0, :], ALU.add)
                dve.tensor_tensor(h[0:D1, 1, cols(b)], h[0:D1, 1, cols(b)], o_ps[0:D1, 1, :], ALU.add).then_inc(added, 1)
                dve.wait_ge(added, n + 2)
                dve.bn_stats(out=stats[:, 0, ds(b, 1), :], in_=h[:, 0, cols(b)])
                dve.bn_stats(out=stats[0:D1, 1, ds(b, 1), :], in_=h[0:D1, 1, cols(b)]).then_inc(z_ready, 1)

            def affine(aff, count, which, n, ready):
                dve.bn_aggr(out=mv[:, 0, :], in_=stats[:, 0, 0:count, :].rearrange("p n s -> p (n s)"))
                ch.step(dve.bn_aggr(out=mv[0:D1, 1, :], in_=stats[0:D1, 1, 0:count, :].rearrange("p n s -> p (n s)")))
                ch.settle()
                dve.tensor_scalar(var_eps[:], mv[:, :, 1], BN_EPS, None, ALU.add).then_inc(var_ready, 1)
                dve.wait_ge(rstd_ready, n)
                ch.step(dve.tensor_tensor(aff[:, 0, :], vecs[:, which, :], rstd[:], ALU.mult))
                ch.settle()
                ch.step(dve.tensor_tensor(shift[:], mv[:, :, 0], aff[:, 0, :], ALU.mult))
                ch.settle()
                dve.tensor_tensor(aff[:, 1, :], vecs[:, which + 1, :], shift[:], ALU.subtract).then_inc(ready, 1)

            LAYER_CHAIN = 6
            with dve.Fori(0, LAYERS) as layer:
                ch.enter(layer * LAYER_CHAIN)
                start, base = ch.start, ch.base
                n0 = layer * BATCH
                dve.wait_ge(aff2_ready, layer + 1)
                dve.tensor_scalar(h[0:D1, 1, :], h[0:D1, 1, :], aff2[0:D1, 0, 1:2], aff2[0:D1, 1, 1:2],
                                  ALU.mult, ALU.add).then_inc(base_high, 1)
                v_relu(n0, 0)
                turns(dve, layer, turn)
                add_mixed(n0 + BATCH - 2, BATCH - 2)
                copy_probs(n0 + BATCH - 1)
                add_mixed(n0 + BATCH - 1, BATCH - 1)
                dve.wait_ge(z_ready, n0 + BATCH)
                dve.sem_inc(passed_dve, 1)
                affine(aff1, BATCH, 1, 2 * layer + 1, aff1_ready)
                done = ch.n
                with dve.Fori(0, FSTEPS // 2) as j:
                    for par in range(2):
                        q = 2 * j + par
                        dve.wait_ge(f_ready, layer * FSTEPS + q + 1)
                        dve.scalar_tensor_tensor(out=h[:, 0, ds(q * FCOL, FCOL)], in0=ps_s[:, par, 0:FCOL], scalar=vecs[:, 0, 0:1],
                                                 in1=tb[:, par, 0, :], op0=ALU.add, op1=ALU.add)
                        dve.scalar_tensor_tensor(out=h[0:D1, 1, ds(q * FCOL, FCOL)], in0=ps_s[0:D1, 2 + par, 0:FCOL],
                                                 scalar=vecs[0:D1, 0, 1:2], in1=tb[0:D1, par, 1, :], op0=ALU.add,
                                                 op1=ALU.add).then_inc(u_made, 1)
                        dve.wait_ge(u_made, layer * FSTEPS + q + 3)
                        dve.bn_stats(out=stats[:, 0, ds(q, 1), :], in_=h[:, 0, ds(q * FCOL, FCOL)])
                        dve.bn_stats(out=stats[0:D1, 1, ds(q, 1), :], in_=h[0:D1, 1, ds(q * FCOL, FCOL)]).then_inc(u_ready, 1)
                ch.base, ch.n = base, done
                dve.wait_ge(u_ready, (layer + 1) * FSTEPS)
                dve.sem_inc(passed_dve, 1)
                affine(aff2, FSTEPS, 3, 2 * layer + 2, aff2_ready)
                assert ch.n == LAYER_CHAIN, ch.n
                ch.start = start
            with dve.Fori(0, BATCH // 2) as j:
                for par in range(2):
                    b = 2 * j + par
                    dve.wait_ge(y_turned, b + 1)
                    dve.tensor_copy(txt[:, ds(b, 1), :], ps_s[0:TXT, par, 0:D]).then_inc(y_stored, 1)


def carry(engine, sem):
    engine.sem_inc(sem, 1)


def fusion_phase(nc, io, out, txt, ident, rows_dram, table_dram, run, sems):
    with ExitStack() as ctx:
        S = Scope(nc, ctx, "f")
        S.sem = lambda name: sems.sem(f"f_{name}")
        xk = S.sb("patches", [128, 2, KP, 2 * CH])
        wt = S.sb("w_tok", [128, KP, D])
        posb = S.sb("pos_bias", [CH, 2, D])
        bias = S.sb("bias", [CH, 2, D])
        wq = S.sb("wq", [128, KD, DIM])
        wk = S.sb("wk", [128, KD, DIM])
        wv = S.sb("wv", [128, KD, DIM])
        wg = S.sb("wg", [128, KD, D])
        wo = S.sb("wo", [128, DIM // 128, D])
        wr = S.sb("wr", [128, KD, EXP])
        lnw = S.sb("lnw", [CH, D])
        mask = S.sb("mask", [CH, ATW])
        tri = S.sb("tri", [CH, CH], BF16)
        ones = S.sb("ones", [CH, CH], BF16)
        rank = S.sb("rank", [CH, NC_, EXP])
        minus_half = S.sb("minus_half", [CH, NC_])
        pad_ids = S.sb("pad_ids", [128, TABLE // 128], I32)
        tid = S.sb("tid", [CH, NC_])
        tid_i = S.sb("tid_i", [CH, 2, NC_], I32)

        h = S.sb("h", [CH, 4, NC_, D])
        st1, st2 = S.sb("st1", [CH, NC_, 6]), S.sb("st2", [CH, NC_, 6])
        mv1, mv2 = S.sb("mv1", [CH, NC_, 2]), S.sb("mv2", [CH, NC_, 2])
        ve1, ve2 = S.sb("ve1", [CH, NC_]), S.sb("ve2", [CH, NC_])
        rs1, rs2, rms = S.sb("rs1", [CH, NC_]), S.sb("rs2", [CH, NC_]), S.sb("rms", [CH, NC_])
        ms1, ms2, ms3 = (S.sb(n, [CH, NC_]) for n in ("ms1", "ms2", "ms3"))
        ln = S.sb("ln", [CH, NC_, D])
        xT = S.sb("xT", [128, 2, KD, PADT])
        e_sb = S.sb("e", [128, 4, SEQ])
        r_sb = S.sb("r", [128, 4, SEQ])
        qk = S.sb("qk", [128, 2, 4, PADT])
        va = S.sb("va", [128, 2, NC_, AH, AD + 1])
        th = S.sb("th", [CH, 2, NC_, D])
        at = S.sb("at", [128, AH, ATW])
        den, rden = S.sb("den", [CH, NC_, AH]), S.sb("rden", [CH, NC_, AH])
        o = S.sb("o", [CH, NC_, AH, AD])
        oT = S.sb("oT", [128, 2, PADT])
        gated = S.sb("gated", [CH, NC_, D])
        ln2 = S.sb("ln2", [CH, NC_, D])
        rt = S.sb("rt", [CH, 2, NC_, ROW])
        nT = S.sb("nT", [128, KD, PADT])
        best = S.sb("best", [CH, NC_])
        eq, less, ex = (S.sb(n, [CH, NC_, EXP]) for n in ("eq", "less", "ex"))
        esum = S.sb("esum", [CH, NC_])
        ranked = S.sb("ranked", [CH, NC_, EXP])
        first = S.sb("first", [CH, NC_])
        hot = S.sb("hot", [CH, NC_, EXP], BF16)
        at_cum, at_run = S.sb("at_cum", [CH, NC_, EXP]), S.sb("at_run", [CH, NC_, EXP])
        prio, place, over = (S.sb(n, [CH, NC_]) for n in ("prio", "place", "over"))
        slot0 = S.sb("slot0", [CH, NC_])
        slot = S.sb("slot", [CH, 2, NC_], I32)
        ob = S.sb("ob", [CH, 2, NC_, D])

        B = [S.ps(f"bank{n}", [128, 512]) for n in range(8)]

        loaded, made, filled = S.sem("loaded"), S.sem("made"), S.sem("filled")
        xk_in = [S.sem("xk_in0"), S.sem("xk_in1")]
        rows_out = [S.sem("rows_out0"), S.sem("rows_out1")]
        slots_out = [S.sem("slots_out0"), S.sem("slots_out1")]
        (tok_done, h_ready, text_ready, var1, rstd1, ln1, xT_turned, xT_lo, xT_hi, qk_done, qk_read, fm,
         vg_done, vg_ready, at_done, masked, num_done, o_ready, oT_turned, oT_ready, oT_high, y_done, h2_ready,
         var2, rstd2, rms_ready, l_ready, normed, base_ready, nT_turned, nT_ready, lg_done, ex_in, ex_ready,
         rp_ready, hot_ready, cum_done, slots_ready, ob_ready, pool_chain, chain, passed_dve, passed_pool) = (S.sem(n) for n in (
             "tok_done", "h_ready", "text_ready", "var1", "rstd1", "ln1", "xT_turned", "xT_lo", "xT_hi", "qk_done",
             "qk_read", "fm", "vg_done", "vg_ready", "at_done", "masked", "num_done", "o_ready", "oT_turned", "oT_ready", "oT_high",
             "y_done", "h2_ready", "var2", "rstd2", "rms_ready", "l_ready", "normed", "base_ready", "nT_turned",
             "nT_ready", "lg_done", "ex_in", "ex_ready", "rp_ready", "hot_ready", "cum_done", "slots_ready", "ob_ready",
             "pool_chain", "chain", "passed_dve", "passed_pool"))
        LOADS = 12
        MADE = 14

        def turns(engine, turn):
            for i in range(8):
                turn(i, i % 4, True, i >= 1, i >= 2, i >= 3, i >= 4)
            with engine.Fori(0, BATCH // 4 - 3) as j:
                for k in range(4):
                    turn(4 * j + 8 + k, k, True, True, True, True, True)
            for i in range(BATCH - 4, BATCH + 4):
                turn(i, i % 4, i < BATCH, i - 1 < BATCH, i - 2 < BATCH, i - 3 < BATCH, True)

        passed_sp = S.sem("passed_sp")
        block = ctx.enter_context(nc.Block())
        rows_v = rows_dram.rearrange("(b t) n -> b t n", t=SEQ)

        @block.sync
        def _(sp):
            sp.dma_start(wt[:], io["w_tok"]).then_inc(loaded, 16)
            sp.dma_start(posb[:], io["pos_emb"]).then_inc(loaded, 16)
            sp.dma_start(bias[:], io["tok_bias"]).then_inc(loaded, 16)
            for t, n in ((wq, "a_wq"), (wk, "a_wk"), (wv, "a_wv"), (wg, "a_wg")):
                sp.dma_start(t[:], io[n]).then_inc(loaded, 16)
            sp.dma_start(wo[:], io["a_wo"].rearrange("(k p) n -> p k n", p=128)).then_inc(loaded, 16)
            sp.dma_start(wr[:], io["w_router"]).then_inc(loaded, 16)
            sp.dma_start(lnw[:], io["ln_w"].partition_broadcast(CH)).then_inc(loaded, 16)
            sp.dma_start(mask[:], io["mask"]).then_inc(loaded, 16)
            sp.dma_start(rank[:], io["rank"]).then_inc(loaded, 16)
            sp.wait_ge(made, MADE)
            sp.dma_start(table_dram.rearrange("(p n) o -> p (n o)", p=128), pad_ids[:]).then_inc(filled, 16)

            def load_patches(b, p2):
                sp.wait_ge(tok_done, b + 1)
                carry(sp, passed_sp)
                sp.dma_start(xk[:, p2, :, :].rearrange("p k t -> p (k t)"),
                             io["patches"][ds(b, 1), :, :].rearrange("b p n -> (b p) n")).then_inc(xk_in[p2], 16)

            def store_rows(b, q):
                sp.wait_ge(ob_ready, b + 1)
                carry(sp, passed_sp)
                for n in range(NC_):
                    rows = slice(0, C_LEN[n])
                    sp.dma_start(rows_v[ds(b, 1), C_OFF[n]:C_OFF[n] + C_LEN[n], :].rearrange("b t n -> (b t) n"),
                                 rt[rows, q, n, :]).then_inc(rows_out[q], 16)
                    sp.dma_start(out[ds(b, 1), C_OFF[n]:C_OFF[n] + C_LEN[n], :].rearrange("b t n -> (b t) n"),
                                 ob[rows, q, n, :]).then_inc(rows_out[q], 16)

            LAG = 5
            for b in range(LAG + 1):
                if b >= LAG:
                    store_rows(b - LAG, (b - LAG) % 2)
                load_patches(b, b % 2)
            with sp.Fori(0, (BATCH - LAG - 1) // 2) as j:
                for k in range(2):
                    store_rows(2 * j + 1 + k, (1 + k) % 2)
                    load_patches(2 * j + LAG + 1 + k, k)
            for b in range(BATCH - LAG, BATCH):
                store_rows(b, b % 2)
            for q in range(2):
                sp.wait_ge(rows_out[q], 16 * 6 * (BATCH // 2))

        @block.gpsimd
        def _(pool):
            pool.memset(pad_ids[:], NO_ROW).then_inc(made, 1)
            for t in (h, th, den):
                pool.memset(t[:], 1.0).then_inc(made, 1)
            for t in (xT, qk, oT, nT, rt, at):
                pool.memset(t[:], 0.0).then_inc(made, 1)
            pool.memset(va[:], 1.0).then_inc(made, 1)
            pool.memset(minus_half[:], -0.5).then_inc(made, 1)
            pool.memset(ones[:], 1.0).then_inc(made, 1)
            pool.iota(tid[:], [[CH, NC_]], base=0, channel_multiplier=1, allow_small_or_imprecise_dtypes=True).then_inc(made, 1)
            pool.wait_ge(made, MADE)
            pool.wait_ge(loaded, 16 * LOADS)
            pool.wait_ge(filled, 16)

            ch = Chain(pool, pool_chain)

            def turn(i, p4, a, b1, b2, c, d):
                p2 = p4 % 2
                if c:
                    pool.wait_ge(var2, i - 2)
                    pool.tensor_tensor(rs2[:], ve2[:], minus_half[:], ALU.pow).then_inc(rstd2, 1)
                    pool.wait_ge(rstd2, i - 2)
                    ch.step(pool.tensor_tensor(ms1[:], mv2[:, :, 1], rs2[:], ALU.mult))
                    ch.settle()
                    ch.step(pool.tensor_tensor(ms2[:], ms1[:], rs2[:], ALU.mult))
                    ch.settle()
                    carry(pool, passed_pool)
                    ch.step(pool.tensor_scalar(ms3[:], ms2[:], 1e-6, None, ALU.add))
                    ch.settle()
                    pool.tensor_tensor(rms[:], ms3[:], minus_half[:], ALU.pow).then_inc(rms_ready, 1)
                if a:
                    pool.wait_ge(var1, i + 1)
                    pool.tensor_tensor(rs1[:], ve1[:], minus_half[:], ALU.pow).then_inc(rstd1, 1)
                if c:
                    q = 1 - p2
                    pool.wait_ge(normed, i - 2)
                    pool.tensor_tensor(rt[:, q, :, D:2 * D], h[:, (p4 + 1) % 4, :, :], ln2[:], ALU.add).then_inc(base_ready, 1)
                if d:
                    pool.wait_ge(slots_ready, i - 2)
                    carry(pool, passed_pool)
                    for n in range(NC_):
                        rows = slice(0, C_LEN[n])
                        pool.indirect_dma_start(
                            out=table_dram, out_offset=bass.IndirectOffsetOnAxis(ap=slot[rows, p2, n:n + 1], axis=0),
                            in_=tid_i[rows, p2, n:n + 1], in_offset=None,
                            bounds_check=EXP * REGION - 1, oob_is_err=False).then_inc(slots_out[p2], 16)
                if c:
                    q = 1 - p2
                    pool.wait_ge(rp_ready, i - 2)
                    carry(pool, passed_pool)
                    for n in range(NC_):
                        mm = pool.tensor_scalar(ob[:, q, n, :], rt[:, q, n, 0:D], rt[:, q, n, 2 * D:2 * D + 1], None, ALU.mult)
                    ch.step(mm)
                    ch.settle()
                    pool.tensor_tensor(ob[:, q, :, :], ob[:, q, :, :], rt[:, q, :, D:2 * D], ALU.add).then_inc(ob_ready, 1)
            PER = 4
            for i in range(8):
                turn(i, i % 4, True, i >= 1, i >= 2, i >= 3, i >= 4)
            done = ch.n
            with pool.Fori(0, BATCH // 4 - 3) as j:
                for k in range(4):
                    ch.base, ch.n = done + (4 * j + k) * PER, 0
                    turn(4 * j + 8 + k, k, True, True, True, True, True)
                    assert ch.n == PER, ch.n
            ch.base, ch.n = done + (BATCH - 12) * PER, 0
            for i in range(BATCH - 4, BATCH + 4):
                turn(i, i % 4, i < BATCH, i - 1 < BATCH, i - 2 < BATCH, i - 3 < BATCH, True)
            for q in range(2):
                pool.wait_ge(slots_out[q], 16 * NC_ * (BATCH // 2))

        @block.scalar
        def _(act):
            act.wait_ge(made, MADE)

            def turn(i, p4, a, b1, b2, c, d):
                p2 = p4 % 2
                if a:
                    if not isinstance(i, int) or i >= 4:
                        act.wait_ge(l_ready, i - 3)
                        act.wait_ge(base_ready, i - 3)
                    act.activation(h[0:TXT, p4, 2, :], txt[:, ds(i, 1), :].rearrange("p b n -> p (b n)"), ACT.Copy).then_inc(text_ready, 1)
                if b1:
                    q = 1 - p2
                    for n in range(4):
                        act.wait_ge(qk_done, 4 * (i - 1) + n + 1)
                        act.wait_ge(fm, 4 * (i - 1) + n + 1)
                        act.activation(e_sb[:, n, :], B[3 + n][:, 0:SEQ], ACT.Exp)
                        act.activation(r_sb[:, n, :], B[3 + n][:, 0:SEQ], ACT.Relu).then_inc(qk_read, 1)
                if c:
                    act.wait_ge(nT_turned, i - 2)
                    act.activation(nT[0:96, 0, 0:SEQ], B[1][0:96, 0:SEQ], ACT.Copy)
                    act.activation(nT[0:96, 1, 0:SEQ], B[2][0:96, 0:SEQ], ACT.Copy).then_inc(nT_ready, 1)
                if b1:
                    act.wait_ge(vg_done, 4 * (i - 1) + 1)
                    act.activation(va[0:CH, q, 0:2, :, 0:AD], B[3][0:CH, :].rearrange("p (c h e) -> p c h e", c=2, h=AH), ACT.Copy).then_inc(vg_ready, 1)
                    act.wait_ge(vg_done, 4 * (i - 1) + 2)
                    act.activation(va[0:CH, q, 2, :, 0:AD], B[4][0:CH, 0:DIM].rearrange("p (h e) -> p h e", h=AH), ACT.Copy).then_inc(vg_ready, 1)
                    act.wait_ge(vg_done, 4 * (i - 1) + 3)
                    act.activation(th[:, q, 0:2, :], B[5][0:CH, 0:2 * D].rearrange("p (c n) -> p c n", c=2), ACT.Tanh, scale=0.5).then_inc(vg_ready, 1)
                    act.wait_ge(vg_done, 4 * (i - 1) + 4)
                    act.activation(th[:, q, 2, :], B[6][0:CH, 0:D], ACT.Tanh, scale=0.5).then_inc(vg_ready, 1)
                if a:
                    act.wait_ge(xT_turned, i + 1)
                    act.activation(xT[0:96, p2, 0, 0:SEQ], B[1][0:96, 0:SEQ], ACT.Copy).then_inc(xT_lo, 1)
                if b2:
                    act.wait_ge(oT_turned, i - 1)
                    act.activation(oT[:, 0, 0:SEQ], B[1][:, 0:SEQ], ACT.Copy).then_inc(oT_ready, 1)
                if c:
                    act.wait_ge(ex_in, i - 2)
                    act.activation(ex[:], less[:], ACT.Exp).then_inc(ex_ready, 1)
            turns(act, turn)

        @block.tensor
        def _(pe):
            pe.wait_ge(loaded, 16 * LOADS)
            pe.wait_ge(made, MADE)
            pe.sem_inc(tok_done, 2)

            def tokens(i, p2, part):
                if part == 0:
                    pe.wait_ge(h_ready, i + 1)
                    pe.wait_ge(xk_in[p2], 16 * ((i - p2) // 2) + 16 if isinstance(i, int) else 8 * (i - p2) + 16)
                n, runs = ((0, range(0, KP // 2)), (0, range(KP // 2, KP)), (1, range(KP)))[part]
                for k in runs:
                    mm = pe.matmul(B[0][0:CH, n * D:(n + 1) * D], xk[:, p2, k, n * CH:(n + 1) * CH], wt[:, k, :],
                                   start=(k == 0), stop=(k == KP - 1))
                if part == 2:
                    mm.then_inc(tok_done, 1)

            def turned(source):
                for k in range(KD):
                    for n in range(NC_):
                        mm = pe.transpose(B[1 + k][0:96, C_OFF[n]:C_OFF[n] + C_LEN[n]],
                                          source[0:C_LEN[n], n, 96 * k:96 * k + 96], ident[0:C_LEN[n], 0:C_LEN[n]])
                return mm

            def attend(m, p2, projected):
                pe.wait_ge(fm, 4 * m + 8)
                for g in range(2):
                    for part in range(2):
                        for r in range(2):
                            n = 4 * g + 2 * part + r
                            bank = B[3 + n % 4]
                            if n >= 4:
                                pe.wait_ge(masked, 8 * m + n - 3)
                            elif projected:
                                pe.wait_ge(qk_read, 4 * (m + 1) + n + 1)
                            kh = qk[AD * r:AD * r + AD, p2, 2 + g, :]
                            qh = qk[AD * r:AD * r + AD, p2, g, :]
                            if part == 0:
                                mm = pe.matmul(bank[0:CH, 0:SEQ], kh[:, 0:CH], qh[:, 0:SEQ], start=True, stop=True)
                            else:
                                w1 = SEQ - C_OFF[1]
                                pe.matmul(bank[0:CH, 0:w1], kh[:, C_OFF[1]:C_OFF[1] + CH], qh[:, C_OFF[1]:SEQ], start=True, stop=True)
                                mm = pe.matmul(bank[0:CH, w1:w1 + C_LEN[2]], kh[:, C_OFF[2]:PADT], qh[:, C_OFF[2]:SEQ],
                                               start=True, stop=True)
                            mm.then_inc(at_done, 1)

            def queries_keys(m, p2, attended, finished):
                pe.wait_ge(xT_lo, m + 1)
                pe.wait_ge(xT_hi, m + 1)
                if finished:
                    pe.wait_ge(h2_ready, m - 1)
                elif attended:
                    pe.wait_ge(vg_ready, 4 * m)
                for n, (w, c) in enumerate(((wq, 0), (wq, 1), (wk, 0), (wk, 1))):
                    for k in range(KD):
                        mm = pe.matmul(B[3 + n][:, 0:SEQ], w[:, k, 128 * c:128 * c + 128], xT[:, p2, k, 0:SEQ],
                                       start=(k == 0), stop=(k == KD - 1))
                    mm.then_inc(qk_done, 1)

            def values_gate(m, p2, attended):
                for n, (w, width, chunks) in enumerate(((wv, DIM, (0, 1)), (wv, DIM, (2,)), (wg, D, (0, 1)), (wg, D, (2,)))):
                    if attended:
                        pe.wait_ge(masked, 8 * (m - 1) + n + 5)
                    else:
                        pe.wait_ge(qk_read, 4 * m + n + 1)
                    for c, cc in enumerate(chunks):
                        for k in range(KD):
                            mm = pe.matmul(B[3 + n][0:CH, c * width:(c + 1) * width], xT[:, p2, k, C_OFF[cc]:C_OFF[cc] + CH], w[:, k, :],
                                           start=(k == 0), stop=(k == KD - 1))
                    mm.then_inc(vg_done, 1)

            def numerators(m, p2, projected):
                pe.wait_ge(masked, 8 * m + 8)
                if not projected:
                    pe.wait_ge(vg_ready, 4 * m + 4)
                for n in range(NC_):
                    if projected:
                        pe.wait_ge(vg_ready, 4 * m + 5 + n)
                    for hh in range(AH):
                        for jj in range(n + 1):
                            at0 = (AT0, AT1, AT2)[jj] + C_OFF[n] - C_OFF[jj]
                            mm = pe.matmul(B[3 + n][0:C_LEN[n], hh * (AD + 1):(hh + 1) * (AD + 1)],
                                           at[:, hh, at0:at0 + C_LEN[n]], va[:, p2, jj, hh, :],
                                           start=(jj == 0), stop=(jj == n))
                    mm.then_inc(num_done, 1)

            def counts(m):
                pe.wait_ge(hot_ready, m + 1)
                for n in range(NC_):
                    for jj in range(n + 1):
                        w = tri if jj == n else ones
                        pe.matmul(B[7][0:CH, n * EXP:(n + 1) * EXP], w[0:C_LEN[jj], :], hot[0:C_LEN[jj], jj, :],
                                  start=(jj == 0), stop=(jj == n))
                for jj in range(NC_):
                    mm = pe.matmul(B[7][0:CH, NC_ * EXP:(NC_ + 1) * EXP], ones[0:C_LEN[jj], :], hot[0:C_LEN[jj], jj, :],
                                   start=(jj == 0), stop=(jj == NC_ - 1))
                mm.then_inc(cum_done, 1)

            def turn(i, p4, a, b1, b2, c, d):
                p2 = p4 % 2
                q2 = 1 - p2
                following = not isinstance(i, int) or i + 1 < BATCH
                if isinstance(i, int) and i == 0:
                    tokens(0, 0, 0)
                    tokens(0, 0, 1)
                if a:
                    tokens(i, p2, 2)
                if b1:
                    queries_keys(i - 1, q2, attended=b2, finished=c)
                if b2:
                    if c and not b1:
                        pe.wait_ge(h2_ready, i - 2)
                    attend(i - 2, p2, projected=b1)
                if c:
                    pe.wait_ge(normed, i - 2)
                    turned(rt[:, q2, :, :]).then_inc(nT_turned, 1)
                if b1:
                    values_gate(i - 1, q2, attended=b2)
                if b2:
                    numerators(i - 2, p2, projected=b1)
                if c:
                    pe.wait_ge(nT_ready, i - 2)
                    pe.wait_ge(slots_ready, i - 2)
                    for n in range(NC_):
                        for k in range(KD):
                            mm = pe.matmul(B[7][0:CH, n * EXP:(n + 1) * EXP], nT[:, k, C_OFF[n]:C_OFF[n] + CH], wr[:, k, :],
                                           start=(k == 0), stop=(k == KD - 1))
                    mm.then_inc(lg_done, 1)
                if a:
                    pe.wait_ge(ln1, i + 1)
                    turned(ln).then_inc(xT_turned, 1)
                if following:
                    tokens(i + 1, q2, 0)
                if b2:
                    pe.wait_ge(o_ready, i - 1)
                    if a:
                        pe.wait_ge(xT_lo, i + 1)
                        pe.wait_ge(xT_hi, i + 1)
                    for k in range(2):
                        for n in range(NC_):
                            mm = pe.transpose(B[1 + k][:, C_OFF[n]:C_OFF[n] + C_LEN[n]],
                                              o[0:C_LEN[n], n, 2 * k:2 * k + 2, :].rearrange("p h e -> p (h e)"),
                                              ident[0:C_LEN[n], 0:C_LEN[n]])
                    mm.then_inc(oT_turned, 1)
                if following:
                    tokens(i + 1, q2, 1)
                if b2:
                    pe.wait_ge(oT_ready, i - 1)
                    pe.wait_ge(oT_high, i - 1)
                    for n in range(NC_):
                        bank, col = (B[6], n * D) if n < 2 else (B[3], 0)
                        for k in range(2):
                            mm = pe.matmul(bank[0:CH, col:col + D], oT[:, k, C_OFF[n]:C_OFF[n] + CH], wo[:, k, :],
                                           start=(k == 0), stop=(k == 1))
                    mm.then_inc(y_done, 1)
                if c:
                    counts(i - 3)
            turns(pe, turn)

        @block.vector
        def _(dve):
            ch = Chain(dve, chain)
            dve.sem_inc(h_ready, 1)
            dve.sem_inc(fm, 4)
            dve.sem_inc(slots_ready, 1)
            dve.wait_ge(loaded, 16 * LOADS)
            dve.wait_ge(made, MADE)
            ch.step(dve.tensor_tensor(posb[:], posb[:], bias[:], ALU.add))
            ch.step(dve.tensor_copy(tri[:], mask[:, 0:CH]))
            ch.step(dve.tensor_scalar(run[:], rank[:, 0, :], -float(REGION), float(REGION * EXP - 1), ALU.mult, ALU.add))
            ch.settle()
            ch.step(dve.tensor_scalar(tid[:, 2:3], tid[:, 2:3], float(C_OFF[2] - 2 * CH - 0), None, ALU.add))
            ch.settle()
            ch.step(dve.tensor_scalar(tid[:], tid[:], -float(SEQ), None, ALU.add))
            ch.settle()

            def turn(i, p4, a, b1, b2, c, d):
                p2 = p4 % 2
                q2 = 1 - p2
                hc = (p4 + 1) % 4
                def masks(first):
                    for n in range(first, first + 4):
                        hh, part = 2 * (n // 4) + n % 2, (n % 4) // 2
                        dve.wait_ge(at_done, 8 * (i - 2) + n + 1)
                        lo, hi = (AT0, AT1) if part == 0 else (AT1, ATW)
                        dve.tensor_tensor(at[0:CH, hh, lo:hi], B[3 + n % 4][0:CH, 0:hi - lo], mask[:, lo:hi], ALU.mult).then_inc(masked, 1)

                if c:
                    dve.wait_ge(h2_ready, i - 2)
                    for n in range(NC_):
                        mm = dve.bn_stats(out=st2[:, n, :], in_=h[:, hc, n, :])
                    ch.step(mm)
                    ch.settle()
                    carry(dve, passed_dve)
                    for n in range(NC_):
                        mm = dve.bn_aggr(out=mv2[:, n, :], in_=st2[:, n, :])
                    ch.step(mm)
                    ch.settle()
                    dve.tensor_scalar(ve2[:], mv2[:, :, 1], LN_EPS, None, ALU.add).then_inc(var2, 1)
                if a:
                    if not isinstance(i, int) or i > 3:
                        dve.wait_ge(base_ready, i - 3)
                    dve.wait_ge(tok_done, i + 3)
                    dve.tensor_tensor(h[:, p4, 0:2, :], B[0][0:CH, 0:2 * D].rearrange("p (c n) -> p c n", c=2), posb[:],
                                      ALU.add).then_inc(h_ready, 1)
                    dve.wait_ge(h_ready, i + 2)
                    dve.wait_ge(text_ready, i + 1)
                    for n in range(NC_):
                        mm = dve.bn_stats(out=st1[:, n, :], in_=h[:, p4, n, :])
                    ch.step(mm)
                    ch.settle()
                    carry(dve, passed_dve)
                    for n in range(NC_):
                        mm = dve.bn_aggr(out=mv1[:, n, :], in_=st1[:, n, :])
                    ch.step(mm)
                    ch.settle()
                    dve.tensor_scalar(ve1[:], mv1[:, :, 1], LN_EPS, None, ALU.add).then_inc(var1, 1)
                if c:
                    dve.wait_ge(rstd2, i - 2)
                    if not isinstance(i, int) or i > 3:
                        dve.wait_ge(base_ready, i - 3)
                    for n in range(NC_):
                        mm = dve.tensor_scalar(ln2[:, n, :], h[:, hc, n, :], mv2[:, n, 0:1], rs2[:, n:n + 1], ALU.subtract, ALU.mult)
                    mm.then_inc(l_ready, 1)
                if b1:
                    for n in range(4):
                        dve.wait_ge(qk_read, 4 * (i - 1) + n + 1)
                        dve.scalar_tensor_tensor(out=qk[:, q2, n, 0:SEQ], in0=e_sb[:, n, :], scalar=1.0, in1=r_sb[:, n, :],
                                                 op0=ALU.min, op1=ALU.add).then_inc(fm, 1)
                if b2:
                    masks(0)
                if c:
                    dve.wait_ge(l_ready, i - 2)
                    dve.wait_ge(rms_ready, i - 2)
                    if not isinstance(i, int) or i >= 5:
                        dve.wait_ge(rows_out[q2], 48 * (i - 3 - (1 - p2)) if not isinstance(i, int) else 96 * ((i - 3) // 2))
                    for n in range(NC_):
                        mm = dve.scalar_tensor_tensor(out=rt[:, q2, n, 0:D], in0=ln2[:, n, :], scalar=rms[:, n:n + 1],
                                                      in1=lnw[:], op0=ALU.mult, op1=ALU.mult)
                    mm.then_inc(normed, 1)
                if b2:
                    masks(4)
                if d:
                    wide = [CH, NC_, EXP]
                    cum = B[7][0:CH, 0:NC_ * EXP].rearrange("p (c e) -> p c e", c=NC_)
                    dve.wait_ge(cum_done, i - 3)
                    dve.tensor_tensor(at_cum[:], cum, hot[:], ALU.mult)
                    ch.step(dve.tensor_tensor(at_run[:], hot[:], run[:].unsqueeze(1).to_broadcast(wide), ALU.mult))
                    ch.settle()
                    dve.tensor_reduce(out=prio[:], in_=at_cum[:], axis=AX.X, op=ALU.add)
                    ch.step(dve.tensor_reduce(out=place[:], in_=at_run[:], axis=AX.X, op=ALU.add))
                    ch.step(dve.scalar_tensor_tensor(out=run[:], in0=B[7][0:CH, NC_ * EXP:(NC_ + 1) * EXP], scalar=float(CAP),
                                                     in1=run[:], op0=ALU.min, op1=ALU.add))
                    ch.step(dve.tensor_scalar(tid[:], tid[:], float(SEQ), None, ALU.add))
                    ch.settle()
                    dve.tensor_scalar(over[:], prio[:], CAP + 0.5, float(NO_ROW), ALU.is_gt, ALU.mult)
                    ch.step(dve.tensor_tensor(slot0[:], prio[:], place[:], ALU.add))
                    ch.settle()
                    if not isinstance(i, int) or i >= 6:
                        dve.wait_ge(slots_out[p2], 24 * (i - 4 - p2) if not isinstance(i, int) else 48 * ((i - 4) // 2))
                    dve.tensor_copy(tid_i[:, p2, :], tid[:])
                    dve.tensor_tensor(slot[:, p2, :], slot0[:], over[:], ALU.add).then_inc(slots_ready, 1)
                if a:
                    dve.wait_ge(rstd1, i + 1)
                    if not isinstance(i, int) or i >= 1:
                        dve.wait_ge(xT_turned, i)
                    for n in range(NC_):
                        mm = dve.tensor_scalar(ln[:, n, :], h[:, p4, n, :], mv1[:, n, 0:1], rs1[:, n:n + 1], ALU.subtract, ALU.mult)
                    mm.then_inc(ln1, 1)
                if b2:
                    for n in range(NC_):
                        dve.wait_ge(num_done, 3 * (i - 2) + n + 1)
                        num = B[3 + n][0:C_LEN[n], 0:AH * (AD + 1)].rearrange("p (h e) -> p h e", h=AH)
                        ch.step(dve.tensor_scalar(den[0:C_LEN[n], n, :], num[:, :, AD], 1e-6, None, ALU.max))
                        ch.settle()
                        ch.step(dve.reciprocal(rden[0:C_LEN[n], n, :], den[0:C_LEN[n], n, :]))
                        ch.settle()
                        mm = dve.tensor_tensor(o[0:C_LEN[n], n, :, :], num[:, :, 0:AD],
                                               rden[0:C_LEN[n], n, :].unsqueeze(2).to_broadcast([C_LEN[n], AH, AD]), ALU.mult)
                    mm.then_inc(o_ready, 1)
                if a:
                    dve.wait_ge(xT_turned, i + 1)
                    dve.tensor_copy(xT[0:96, p2, 1, 0:SEQ], B[2][0:96, 0:SEQ]).then_inc(xT_hi, 1)
                if b2:
                    dve.wait_ge(oT_turned, i - 1)
                    dve.tensor_copy(oT[:, 1, 0:SEQ], B[2][:, 0:SEQ]).then_inc(oT_high, 1)
                if c:
                    lg = B[7][0:CH, 0:NC_ * EXP].rearrange("p (c e) -> p c e", c=NC_)
                    wide = [CH, NC_, EXP]
                    dve.wait_ge(lg_done, i - 2)
                    ch.step(dve.tensor_reduce(out=best[:], in_=lg, axis=AX.X, op=ALU.max))
                    ch.settle()
                    dve.tensor_tensor(less[:], lg, best[:].unsqueeze(2).to_broadcast(wide), ALU.subtract).then_inc(ex_in, 1)
                    ch.step(dve.tensor_tensor(eq[:], lg, best[:].unsqueeze(2).to_broadcast(wide), ALU.is_equal))
                    ch.settle()
                    ch.step(dve.tensor_tensor(ranked[:], eq[:], rank[:], ALU.mult))
                    ch.settle()
                    ch.step(dve.tensor_reduce(out=first[:], in_=ranked[:], axis=AX.X, op=ALU.max))
                    ch.settle()
                    dve.tensor_tensor(hot[:], rank[:], first[:].unsqueeze(2).to_broadcast(wide), ALU.is_equal).then_inc(hot_ready, 1)
                    dve.wait_ge(ex_ready, i - 2)
                    ch.step(dve.tensor_reduce(out=esum[:], in_=ex[:], axis=AX.X, op=ALU.add))
                    ch.settle()
                    dve.reciprocal(rt[:, q2, :, 2 * D:2 * D + 1].rearrange("p c o -> p (c o)"), esum[:]).then_inc(rp_ready, 1)
                if b2:
                    dve.wait_ge(y_done, i - 1)
                    dve.scalar_tensor_tensor(out=gated[:, 0:2, :], in0=th[:, p2, 0:2, :], scalar=1.0,
                                             in1=B[6][0:CH, 0:2 * D].rearrange("p (c n) -> p c n", c=2), op0=ALU.add, op1=ALU.mult)
                    ch.step(dve.scalar_tensor_tensor(out=gated[:, 2, :], in0=th[:, p2, 2, :], scalar=1.0, in1=B[3][0:CH, 0:D],
                                                     op0=ALU.add, op1=ALU.mult))
                    ch.settle()
                    dve.scalar_tensor_tensor(out=h[:, (p4 + 2) % 4, :, :], in0=gated[:], scalar=0.5, in1=h[:, (p4 + 2) % 4, :, :],
                                             op0=ALU.mult, op1=ALU.add).then_inc(h2_ready, 1)

            PER = 21
            for i in range(8):
                turn(i, i % 4, True, i >= 1, i >= 2, i >= 3, i >= 4)
            done = ch.n
            with dve.Fori(0, BATCH // 4 - 3) as j:
                for k in range(4):
                    ch.base, ch.n = done + (4 * j + k) * PER, 0
                    turn(4 * j + 8 + k, k, True, True, True, True, True)
                    assert ch.n == PER, ch.n
            ch.base, ch.n = done + (BATCH - 12) * PER, 0
            for i in range(BATCH - 4, BATCH + 4):
                turn(i, i % 4, i < BATCH, i - 1 < BATCH, i - 2 < BATCH, i - 3 < BATCH, True)
            ch.settle()


def moe_phase(nc, io, out, ident, rows_dram, table_dram, run, wir, wir_in, sems):
    with ExitStack() as ctx:
        S = Scope(nc, ctx, "m")
        S.sem = lambda name: sems.sem(f"m_{name}")
        wi0 = S.sb("wi0", [128, EXP, F])
        wo = S.sb("wo", [128, EXP, FC, D])
        cnt = S.sb("cnt", [1, EXP])
        cnt_i, nt_i = S.sb("cnt_i", [1, EXP], I32), S.sb("nt_i", [1, EXP], I32)
        nt = S.sb("nt", [1, EXP])
        below = S.sb("below", [1, EXP, EXP])
        upto = S.sb("upto", [1, EXP, EXP])
        ends = S.sb("ends", [1, EXP])
        rank = S.sb("rank", [1, EXP])
        tnum = S.sb("tnum", [1, TILES])
        past = S.sb("past", [1, TILES, EXP])
        start = S.sb("start", [1, TILES])
        expert = S.sb("expert", [1, TILES])
        expert_i, offs_i = S.sb("expert_i", [1, TILES], I32), S.sb("offs_i", [1, TILES], I32)
        offs = S.sb("offs", [1, TILES])
        N3 = 3
        idt = S.sb("ids", [TILE, N3], I32)
        ids_g, ids_s = S.sb("ids_g", [TILE, N3], I32), S.sb("ids_s", [TILE, N3], I32)
        g = S.sb("rows", [TILE, N3, ROW])
        xa = S.sb("xa", [128, TILE])
        xr = S.sb("xr", [128, 2, TILE])
        hid = S.sb("hid", [TILE, F])
        hidT = S.sb("hidT", [128, FC, TILE])
        ob = S.sb("ob", [TILE, N3, D])
        ps_x, ps_y = S.ps("x", [128, 512]), S.ps("y", [128, 512])
        ps_u = [S.ps("u0", [128, 512]), S.ps("u1", [128, 512])]
        ps_t = [S.ps("t0", [128, 512]), S.ps("t1", [128, 512])]
        FH = F // 2
        loaded, small, made, tiles_ready = S.sem("loaded"), S.sem("small"), S.sem("made"), S.sem("tiles_ready")
        ids_in = [S.sem(f"ids_in{n}") for n in range(N3)]
        rows_in = [S.sem(f"rows_in{n}") for n in range(N3)]
        rows_out = [S.sem(f"rows_out{n}") for n in range(N3)]
        (x_turned, x_ready, up_done, relu_lo, relu_hi, h_turned, hT_lo, hT_hi, y_done, y_ready, chain, passed) = (S.sem(n) for n in (
            "x_turned", "x_ready", "up_done", "relu_lo", "relu_hi", "h_turned", "hT_lo", "hT_hi", "y_done", "y_ready", "chain", "passed"))
        passed_sp, ids_taken, ids_kept = S.sem("passed_sp"), S.sem("ids_taken"), S.sem("ids_kept")
        block = ctx.enter_context(nc.Block())
        GRP = TILES // N3
        assert GRP * N3 == TILES

        @block.sync
        def _(sp):
            sp.dma_start(below[:], io["below"]).then_inc(small, 16)
            sp.dma_start(tnum[:], io["tnum"]).then_inc(small, 16)
            sp.dma_start(rank[:], io["rank"][0:1, 0, :]).then_inc(small, 16)
            sp.dma_start(wi0[:], io["wi0"]).then_inc(loaded, 16)
            sp.dma_start(wo[:], io["wo"]).then_inc(loaded, 16)
            sp.wait_ge(tiles_ready, 1)

            def load_ids(j, p):
                off = sp.value_load(offs_i[0:1, ds(N3 * j + p, 1)], min_val=0, max_val=EXP * REGION)
                if not isinstance(j, int):
                    sp.wait_ge(ids_taken, N3 * j + p - N3 + 1)
                    carry(sp, passed_sp)
                sp.dma_start(idt[:, p:p + 1], table_dram[ds(off, TILE), :]).then_inc(ids_in[p], 16)

            for p in range(N3):
                load_ids(0, p)
            with sp.Fori(1, GRP) as j:
                for p in range(N3):
                    load_ids(j, p)

        @block.gpsimd
        def _(pool):
            pool.memset(g[:], 0.0).then_inc(made, 1)
            pool.memset(xr[:], 0.0).then_inc(made, 1)
            pool.wait_ge(made, 2)

            def gather(t, j, p):
                pool.wait_ge(ids_in[p], 16 * j + 16)
                carry(pool, passed)
                pool.tensor_copy(ids_g[:, p:p + 1], idt[:, p:p + 1]).then_inc(ids_taken, 1)
                pool.wait_ge(ids_taken, t + 1)
                pool.wait_ge(y_ready, t + 1)
                carry(pool, passed)
                pool.indirect_dma_start(
                    out=g[:, p, :], out_offset=None, in_=rows_dram,
                    in_offset=bass.IndirectOffsetOnAxis(ap=ids_g[:, p:p + 1], axis=0),
                    bounds_check=BATCH * SEQ - 1, oob_is_err=False).then_inc(rows_in[p], 16)

            def scatter(t, j, p):
                if not isinstance(j, int) or j > 0:
                    pool.wait_ge(rows_out[p], 16 * j)
                carry(pool, passed)
                pool.tensor_copy(ids_s[:, p:p + 1], ids_g[:, p:p + 1]).then_inc(ids_kept, 1)
                pool.wait_ge(ids_kept, t + 1)
                pool.wait_ge(y_ready, t + 4)
                carry(pool, passed)
                pool.indirect_dma_start(
                    out=out.rearrange("b t n -> (b t) n"), out_offset=bass.IndirectOffsetOnAxis(ap=ids_s[:, p:p + 1], axis=0),
                    in_=ob[:, p, :], in_offset=None,
                    bounds_check=BATCH * SEQ - 1, oob_is_err=False).then_inc(rows_out[p], 16)

            gather(0, 0, 0)
            gather(1, 0, 1)

            def three(j):
                for p in range(N3):
                    gather(N3 * j + p + 2, j + (p + 2) // N3, (p + 2) % N3)
                    scatter(N3 * j + p, j, p)

            three(0)
            with pool.Fori(1, GRP - 1) as j:
                three(j)
            gather(TILES - 1, GRP - 1, 2)
            for p in range(N3):
                scatter(TILES - N3 + p, GRP - 1, p)
            for p in range(N3):
                pool.wait_ge(rows_out[p], 16 * GRP)

        @block.scalar
        def _(act):
            act.wait_ge(made, 2)

            def relu(t):
                act.wait_ge(up_done, t + 1)
                act.activation(hid[:, 0:FH], ps_u[0][:, 0:FH], ACT.Relu).then_inc(relu_lo, 1)

            def hT(t):
                act.wait_ge(h_turned, t + 1)
                act.activation(hidT[:, 0:3, :], ps_t[0][:, 0:FH].rearrange("p (f t) -> p f t", f=3), ACT.Copy).then_inc(hT_lo, 1)

            def x_copy(t):
                act.wait_ge(x_turned, t + 1)
                act.activation(xa[:], ps_x[:, 0:TILE], ACT.Copy)
                act.activation(xr[0:D1, 0, :], ps_x[0:D1, TILE:2 * TILE], ACT.Copy)
                act.activation(xr[D1:128, 1, :], ps_x[0:D1, TILE:2 * TILE], ACT.Copy).then_inc(x_ready, 1)

            act.sem_inc(x_ready, 1)
            x_copy(0)
            relu(0)
            x_copy(1)
            with act.Fori(0, TILES - 2) as t:
                hT(t)
                relu(t + 1)
                x_copy(t + 2)
            hT(TILES - 2)
            relu(TILES - 1)
            hT(TILES - 1)

        @block.tensor
        def _(pe):
            pe.wait_ge(loaded, 32)
            pe.wait_ge(wir_in, 16)
            pe.wait_ge(tiles_ready, 1)

            def turn_x(t, j, p):
                pe.wait_ge(rows_in[p], 16 * j + 16)
                pe.wait_ge(x_ready, t + 1)
                pe.transpose(ps_x[:, 0:TILE], g[:, p, 0:D0], ident[:])
                pe.transpose(ps_x[0:D1, TILE:2 * TILE], g[:, p, D0:D], ident[:]).then_inc(x_turned, 1)

            def expert_of(t):
                return pe.value_load(expert_i[0:1, ds(t, 1)], min_val=0, max_val=EXP - 1)

            def up(t):
                e = expert_of(t)
                pe.wait_ge(x_ready, t + 2)
                for half in range(2):
                    pe.matmul(ps_u[half][:, 0:FH], xa[:], wi0[:, ds(e, 1), half * FH:(half + 1) * FH].rearrange("p e f -> p (e f)"),
                              start=True, stop=False)
                    mm = pe.matmul(ps_u[half][:, 0:FH], xr[:, half, :], wir[:, ds(e, 1), :].rearrange("p e f -> p (e f)"),
                                   start=False, stop=True)
                mm.then_inc(up_done, 1)
                return e

            def turn_h(t):
                pe.wait_ge(relu_lo, t + 1)
                pe.wait_ge(relu_hi, t + 1)
                for f in range(FC):
                    mm = pe.transpose(ps_t[f // 3][:, (f % 3) * TILE:(f % 3 + 1) * TILE], hid[:, f * 128:(f + 1) * 128], ident[:])
                mm.then_inc(h_turned, 1)

            def down(t, e=None):
                if e is None:
                    e = expert_of(t)
                pe.wait_ge(hT_lo, t + 1)
                pe.wait_ge(hT_hi, t + 1)
                pe.wait_ge(y_ready, t + 3)
                for f in range(FC):
                    mm = pe.matmul(ps_y[:, 0:D], hidT[:, f, :], wo[:, ds(e, 1), f, :].rearrange("p e n -> p (e n)"),
                                   start=(f == 0), stop=(f == FC - 1))
                mm.then_inc(y_done, 1)

            turn_x(0, 0, 0)
            up(0)
            turn_x(1, 0, 1)
            with pe.Fori(0, GRP - 1) as j:
                following = None
                for p in range(N3):
                    t = N3 * j + p
                    turn_h(t)
                    present, following = following, up(t + 1)
                    down(t, present)
                    turn_x(t + 2, j + (p + 2) // N3, (p + 2) % N3)
            t = TILES - 3
            turn_h(t)
            up(t + 1)
            down(t)
            turn_x(t + 2, GRP - 1, 2)
            turn_h(t + 1)
            up(t + 2)
            down(t + 1)
            turn_h(t + 2)
            down(t + 2)

        @block.vector
        def _(dve):
            ch = Chain(dve, chain)
            dve.sem_inc(y_ready, 3)
            dve.wait_ge(small, 48)
            dve.wait_ge(made, 2)
            ch.step(dve.scalar_tensor_tensor(out=cnt[:], in0=rank[:], scalar=float(REGION), in1=run[0:1, :], op0=ALU.mult, op1=ALU.add))
            ch.settle()
            ch.step(dve.tensor_scalar(cnt_i[:], cnt[:], float(1 - REGION * EXP + TILE - 1), None, ALU.add))
            ch.settle()
            ch.step(dve.tensor_scalar(nt_i[:], cnt_i[:], TILE.bit_length() - 1, None, ALU.arith_shift_right))
            ch.settle()
            ch.step(dve.tensor_copy(nt[:], nt_i[:]))
            ch.settle()
            ch.step(dve.tensor_tensor(upto[:], below[:], nt[:].unsqueeze(1).to_broadcast([1, EXP, EXP]), ALU.mult))
            ch.settle()
            ch.step(dve.tensor_reduce(out=ends[:], in_=upto[:], axis=AX.X, op=ALU.add))
            ch.settle()
            w = [1, TILES, EXP]
            ch.step(dve.tensor_tensor(past[:], tnum[:].unsqueeze(2).to_broadcast(w), ends[:].unsqueeze(1).to_broadcast(w), ALU.is_ge))
            ch.settle()
            ch.step(dve.tensor_reduce(out=expert[:], in_=past[:], axis=AX.X, op=ALU.add))
            ch.settle()
            ch.step(dve.tensor_tensor(past[:], past[:], nt[:].unsqueeze(1).to_broadcast(w), ALU.mult))
            ch.settle()
            ch.step(dve.tensor_reduce(out=start[:], in_=past[:], axis=AX.X, op=ALU.add))
            ch.settle()
            ch.step(dve.tensor_tensor(start[:], tnum[:], start[:], ALU.subtract))
            ch.settle()
            ch.step(dve.tensor_scalar(start[:], start[:], float(TILE), None, ALU.mult))
            ch.settle()
            ch.step(dve.scalar_tensor_tensor(out=offs[:], in0=expert[:], scalar=float(REGION), in1=start[:], op0=ALU.mult, op1=ALU.add))
            ch.settle()
            dve.tensor_scalar(offs_i[:], offs[:], float(EXP * REGION), None, ALU.min)
            ch.step(dve.tensor_scalar(expert_i[:], expert[:], float(EXP - 1), None, ALU.min))
            ch.settle()
            dve.sem_inc(tiles_ready, 1)

            def relu(t):
                dve.wait_ge(up_done, t + 1)
                dve.tensor_scalar(hid[:, FH:F], ps_u[1][:, 0:FH], 0.0, None, ALU.max).then_inc(relu_hi, 1)

            def hT(t):
                dve.wait_ge(h_turned, t + 1)
                dve.tensor_copy(hidT[:, 3:6, :], ps_t[1][:, 0:FH].rearrange("p (f t) -> p f t", f=3)).then_inc(hT_hi, 1)

            def finish(t, j, p):
                dve.wait_ge(y_done, t + 1)
                if not isinstance(j, int) or j > 0:
                    dve.wait_ge(rows_out[p], 16 * j)
                dve.scalar_tensor_tensor(out=ob[:, p, :], in0=ps_y[:, 0:D], scalar=g[:, p, 2 * D:2 * D + 1], in1=g[:, p, D:2 * D],
                                         op0=ALU.mult, op1=ALU.add).then_inc(y_ready, 1)

            relu(0)

            def three(j):
                for p in range(N3):
                    t = N3 * j + p
                    hT(t)
                    relu(t + 1)
                    finish(t, j, p)

            three(0)
            with dve.Fori(1, GRP - 1) as j:
                three(j)
            t = TILES - 3
            hT(t)
            relu(t + 1)
            finish(t, GRP - 1, 0)
            hT(t + 1)
            relu(t + 2)
            finish(t + 1, GRP - 1, 1)
            hT(t + 2)
            finish(t + 2, GRP - 1, 2)


def build(nc, io, out):
    with ExitStack() as ctx:
        S = Scope(nc, ctx, "g")
        rows_dram = nc.dram_tensor("token_rows", [BATCH * SEQ, ROW], F32, kind="Internal").ap()
        table_dram = nc.dram_tensor("expert_table", [TABLE, 1], I32, kind="Internal").ap()
        ident = S.sb("ident", [128, 128])
        run = S.sb("run", [CH, EXP])
        wir = S.sb("wir", [128, EXP, F // 2])
        wir_in = S.sem("wir_in")
        made = S.sem("made")
        with nc.Block() as block:
            @block.gpsimd
            def _(pool):
                pool.memset(ident[:], 0.0).then_inc(made, 1)
                pool.wait_ge(made, 1)
                pool.affine_select(out=ident[:], in_=ident[:], compare_op=ALU.not_equal, fill=1.0, base=0,
                                   pattern=[[-1, 128]], channel_multiplier=1).then_inc(made, 1)
                pool.wait_ge(made, 2)
        with ExitStack() as texts:
            txt = Scope(nc, texts, "g").sb("txt", [TXT, BATCH, D])
            text_phase(nc, io, txt, ident, wir, wir_in, S)
            fusion_phase(nc, io, out, txt, ident, rows_dram, table_dram, run, S)
        moe_phase(nc, io, out, ident, rows_dram, table_dram, run, wir, wir_in, S)


def layout(inputs):
    a = {k: np.asarray(v) for k, v in inputs.items()}
    f = np.float32
    r = {}
    r["ids"] = np.ascontiguousarray(a["x_txt"].T)
    r["emb"] = a["L0_txt_emb"]
    p, i = np.meshgrid(np.arange(TXT), np.arange(D // 2))
    pe = np.zeros((TXT, D), f)
    pe[:, ::2] = np.sin(p / 2500 ** (2 * i / D)).T
    pe[:, 1::2] = np.cos(p / 2500 ** (2 * i / D)).T
    pos = np.zeros((128, 2, TXT), f)
    pos[:, 0] = pe.T[0:D0]
    pos[0:D1, 1] = pe.T[D0:D]
    r["pos"] = pos
    wqk = np.zeros((128, 2, 3, 4, 32), f)
    for s, n in enumerate("qk"):
        wqk[0:SLICE, s, :, :, 0:HD] = a[f"L0_txt_W{n}"].reshape(SLICE, 3, 4, HD)
        wqk[SLICE, s, :, :, 0:HD] = a[f"L0_txt_b{n}"].reshape(3, 4, HD)
    r["wqk"] = wqk.reshape(128, 2, 3, 128)
    r["wv"] = np.zeros((128, D), f)
    r["wv"][0:SLICE], r["wv"][SLICE] = a["L0_txt_Wv"], a["L0_txt_bv"]
    r["Wf"] = np.zeros((128, 2, D), f)
    r["Wf"][:, 0], r["Wf"][0:D1, 1] = a["L0_txt_Wf"][0:D0], a["L0_txt_Wf"][D0:D]
    vecs = np.zeros((128, 5, 2), f)
    for n, name in enumerate(("bf", "g1", "b1", "g2", "b2")):
        vecs[:, n, 0] = a[f"L0_txt_{name}"][0:D0]
        vecs[0:D1, n, 1] = a[f"L0_txt_{name}"][D0:D]
    r["vecs"] = vecs
    r["ones"] = np.ones((1, 3, 2 * TXT), f)
    G, P = 14, 16
    x = a["x"].reshape(BATCH, 3, G, P, G, P).transpose(0, 1, 3, 5, 2, 4).reshape(BATCH, KP, 128, IMG)
    patches = np.zeros((BATCH, 128, KP, 2 * CH), f)
    patches[:, :, :, 1:1 + IMG] = x.transpose(0, 2, 1, 3)
    r["patches"] = patches.reshape(BATCH, 128, KP * 2 * CH)
    r["w_tok"] = a["L0_tok_W"].T.reshape(KP, 128, D).transpose(1, 0, 2)
    pe = np.zeros((2 * CH, D), f)
    pe[0:1 + IMG] = a["L0_tok_pos_emb"]
    r["pos_emb"] = pe.reshape(2, CH, D).transpose(1, 0, 2)
    tb = np.zeros((2 * CH, D), f)
    tb[0] = a["L0_tok_class_token"]
    tb[1:1 + IMG] = a["L0_tok_b"]
    r["tok_bias"] = tb.reshape(2, CH, D).transpose(1, 0, 2)
    for n, w in (("a_wq", "L0_attn_Wq"), ("a_wk", "L0_attn_Wk"), ("a_wv", "L0_attn_Wv"), ("a_wg", "L0_attn_Wg"),
                 ("w_router", "L0_ffn_w_router")):
        r[n] = np.zeros((128, KD, a[w].shape[1]), f)
        r[n][0:96] = a[w].reshape(KD, 96, -1).transpose(1, 0, 2)
    r["a_wo"] = a["L0_attn_Wo"]
    r["ln_w"] = a["L0_ffn_ln_w"]
    s, t = np.arange(CH)[:, None], np.arange(SEQ)[None, :]
    r["mask"] = np.concatenate([(t[:, o:] >= s + o) & (s < n) for o, n in zip(C_OFF, C_LEN)], axis=1).astype(f)
    r["rank"] = np.broadcast_to(np.arange(EXP, 0, -1, dtype=f), (CH, NC_, EXP))
    r["below"] = np.tril(np.ones((EXP, EXP), f))[None]
    r["tnum"] = np.arange(TILES, dtype=f)[None]
    wi, wo = a["L0_ffn_wi"], a["L0_ffn_wo"]
    r["wi0"] = wi[:, 0:D0].transpose(1, 0, 2)
    r["wir"] = wi[:, D0:D].reshape(EXP, D1, 2, F // 2).transpose(2, 1, 0, 3).reshape(128, EXP, F // 2)
    r["wo"] = wo.reshape(EXP, FC, 128, D).transpose(2, 0, 1, 3)
    return {k: np.ascontiguousarray(v) for k, v in r.items()}


def kernel(**inputs):
    from concourse import bacc
    from concourse.bass_utils import run_bass_kernel_spmd as run

    nc = bacc.Bacc("TRN2", target_bir_lowering=False, num_devices=1)
    arrays = layout(inputs)
    io = {k: nc.dram_tensor(f"in_{k}", v.shape, mybir.dt.from_np(v.dtype), kind="ExternalInput").ap()
          for k, v in arrays.items()}
    out = nc.dram_tensor("out", [BATCH, SEQ, D], F32, kind="ExternalOutput").ap()
    build(nc, io, out)
    r = run(nc, [{f"in_{k}": v for k, v in arrays.items()}], core_ids=[0])
    return r.results[0]["out"]
```
